# Optimizing a Trainium2 kernel written in Bass

```python
import numpy as np
import jax
import jax.numpy as jnp

def _softmax(x, axis=-1):
    return jax.nn.softmax(x, axis=axis)

def _gelu(x):
    return jax.nn.gelu(x, approximate=True)

def _silu(x):
    return jax.nn.silu(x)

def _sigmoid(x):
    return jax.nn.sigmoid(x)

def _layernorm(x, axis=-1, eps=1e-05):
    m = jnp.mean(x, axis=axis, keepdims=True)
    v = jnp.var(x, axis=axis, keepdims=True)
    return (x - m) / jnp.sqrt(v + eps)

def _scatter_add(tgt, idx, src, axis=0):
    return tgt.at[idx].add(src)

def _segment_sum(src, seg, n):
    return jax.ops.segment_sum(src, seg, n)
kernel_name = 'mk_sandwich_d2_jaxref_r8_ab87f9'

def setup_inputs(seed: int=0):
    np.random.seed(seed)
    _w = jnp.asarray

    def _L0_attn_setup():
        import jax, jax.numpy as jnp
        import numpy as np
        B, T, HID = (2, 256, 256)
        HK, HV, DK, DV = (16, 16, 128, 128)
        KEY_DIM = HK * DK
        VAL_DIM = HV * DV
        CONV_K = 4
        EPS = 1e-05
        L2_EPS = 1e-06

        def _l2norm(x):
            return x / jnp.sqrt(jnp.sum(x * x, axis=-1, keepdims=True) + L2_EPS)

        def _causal_depthwise_conv(x, w):
            Kc = w.shape[1]
            xp = jnp.pad(x, ((0, 0), (Kc - 1, 0), (0, 0)))
            t = x.shape[1]
            out = jnp.zeros_like(x)
            for j in range(Kc):
                out = out + w[:, j] * xp[:, j:j + t, :]
            return out

        def _gated_delta_rule(q, k, v, g, beta):
            b, t, h, dk = q.shape
            dv = v.shape[-1]
            qs, ks_, vs, gs, bs = (jnp.moveaxis(a, 1, 0) for a in (q, k, v, g, beta))
            S0 = jnp.zeros((b, h, dk, dv), q.dtype)

            def step(S, inp):
                qt, kt, vt, gt, bt = inp
                S = S * jnp.exp(gt)[..., None, None]
                v_old = jnp.einsum('bhk,bhkv->bhv', kt, S)
                delta = (vt - v_old) * bt[..., None]
                S = S + jnp.einsum('bhk,bhv->bhkv', kt, delta)
                ot = jnp.einsum('bhk,bhkv->bhv', qt, S)
                return (S, ot)
            _, o = jax.lax.scan(step, S0, (qs, ks_, vs, gs, bs))
            return jnp.moveaxis(o, 0, 1)
        key = jax.random.key(seed)
        ks = jax.random.split(key, 8)
        std = 0.02
        return {'hidden_states': jax.random.normal(ks[0], (B, T, HID), jnp.float32), 'W_qkv': jax.random.normal(ks[1], (HID, 2 * KEY_DIM + VAL_DIM), jnp.float32) * std, 'W_ab': jax.random.normal(ks[2], (HID, 2 * HV + VAL_DIM), jnp.float32) * std, 'conv_w': jax.random.normal(ks[3], (2 * KEY_DIM + VAL_DIM, CONV_K), jnp.float32) * std, 'A_log': jnp.log(jax.random.uniform(ks[4], (HV,), jnp.float32, 0.01, 16.0)), 'dt_bias': jax.random.normal(ks[5], (HV,), jnp.float32) * 0.1, 'o_norm_w': jnp.ones((DV,), jnp.float32), 'W_o': jax.random.normal(ks[6], (VAL_DIM, HID), jnp.float32) * (std / np.sqrt(2 * 24))}
    _L0_attn_in = _L0_attn_setup()

    def _L0_ffn_setup():
        import jax, jax.numpy as jnp
        import numpy as np
        ZERO_POINT = 128.0

        def _dequant(wq, scale):
            return (wq.astype(jnp.float32) - ZERO_POINT) * scale[:, None]
        key = jax.random.key(seed)
        ks = jax.random.split(key, 7)
        H, I = (256, 1024)
        B, S = (2, 256)
        hidden_state = jax.random.normal(ks[0], (B, S, H), dtype=jnp.float32)
        gate_w = jax.random.randint(ks[1], (I, H), 0, 32, dtype=jnp.int32)
        up_w = jax.random.randint(ks[2], (I, H), 0, 32, dtype=jnp.int32)
        down_w = jax.random.randint(ks[3], (H, I), 0, 32, dtype=jnp.int32)
        gate_scale = jax.random.uniform(ks[4], (I,), dtype=jnp.float32) * 0.02
        up_scale = jax.random.uniform(ks[5], (I,), dtype=jnp.float32) * 0.02
        down_scale = jax.random.uniform(ks[6], (H,), dtype=jnp.float32) * 0.02
        return {'hidden_state': hidden_state, 'gate_w': gate_w, 'gate_scale': gate_scale, 'up_w': up_w, 'up_scale': up_scale, 'down_w': down_w, 'down_scale': down_scale}
    _L0_ffn_in = _L0_ffn_setup()

    def _L1_attn_setup():
        import math
        import jax, jax.numpy as jnp
        import numpy as np
        HIDDEN = 256
        NUM_HEADS = 16
        HEAD_DIM = HIDDEN // NUM_HEADS
        ROTARY_NDIMS = int(HEAD_DIM * 0.25)
        ROPE_BASE = 10000.0

        def rotate_half(x):
            x1, x2 = (x[..., :x.shape[-1] // 2], x[..., x.shape[-1] // 2:])
            return jnp.concatenate((-x2, x1), axis=-1)
        key = jax.random.key(seed)
        k1, k2, k3, k4, k5 = jax.random.split(key, 5)
        b, s = (2, 256)
        scale_in = 1.0 / math.sqrt(HIDDEN)
        return {'hidden_states': jax.random.normal(k1, (b, s, HIDDEN), dtype=jnp.float32), 'W_qkv': jax.random.normal(k2, (HIDDEN, 3 * HIDDEN), dtype=jnp.float32) * scale_in, 'b_qkv': jnp.zeros((3 * HIDDEN,), dtype=jnp.float32), 'W_dense': jax.random.normal(k3, (HIDDEN, HIDDEN), dtype=jnp.float32) * scale_in, 'b_dense': jnp.zeros((HIDDEN,), dtype=jnp.float32)}
    _L1_attn_in = _L1_attn_setup()

    def _L1_ffn_setup():
        import jax, jax.numpy as jnp
        import numpy as np
        TOP_K = 4
        key = jax.random.key(seed)
        ks = jax.random.split(key, 8)
        B, S, D, E, H, HS = (2, 256, 256, 16, 128, 512)
        scaled = lambda k, shape, fan: jax.random.normal(k, shape, jnp.float32) * fan ** (-0.5)
        return {'x': jax.random.normal(ks[0], (B, S, D), jnp.float32), 'w_router': scaled(ks[1], (D, E), D), 'we1': scaled(ks[2], (E, D, H), D), 'we3': scaled(ks[3], (E, D, H), D), 'we2': scaled(ks[4], (E, H, D), H), 'ws1': scaled(ks[5], (D, HS), D), 'ws3': scaled(ks[6], (D, HS), D), 'ws2': scaled(ks[7], (HS, D), HS)}
    _L1_ffn_in = _L1_ffn_setup()
    _d = {'L0_attn_hidden_states': _L0_attn_in['hidden_states'], 'L0_attn_W_qkv': _L0_attn_in['W_qkv'], 'L0_attn_W_ab': _L0_attn_in['W_ab'], 'L0_attn_conv_w': _L0_attn_in['conv_w'], 'L0_attn_A_log': _L0_attn_in['A_log'], 'L0_attn_dt_bias': _L0_attn_in['dt_bias'], 'L0_attn_o_norm_w': _L0_attn_in['o_norm_w'], 'L0_attn_W_o': _L0_attn_in['W_o'], 'L0_ffn_gate_w': _L0_ffn_in['gate_w'], 'L0_ffn_gate_scale': _L0_ffn_in['gate_scale'], 'L0_ffn_up_w': _L0_ffn_in['up_w'], 'L0_ffn_up_scale': _L0_ffn_in['up_scale'], 'L0_ffn_down_w': _L0_ffn_in['down_w'], 'L0_ffn_down_scale': _L0_ffn_in['down_scale'], 'L1_attn_W_qkv': _L1_attn_in['W_qkv'], 'L1_attn_b_qkv': _L1_attn_in['b_qkv'], 'L1_attn_W_dense': _L1_attn_in['W_dense'], 'L1_attn_b_dense': _L1_attn_in['b_dense'], 'L1_ffn_w_router': _L1_ffn_in['w_router'], 'L1_ffn_we1': _L1_ffn_in['we1'], 'L1_ffn_we3': _L1_ffn_in['we3'], 'L1_ffn_we2': _L1_ffn_in['we2'], 'L1_ffn_ws1': _L1_ffn_in['ws1'], 'L1_ffn_ws3': _L1_ffn_in['ws3'], 'L1_ffn_ws2': _L1_ffn_in['ws2']}
    _x0 = _d['L0_attn_hidden_states']
    _d['L0_attn_hidden_states'] = jax.random.normal(jax.random.fold_in(jax.random.key(seed), 1), (2, 1024, 256), dtype=_x0.dtype)
    del _x0
    return _d

def reference(L0_attn_hidden_states, L0_attn_W_qkv, L0_attn_W_ab, L0_attn_conv_w, L0_attn_A_log, L0_attn_dt_bias, L0_attn_o_norm_w, L0_attn_W_o, L0_ffn_gate_w, L0_ffn_gate_scale, L0_ffn_up_w, L0_ffn_up_scale, L0_ffn_down_w, L0_ffn_down_scale, L1_attn_W_qkv, L1_attn_b_qkv, L1_attn_W_dense, L1_attn_b_dense, L1_ffn_w_router, L1_ffn_we1, L1_ffn_we3, L1_ffn_we2, L1_ffn_ws1, L1_ffn_ws3, L1_ffn_ws2):

    def _L0_attn_ref(hidden_states, W_qkv, W_ab, conv_w, A_log, dt_bias, o_norm_w, W_o):
        import jax, jax.numpy as jnp
        import numpy as np
        B, T, HID = (2, 256, 256)
        HK, HV, DK, DV = (16, 16, 128, 128)
        KEY_DIM = HK * DK
        VAL_DIM = HV * DV
        CONV_K = 4
        EPS = 1e-05
        L2_EPS = 1e-06

        def _l2norm(x):
            return x / jnp.sqrt(jnp.sum(x * x, axis=-1, keepdims=True) + L2_EPS)

        def _causal_depthwise_conv(x, w):
            Kc = w.shape[1]
            xp = jnp.pad(x, ((0, 0), (Kc - 1, 0), (0, 0)))
            t = x.shape[1]
            out = jnp.zeros_like(x)
            for j in range(Kc):
                out = out + w[:, j] * xp[:, j:j + t, :]
            return out

        def _gated_delta_rule(q, k, v, g, beta):
            b, t, h, dk = q.shape
            dv = v.shape[-1]
            qs, ks_, vs, gs, bs = (jnp.moveaxis(a, 1, 0) for a in (q, k, v, g, beta))
            S0 = jnp.zeros((b, h, dk, dv), q.dtype)

            def step(S, inp):
                qt, kt, vt, gt, bt = inp
                S = S * jnp.exp(gt)[..., None, None]
                v_old = jnp.einsum('bhk,bhkv->bhv', kt, S)
                delta = (vt - v_old) * bt[..., None]
                S = S + jnp.einsum('bhk,bhv->bhkv', kt, delta)
                ot = jnp.einsum('bhk,bhkv->bhv', qt, S)
                return (S, ot)
            _, o = jax.lax.scan(step, S0, (qs, ks_, vs, gs, bs))
            return jnp.moveaxis(o, 0, 1)
        b, t, _ = hidden_states.shape
        qkv = hidden_states @ W_qkv
        ab = hidden_states @ W_ab
        a, bb, gate = jnp.split(ab, [HV, 2 * HV], axis=-1)
        qkv = jax.nn.silu(_causal_depthwise_conv(qkv, conv_w))
        q, k, v = jnp.split(qkv, [KEY_DIM, 2 * KEY_DIM], axis=-1)
        q = q.reshape(b, t, HK, DK)
        k = k.reshape(b, t, HK, DK)
        v = v.reshape(b, t, HV, DV)
        rep = HV // HK
        if rep > 1:
            q = jnp.repeat(q, rep, axis=2)
            k = jnp.repeat(k, rep, axis=2)
        beta = jax.nn.sigmoid(bb) * 2.0
        g = -jnp.exp(A_log) * jax.nn.softplus(a + dt_bias)
        q = _l2norm(q) * DK ** (-0.5)
        k = _l2norm(k)
        o = _gated_delta_rule(q, k, v, g, beta)
        gate = gate.reshape(b, t, HV, DV)
        o = o * jax.nn.silu(gate)
        o = o * jax.lax.rsqrt(jnp.mean(o * o, axis=-1, keepdims=True) + EPS) * o_norm_w
        o = o.reshape(b, t, VAL_DIM) @ W_o
        return o

    def _L0_ffn_ref(hidden_state, gate_w, gate_scale, up_w, up_scale, down_w, down_scale):
        import jax, jax.numpy as jnp
        import numpy as np
        ZERO_POINT = 128.0

        def _dequant(wq, scale):
            return (wq.astype(jnp.float32) - ZERO_POINT) * scale[:, None]
        Wg = _dequant(gate_w, gate_scale)
        Wu = _dequant(up_w, up_scale)
        Wd = _dequant(down_w, down_scale)
        g = jnp.einsum('bsh,ih->bsi', hidden_state, Wg)
        u = jnp.einsum('bsh,ih->bsi', hidden_state, Wu)
        h = jax.nn.silu(g) * u
        return jnp.einsum('bsi,hi->bsh', h, Wd)

    def _L1_attn_ref(hidden_states, W_qkv, b_qkv, W_dense, b_dense):
        import math
        import jax, jax.numpy as jnp
        import numpy as np
        HIDDEN = 256
        NUM_HEADS = 16
        HEAD_DIM = HIDDEN // NUM_HEADS
        ROTARY_NDIMS = int(HEAD_DIM * 0.25)
        ROPE_BASE = 10000.0

        def rotate_half(x):
            x1, x2 = (x[..., :x.shape[-1] // 2], x[..., x.shape[-1] // 2:])
            return jnp.concatenate((-x2, x1), axis=-1)
        b, s, _ = hidden_states.shape
        qkv = hidden_states @ W_qkv + b_qkv
        qkv = qkv.reshape(b, s, NUM_HEADS, 3 * HEAD_DIM)
        qkv = qkv.transpose(0, 2, 1, 3)
        q, k, v = jnp.split(qkv, 3, axis=-1)
        inv_freq = 1.0 / ROPE_BASE ** (jnp.arange(0, ROTARY_NDIMS, 2, dtype=jnp.float32) / ROTARY_NDIMS)
        t = jnp.arange(s, dtype=jnp.float32)
        freqs = jnp.outer(t, inv_freq)
        emb = jnp.concatenate((freqs, freqs), axis=-1)
        cos = jnp.cos(emb)[None, None]
        sin = jnp.sin(emb)[None, None]
        q_rot, q_pass = (q[..., :ROTARY_NDIMS], q[..., ROTARY_NDIMS:])
        k_rot, k_pass = (k[..., :ROTARY_NDIMS], k[..., ROTARY_NDIMS:])
        q_rot = q_rot * cos + rotate_half(q_rot) * sin
        k_rot = k_rot * cos + rotate_half(k_rot) * sin
        q = jnp.concatenate([q_rot, q_pass], axis=-1)
        k = jnp.concatenate([k_rot, k_pass], axis=-1)
        scale = 1.0 / math.sqrt(HEAD_DIM)
        scores = jnp.einsum('bhqd,bhkd->bhqk', q, k) * scale
        causal = jnp.triu(jnp.ones((s, s), dtype=bool), k=1)
        scores = jnp.where(causal, jnp.float32(-jnp.inf), scores)
        attn = jax.nn.softmax(scores, axis=-1)
        out = jnp.einsum('bhqk,bhkd->bhqd', attn, v)
        out = out.transpose(0, 2, 1, 3).reshape(b, s, HIDDEN)
        return out @ W_dense + b_dense

    def _L1_ffn_ref(x, w_router, we1, we3, we2, ws1, ws3, ws2):
        import jax, jax.numpy as jnp
        import numpy as np
        TOP_K = 4
        B, S, D = x.shape
        T = B * S
        E = w_router.shape[1]
        xt = x.reshape(T, D)
        probs = jax.nn.softmax(xt @ w_router, axis=-1)
        top_w, top_i = jax.lax.top_k(probs, TOP_K)
        top_w = top_w / jnp.sum(top_w, axis=-1, keepdims=True)
        cw = jnp.zeros((T, E), xt.dtype).at[jnp.arange(T)[:, None], top_i].add(top_w)
        g = jax.nn.silu(jnp.einsum('td,edh->teh', xt, we1)) * jnp.einsum('td,edh->teh', xt, we3)
        g = g * cw[:, :, None]
        moe_out = jnp.einsum('teh,ehd->td', g, we2)
        shared = jax.nn.silu(xt @ ws1) * (xt @ ws3) @ ws2
        k = TOP_K
        out = shared / (k + 1) + moe_out * (k / (k + 1))
        return out.reshape(B, S, D)
    x = L0_attn_hidden_states
    x = x + _layernorm(_L0_attn_ref(_layernorm(x, axis=-1), L0_attn_W_qkv, L0_attn_W_ab, L0_attn_conv_w, L0_attn_A_log, L0_attn_dt_bias, L0_attn_o_norm_w, L0_attn_W_o), axis=-1)
    x = x + _layernorm(_L0_ffn_ref(_layernorm(x, axis=-1), L0_ffn_gate_w, L0_ffn_gate_scale, L0_ffn_up_w, L0_ffn_up_scale, L0_ffn_down_w, L0_ffn_down_scale), axis=-1)
    x = x + _layernorm(_L1_attn_ref(_layernorm(x, axis=-1), L1_attn_W_qkv, L1_attn_b_qkv, L1_attn_W_dense, L1_attn_b_dense), axis=-1)
    x = x + _layernorm(_L1_ffn_ref(_layernorm(x, axis=-1), L1_ffn_w_router, L1_ffn_we1, L1_ffn_we3, L1_ffn_we2, L1_ffn_ws1, L1_ffn_ws3, L1_ffn_ws2), axis=-1)
    return x

_drawn_inputs = setup_inputs


def setup_inputs(seed=0):
    import zlib

    import numpy as np

    out = dict(_drawn_inputs(seed))
    spreads = {'L0_attn_o_norm_w': (1.0, 0.2), 'L1_attn_b_qkv': (0.0, 0.1), 'L1_attn_b_dense': (0.0, 0.1)}
    factors = {'L0_attn_dt_bias': 3.908}
    for name, (base, spread) in spreads.items():
        noise = np.random.default_rng([zlib.crc32(name.encode()), seed]).standard_normal(out[name].shape)
        drawn = base * np.exp(spread * noise) if base else spread * noise
        out[name] = jnp.asarray(drawn.astype(out[name].dtype))
    for name, factor in factors.items():
        out[name] = (out[name] * factor).astype(out[name].dtype)
    return out
```

```python
from contextlib import ExitStack

import numpy as np

import concourse.bass as bass
from concourse import mybir

F32 = mybir.dt.float32
BF16 = mybir.dt.bfloat16
I32 = mybir.dt.int32
ALU = mybir.AluOpType
ACT = mybir.ActivationFunctionType
AX = mybir.AxisListType
ds = bass.ds

P = 128
B, T, D = 2, 1024, 256
NC = T // P
KD = D // P
LN_EPS = 1e-5
H, DK = 16, 128
HP = H // 2
U = 2 * B
TAPS = 4
HALO = TAPS - 1
CW = P + HALO
L2_EPS = 1e-6
KINDS = (1, 0, 2)
LEVELS = 7
SLOTS = HP * NC
FI = 1024
AH, AD = 16, 16
E, EH, TOPK = 16, 128, 4
NSH = 4
NEG = -1e30


class PerSlot:

    def __init__(self, sem, n):
        self.sem, self.n = sem, n

    def after(self, s):
        return (s + 2) * self.n

    def step(self, s, k):
        return (s + 1) * self.n + k

    def before(self, s):
        return (s + 1) * self.n


class Counter:

    def __init__(self, sem):
        self.sem, self.v = sem, 0

    def bump(self, k=1):
        self.v += k
        return self.sem, k


class Tools:
    def __init__(self, nc, ctx):
        self.nc, self.ctx, self.phase = nc, ctx, []

    def sb(self, name, shape, dt=F32, ctx=None):
        return (ctx or self.ctx).enter_context(self.nc.sbuf_tensor(name, shape, dt))

    def sem(self, name, ctx=None):
        x = (ctx or self.ctx).enter_context(self.nc.semaphore(name))
        if ctx is not None:
            self.phase.append(x)
        return x

    def clear(self):
        with self.nc.Block() as block:
            @block.sync
            def _(sp):
                for x in self.phase:
                    sp.sem_clear(x)
        self.phase = []


def residual_and_norm(nc, tools, tag, bank, ident, half, X, Y, put, x_in=None, store=None):
    with ExitStack() as ctx:
        stats = tools.sb(tag + "_stats", [P, NC, B, 6], ctx=ctx)
        mv = tools.sb(tag + "_mv", [P, NC, B, 2], ctx=ctx)
        rstd = tools.sb(tag + "_rstd", [P, NC, B, 1], ctx=ctx)
        stats2 = tools.sb(tag + "_stats2", [P, NC, B, 6], ctx=ctx)
        mv2 = tools.sb(tag + "_mv2", [P, NC, B, 2], ctx=ctx)
        rstd2 = tools.sb(tag + "_rstd2", [P, NC, B, 1], ctx=ctx)
        normed = tools.sb(tag + "_normed", [P, B, D], ctx=ctx)
        yn = tools.sb(tag + "_yn", [P, NC, B, D], ctx=ctx) if Y else None
        x_loaded = tools.sem(tag + "_x_loaded")
        y_stats = tools.sem(tag + "_y_stats")
        y_aggr = tools.sem(tag + "_y_aggr")
        y_var = tools.sem(tag + "_y_var")
        y_rstd = tools.sem(tag + "_y_rstd")
        y_normed = tools.sem(tag + "_y_normed")
        x_added = tools.sem(tag + "_x_added")
        x_stats = tools.sem(tag + "_x_stats")
        x_aggr = tools.sem(tag + "_x_aggr")
        x_var = tools.sem(tag + "_x_var")
        x_rstd = tools.sem(tag + "_x_rstd")
        x_normed = tools.sem(tag + "_x_normed")
        transposed = tools.sem(tag + "_transposed")
        laid = tools.sem(tag + "_laid")
        stored = tools.sem(tag + "_stored")

        with nc.Block() as block:
            @block.sync
            def _(sp):
                if x_in is not None:
                    for b in range(B):
                        sp.dma_start(X[:, :, b, :], x_in[b].rearrange("(c p) d -> p c d", p=P)).then_inc(x_loaded, 16)
                if store is not None:
                    sp.wait_ge(x_added, NC * B)
                    for b in range(B):
                        sp.dma_start(store[b].rearrange("(c p) d -> p c d", p=P), X[:, :, b, :]).then_inc(stored, 16)
                    sp.wait_ge(stored, 16 * B)

            @block.vector
            def _(dve):
                if x_in is not None:
                    dve.wait_ge(x_loaded, 16 * B)
                if Y:
                    with dve.Fori(0, NC) as c:
                        for b in range(B):
                            nc.vector.bn_stats(stats[:, ds(c, 1), b, :], Y(c, b)).then_inc(y_stats, 1)
                    for t in range(NC * B):
                        dve.wait_ge(y_stats, t + 1)
                        nc.vector.bn_aggr(mv[:, t // B, t % B, :], stats[:, t // B, t % B, :]).then_inc(y_aggr, 1)
                    dve.wait_ge(y_aggr, NC * B)
                    nc.vector.tensor_scalar(rstd[:, :, :, 0], mv[:, :, :, 1], LN_EPS, None, ALU.add).then_inc(y_var, 1)
                    dve.wait_ge(y_rstd, 1)
                    with dve.Fori(0, NC) as c:
                        for b in range(B):
                            nc.vector.tensor_scalar(yn[:, ds(c, 1), b, :], Y(c, b), mv[:, ds(c, 1), b, 0:1],
                                                    rstd[:, ds(c, 1), b, :], ALU.subtract, ALU.mult).then_inc(y_normed, 1)
                        for b in range(B):
                            dve.wait_ge(y_normed, c * B + b + 1)
                            nc.vector.tensor_tensor(X[:, ds(c, 1), b, :], X[:, ds(c, 1), b, :], yn[:, ds(c, 1), b, :],
                                                    ALU.add).then_inc(x_added, 1)
                if put is None:
                    return
                with dve.Fori(0, NC) as c:
                    for b in range(B):
                        if Y:
                            dve.wait_ge(x_added, c * B + b + 1)
                        nc.vector.bn_stats(stats2[:, ds(c, 1), b, :], X[:, ds(c, 1), b, :]).then_inc(x_stats, 1)
                for t in range(NC * B):
                    dve.wait_ge(x_stats, t + 1)
                    nc.vector.bn_aggr(mv2[:, t // B, t % B, :], stats2[:, t // B, t % B, :]).then_inc(x_aggr, 1)
                dve.wait_ge(x_aggr, NC * B)
                nc.vector.tensor_scalar(rstd2[:, :, :, 0], mv2[:, :, :, 1], LN_EPS, None, ALU.add).then_inc(x_var, 1)
                dve.wait_ge(x_rstd, 1)
                for c in range(NC):
                    for b in range(B):
                        if c >= 1:
                            dve.wait_ge(transposed, (c - 1) * B + b + 1)
                        nc.vector.tensor_scalar(normed[:, b, :], X[:, c, b, :], mv2[:, c, b, 0:1], rstd2[:, c, b, :],
                                                ALU.subtract, ALU.mult).then_inc(x_normed, 1)

            @block.gpsimd
            def _(pool):
                if Y:
                    pool.wait_ge(y_var, 1)
                    nc.gpsimd.tensor_tensor(rstd[:, :, :, 0], rstd[:, :, :, 0],
                                            half[:, 0:1].broadcast_to([P, NC * B]).rearrange("p (c b) -> p c b", b=B),
                                            ALU.pow).then_inc(y_rstd, 1)
                if put is None:
                    return
                pool.wait_ge(x_var, 1)
                nc.gpsimd.tensor_tensor(rstd2[:, :, :, 0], rstd2[:, :, :, 0],
                                        half[:, 0:1].broadcast_to([P, NC * B]).rearrange("p (c b) -> p c b", b=B),
                                        ALU.pow).then_inc(x_rstd, 1)

            @block.tensor
            def _(pe):
                if put is None:
                    return
                for c in range(NC):
                    for b in range(B):
                        t = c * B + b
                        pe.wait_ge(x_normed, t + 1)
                        if t >= 2:
                            pe.wait_ge(laid, t - 1)
                        for k in range(KD):
                            last = nc.tensor.transpose(bank[t % 2][:, k * P:(k + 1) * P], normed[:, b, k * P:(k + 1) * P],
                                                       ident[:])
                        last.then_inc(transposed, 1)

            @block.scalar
            def _(act):
                if put is None:
                    return
                for c in range(NC):
                    for b in range(B):
                        t = c * B + b
                        act.wait_ge(transposed, t + 1)
                        put(act, c, b, bank[t % 2][:, 0:KD * P].rearrange("p (k n) -> p k n", k=KD)).then_inc(laid, 1)


def delta_rule(nc, tools, bank, cst, X, Xc, Acc, A_qkv, A_ab, A_conv, A_alog, A_dt, A_onorm, A_wo):
    ident, half, cumsum_mask, ones, ident16, causal16, level0, level0_t, level_masks = cst
    with ExitStack() as ctx:
        def sb(name, shape, dt=F32):
            return tools.sb("dr_" + name, shape, dt, ctx)

        def sem(name):
            return tools.sem("dr_" + name, ctx)

        Wab = sb("Wab", [P, KD, 2 * H])
        alog = sb("alog", [P, H])
        dtb = sb("dtb", [P, H])
        onorm = sb("onorm", [P, 1])
        z = sb("z", [P, NC * B, H])
        absz = sb("absz", [P, NC * B, H])
        g_all = sb("g_all", [P, NC * B, H])
        nG = sb("nG", [P, NC * B, H])
        eG = sb("eG", [P, NC * B, H])
        eGl = sb("eGl", [P, NC * B, H])
        beta = sb("beta", [P, NC * B, H])
        vecF_all = sb("vecF_all", [P, SLOTS, 3, U])
        vecB_all = sb("vecB_all", [P, SLOTS + 1, 3, U])
        ab_loaded = sem("ab_loaded")
        ab_ready = sem("ab_ready")
        sums_ready = sem("sums_ready")
        alog_exp = sem("alog_exp")
        abs_steps = sem("abs_steps")
        soft_exp = sem("soft_exp")
        soft_ln = sem("soft_ln")
        g_steps = sem("g_steps")
        beta_exp = sem("beta_exp")
        beta_steps = sem("beta_steps")
        G_neg = sem("G_neg")
        G_exp = sem("G_exp")
        firsts_cleared = sem("firsts_cleared")
        spread_done = sem("spread_done")

        with nc.Block() as block:
            @block.sync
            def _(sp):
                sp.dma_start(Wab[:], A_ab[:, 0:2 * H].rearrange("(k p) n -> p k n", p=P)).then_inc(ab_loaded, 16)
                sp.dma_start(alog[:], A_alog.partition_broadcast(P)).then_inc(ab_loaded, 16)
                sp.dma_start(dtb[:], A_dt.partition_broadcast(P)).then_inc(ab_loaded, 16)
                sp.dma_start(onorm[:], A_onorm.rearrange("(p a) -> p a", a=1)).then_inc(ab_loaded, 16)

            @block.tensor
            def _(pe):
                pe.wait_ge(ab_loaded, 64)
                for c in range(NC):
                    for b in range(B):
                        t = (c * B + b) * 2 * H
                        for k in range(KD):
                            last = nc.tensor.matmul(bank[0][:, t:t + 2 * H], Xc[:, c, k, b, HALO:CW], Wab[:, k, :],
                                                    start=(t == 0 and k == 0), stop=(k == KD - 1), skip_group_check=True)
                last.then_inc(ab_ready, 1)
                pe.wait_ge(g_steps, 3)
                gf = g_all[:].rearrange("p t h -> p (t h)")
                nc.tensor.matmul(bank[1][:, 0:NC * B * H], cumsum_mask[:], gf, start=True, stop=True).then_inc(sums_ready, 1)
                nc.tensor.matmul(bank[2][:, 0:NC * B * H], ones[:], gf, start=True, stop=True).then_inc(sums_ready, 1)

            ab = bank[0][:, :].rearrange("p (t n) -> p t n", n=2 * H)
            running = bank[1][:, 0:NC * B * H].rearrange("p (t h) -> p t h", h=H)
            whole = bank[2][:, 0:NC * B * H].rearrange("p (t h) -> p t h", h=H)

            @block.scalar
            def _(act):
                act.wait_ge(ab_loaded, 64)
                nc.scalar.activation(alog[:], alog[:], ACT.Exp).then_inc(alog_exp, 1)
                act.wait_ge(abs_steps, 3)
                nc.scalar.activation(absz[:], absz[:], ACT.Exp).then_inc(soft_exp, 1)
                nc.scalar.activation(beta[:], ab[:, :, H:2 * H], ACT.Exp, scale=-1.0).then_inc(beta_exp, 1)
                act.wait_ge(soft_exp, 1)
                nc.scalar.activation(absz[:], absz[:], ACT.Ln, bias=1.0).then_inc(soft_ln, 1)
                act.wait_ge(sums_ready, 2)
                act.wait_ge(G_neg, 1)
                nc.scalar.activation(eG[:], running, ACT.Exp).then_inc(G_exp, 1)
                nc.scalar.activation(eGl[:], whole, ACT.Exp).then_inc(G_exp, 1)

            @block.vector
            def _(dve):
                dve.wait_ge(ab_ready, 1)
                dve.wait_ge(alog_exp, 1)
                dtb_all = dtb[:].rearrange("p (a h) -> p a h", a=1).broadcast_to([P, NC * B, H])
                alog_all = alog[:].rearrange("p (a h) -> p a h", a=1).broadcast_to([P, NC * B, H])
                nc.vector.tensor_tensor(z[:], ab[:, :, 0:H], dtb_all, ALU.add).then_inc(abs_steps, 1)
                dve.wait_ge(abs_steps, 1)
                nc.vector.tensor_scalar(absz[:], z[:], -1.0, None, ALU.mult).then_inc(abs_steps, 1)
                dve.wait_ge(abs_steps, 2)
                nc.vector.tensor_tensor(absz[:], z[:], absz[:], ALU.min).then_inc(abs_steps, 1)
                dve.wait_ge(soft_ln, 1)
                nc.vector.scalar_tensor_tensor(g_all[:], z[:], 0.0, absz[:], ALU.max, ALU.add).then_inc(g_steps, 1)
                dve.wait_ge(g_steps, 1)
                nc.vector.tensor_tensor(g_all[:], g_all[:], alog_all, ALU.mult).then_inc(g_steps, 1)
                dve.wait_ge(g_steps, 2)
                nc.vector.tensor_scalar(g_all[:], g_all[:], -1.0, None, ALU.mult).then_inc(g_steps, 1)
                dve.wait_ge(beta_exp, 1)
                nc.vector.tensor_scalar(beta[:], beta[:], 1.0, None, ALU.add).then_inc(beta_steps, 1)
                dve.wait_ge(beta_steps, 1)
                nc.vector.reciprocal(beta[:], beta[:]).then_inc(beta_steps, 1)
                dve.wait_ge(beta_steps, 2)
                nc.vector.tensor_scalar(beta[:], beta[:], -2.0, None, ALU.mult).then_inc(beta_steps, 1)
                dve.wait_ge(sums_ready, 1)
                nc.vector.tensor_scalar(nG[:], running, -1.0, None, ALU.mult).then_inc(G_neg, 1)
                dve.wait_ge(G_exp, 2)
                nc.vector.memset(eG[:, 0:B, :], 0.0).then_inc(firsts_cleared, 1)
                nc.vector.memset(eGl[:, 0:B, :], 0.0).then_inc(firsts_cleared, 1)
                nc.vector.memset(vecB_all[:, 0, :, :], 0.0).then_inc(spread_done, 1)

                def spread(dst, src):
                    for b in range(B):
                        for hh in range(2):
                            nc.vector.tensor_copy(
                                dst[:, :, 2 * b + hh].rearrange("p (q c) -> p q c", c=NC),
                                src[:].rearrange("p (c b) h -> p b h c", b=B)[:, b, hh::2, :]).then_inc(spread_done, 1)

                dve.wait_ge(firsts_cleared, 2)
                dve.wait_ge(beta_steps, 3)
                dve.wait_ge(G_neg, 1)
                spread(vecF_all[:, :, 0, :], beta)
                spread(vecF_all[:, :, 1, :], g_all)
                spread(vecF_all[:, :, 2, :], nG)
                spread(vecB_all[:, 1:, 1, :], eG)
                spread(vecB_all[:, 1:, 2, :], eGl)
                dve.wait_ge(spread_done, 1 + 5 * U)
                nc.vector.tensor_scalar(vecB_all[:, 1:, 0, :], vecB_all[:, 1:, 1, :], -1.0, None,
                                        ALU.mult).then_inc(spread_done, 1)

        Wp = sb("Wp", [P, KD, 4, 2, P])
        Wo = sb("Wo", [P, 2, D])
        cw = sb("cw", [P, 2, 3, TAPS])
        xc = sb("xc", [P, KD, B, CW])
        conv = sb("conv", [P, 3, U, P])
        vecF = sb("vecF", [P, 3, U])
        vecB = sb("vecB", [P, 3, U])
        QK = sb("QK", [P, 2, U, P])
        Vt = sb("Vt", [P, U, P])
        QKsq = sb("QKsq", [P, 2, U, P])
        Ktok = sb("Ktok", [P, U, P])
        Vn = sb("Vn", [P, U, P])
        gate_next = sb("gate_next", [P, U, P])
        gate_this = sb("gate_this", [P, U, P])
        gate = sb("gate", [P, U, P])
        ss = sb("ss", [P, 2 * U])
        rs = sb("rs", [P, 2 * U])
        nk = sb("nk", [P, U])
        rk2 = sb("rk2", [P, U])
        negc = sb("negc", [P, U])
        w_next = sb("w_next", [P, U])
        w = sb("w", [P, U])
        rq = sb("rq", [P, U])
        Ex = sb("Ex", [P, U, P])
        AM = sb("AM", [P, U, 2, P])
        Tm = sb("Tm", [P, U, P])
        Xm = sb("Xm", [P, U, P])
        Lv = sb("Lv", [P, LEVELS - 1, U, P])
        RHS = sb("RHS", [P, U, P])
        Y = sb("Y", [P, U, P])
        Yw = sb("Yw", [P, U, P])
        QSg = sb("QSg", [P, U, P])
        O = sb("O", [P, U, P])
        Z = sb("Z", [P, U, P])
        Zsq = sb("Zsq", [P, U, P])
        ssz = sb("ssz", [P, U])
        f1 = sb("f1", [P, U])
        f2 = sb("f2", [P, U])
        f3 = sb("f3", [P, U])
        f4 = sb("f4", [P, U])
        f = sb("f", [P, U])
        Zf = sb("Zf", [P, U, P])
        ZT = sb("ZT", [P, U, P])
        S = sb("S", [P, U, P])
        half_u = half[:, 0:1].broadcast_to([P, 2 * U])

        credited = []

        def per_slot(name, n, credit=True):
            x = PerSlot(sem(name), n)
            if credit:
                credited.append(x)
            return x

        vecF_in = per_slot("vecF_in", 1)
        vecB_in = per_slot("vecB_in", 1)
        xc_in = PerSlot(sem("xc_in"), 1)
        W_ok = PerSlot(sem("W_ok"), 1)
        Wo_ok = PerSlot(sem("Wo_ok"), 1)
        W_dma = sem("W_dma")
        Wo_dma = sem("Wo_dma")
        projected = per_slot("projected", 6, credit=False)
        convolved = per_slot("convolved", 6, credit=False)
        taps = sem("taps")
        gate_projected = per_slot("gate_projected", 1, credit=False)
        gate_kept = per_slot("gate_kept", 1, credit=False)
        gate_moved = per_slot("gate_moved", 1)
        qk_silu = per_slot("qk_silu", 1)
        v_silu = per_slot("v_silu", 1)
        k_turned = per_slot("k_turned", 1)
        k_copied = per_slot("k_copied", 1)
        v_turned = per_slot("v_turned", 1)
        v_scaled = per_slot("v_scaled", 1)
        qk_squared = per_slot("qk_squared", 1)
        ss_ready = per_slot("ss_ready", 1)
        ss_copied = per_slot("ss_copied", 1)
        rs_ready = per_slot("rs_ready", 1)
        nk_ready = per_slot("nk_ready", 1)
        rk2_ready = per_slot("rk2_ready", 1)
        c_ready = per_slot("c_ready", 1)
        kq_ready = per_slot("kq_ready", 2)
        decay_ready = per_slot("decay_ready", 1)
        exp_ready = per_slot("exp_ready", 1)
        am_ready = per_slot("am_ready", U)
        diag_filled = per_slot("diag_filled", 1)
        x0_ready = per_slot("x0_ready", 1)
        w_ready = per_slot("w_ready", 1)
        at_ready = per_slot("at_ready", 2 * LEVELS)
        masked = per_slot("masked", 2 * LEVELS)
        tx_ready = per_slot("tx_ready", 2 * (LEVELS - 1))
        tx_copied = per_slot("tx_copied", 2 * (LEVELS - 1))
        gate_silu = per_slot("gate_silu", 1)
        ks_ready = per_slot("ks_ready", 1)
        qs_ready = per_slot("qs_ready", 1)
        rhs_ready = per_slot("rhs_ready", U)
        qs_scaled = per_slot("qs_scaled", 1)
        y_ready = per_slot("y_ready", 1)
        y_copied = per_slot("y_copied", 1)
        my_ready = per_slot("my_ready", 1)
        yw_ready = per_slot("yw_ready", 1)
        su_ready = per_slot("su_ready", 1)
        s_updated = per_slot("s_updated", 1)
        o_ready = per_slot("o_ready", 1)
        z_ready = per_slot("z_ready", 1)
        z_squared = per_slot("z_squared", 1)
        f_steps = per_slot("f_steps", 5)
        carried = per_slot("carried", 2)
        z_scaled = per_slot("z_scaled", 1)
        z_turned = per_slot("z_turned", 1)
        zt_copied = per_slot("zt_copied", 1)
        out_ready = per_slot("out_ready", 1)
        out_added = per_slot("out_added", 1)
        cleared = sem("cleared")
        settles = sem("settles")

        grp = lambda t, gi: t[:, 2 * gi:2 * gi + 2]

        def halves(ap, n):
            v = ap.rearrange("p u (m two n) -> p u m two n", two=2, n=n)
            return v[:, :, :, 0, :], v[:, :, :, 1, :]

        with nc.Block() as block:
            @block.gpsimd
            def _(pool):
                for t in (QK, Vn, Xm, AM, Ktok, S, gate_this):
                    nc.gpsimd.memset(t[:], 0.0)
                for t in (w, rq, w_next, rs, vecB):
                    nc.gpsimd.memset(t[:], 0.0)
                nc.gpsimd.memset(Acc[:], 0.0)
                for l in range(LEVELS - 1):
                    nc.gpsimd.tensor_copy(Lv[:, l, :, :], ident[:].rearrange("p (a n) -> p a n", a=1).broadcast_to([P, U, P]))
                nc.gpsimd.memset(Wo[:], 0.0).then_inc(cleared, 1)

            @block.sync
            def _(sp):
                for x in credited:
                    sp.sem_inc(x.sem, x.n)
                sp.sem_inc(Wo_ok.sem, 1)

        with nc.Block() as block:
            @block.sync
            def _(sp):
                def load_pair(hp):
                    for k in range(KD):
                        for kind, t in enumerate(KINDS):
                            sp.dma_start(Wp[:, k, kind, :, :], A_qkv[k * P:(k + 1) * P, ds(t * H * DK + hp * 2 * DK, 2 * DK)]
                                         .rearrange("p (h n) -> p h n", h=2)).then_inc(W_dma, 16)
                        sp.dma_start(Wp[:, k, 3, :, :], A_ab[k * P:(k + 1) * P, ds(2 * H + hp * 2 * DK, 2 * DK)]
                                     .rearrange("p (h n) -> p h n", h=2)).then_inc(W_dma, 16)
                    for kind, t in enumerate(KINDS):
                        for hh in range(2):
                            sp.dma_start(cw[:, hh, kind, :], A_conv[ds(t * H * DK + (hp * 2 + hh) * DK, DK), :]).then_inc(W_dma, 16)

                LOADS = 4 * KD + 6
                load_pair(0)
                sp.wait_ge(W_dma, 16 * LOADS)
                sp.sem_inc(W_ok.sem, NC)
                with sp.Fori(0, HP - 1) as q:
                    sp.wait_ge(out_ready.sem, out_ready.after(q * NC))
                    sp.dma_start(Wo[:], A_wo[ds(q * 2 * DK, 2 * DK), :].rearrange("(h p) n -> p h n", p=P)).then_inc(Wo_dma, 16)
                    sp.wait_ge(Wo_dma, (q + 1) * 16)
                    sp.sem_inc(Wo_ok.sem, NC)
                    last = q * NC + NC - 2
                    sp.wait_ge(projected.sem, projected.after(last))
                    sp.wait_ge(gate_projected.sem, gate_projected.after(last))
                    sp.wait_ge(convolved.sem, convolved.after(last))
                    load_pair(q + 1)
                    sp.wait_ge(W_dma, (q + 2) * 16 * LOADS)
                    sp.sem_inc(W_ok.sem, NC)
                q = HP - 1
                sp.sem_inc(W_ok.sem, 1)
                sp.wait_ge(out_ready.sem, out_ready.after(q * NC))
                sp.dma_start(Wo[:], A_wo[ds(q * 2 * DK, 2 * DK), :].rearrange("(h p) n -> p h n", p=P)).then_inc(Wo_dma, 16)
                sp.wait_ge(Wo_dma, (q + 1) * 16)
                sp.sem_inc(Wo_ok.sem, NC)

            @block.gpsimd
            def _(pool):
                def settled():
                    pool.sem_inc(settles, 1)

                def stage_x(c):
                    settled()
                    nc.gpsimd.tensor_copy(xc[:].rearrange("p k b n -> p (k b n)"),
                                          Xc[:, ds(c, 1), :, :, :].rearrange("p a k b n -> p (a k b n)")
                                          ).then_inc(xc_in.sem, 1)

                def stage_back(s):
                    pool.wait_ge(rhs_ready.sem, rhs_ready.before(s))
                    pool.wait_ge(qs_scaled.sem, qs_scaled.before(s))
                    pool.wait_ge(s_updated.sem, s_updated.before(s))
                    settled()
                    nc.gpsimd.tensor_copy(vecB[:], vecB_all[:, ds(s, 1), :, :].rearrange("p a v u -> p (a v) u")
                                          ).then_inc(vecB_in.sem, 1)

                def out_factors(s):
                    pool.wait_ge(z_squared.sem, z_squared.after(s))
                    pool.wait_ge(z_scaled.sem, z_scaled.before(s))
                    nc.gpsimd.tensor_tensor(f1[:], ssz[:], rq[:], ALU.mult).then_inc(f_steps.sem, 1)
                    pool.wait_ge(f_steps.sem, f_steps.step(s, 1))
                    nc.gpsimd.tensor_tensor(f2[:], f1[:], rq[:], ALU.mult).then_inc(f_steps.sem, 1)
                    pool.wait_ge(f_steps.sem, f_steps.step(s, 2))
                    settled()
                    nc.gpsimd.tensor_scalar(f3[:], f2[:], 1.0 / DK, LN_EPS * DK, ALU.mult, ALU.add).then_inc(f_steps.sem, 1)
                    pool.wait_ge(f_steps.sem, f_steps.step(s, 3))
                    nc.gpsimd.tensor_tensor(f4[:], f3[:], half_u[:, 0:U], ALU.pow).then_inc(f_steps.sem, 1)
                    pool.wait_ge(f_steps.sem, f_steps.step(s, 4))
                    nc.gpsimd.tensor_tensor(f[:], f4[:], rq[:], ALU.mult).then_inc(f_steps.sem, 1)

                stage_x(0)
                with pool.Fori(0, HP) as q:
                    with pool.Fori(0, NC) as c:
                        s = q * NC + c
                        stage_back(s)
                        pool.wait_ge(exp_ready.sem, exp_ready.before(s))
                        pool.wait_ge(decay_ready.sem, decay_ready.before(s))
                        settled()
                        nc.gpsimd.tensor_copy(vecF[:], vecF_all[:, ds(s, 1), :, :].rearrange("p a v u -> p (a v) u")
                                              ).then_inc(vecF_in.sem, 1)
                        pool.wait_ge(projected.sem, projected.before(s))
                        pool.wait_ge(gate_projected.sem, gate_projected.before(s))
                        stage_x(c + 1)
                        pool.wait_ge(gate_silu.sem, gate_silu.after(s))
                        pool.wait_ge(gate_kept.sem, gate_kept.before(s))
                        settled()
                        nc.gpsimd.tensor_copy(gate_this[:], gate_next[:]).then_inc(gate_moved.sem, 1)
                        pool.wait_ge(qk_silu.sem, qk_silu.after(s))
                        pool.wait_ge(ss_ready.sem, ss_ready.before(s))
                        nc.gpsimd.tensor_tensor(QKsq[:], QK[:], QK[:], ALU.mult).then_inc(qk_squared.sem, 1)
                        pool.wait_ge(ss_copied.sem, ss_copied.after(s))
                        nc.gpsimd.tensor_tensor(rs[:], ss[:], half_u, ALU.pow).then_inc(rs_ready.sem, 1)
                        pool.wait_ge(rs_ready.sem, rs_ready.after(s))
                        pool.wait_ge(v_scaled.sem, v_scaled.before(s))
                        nc.gpsimd.tensor_tensor(nk[:], ss[:, 0:U], rs[:, 0:U], ALU.mult).then_inc(nk_ready.sem, 1)
                        nc.gpsimd.tensor_tensor(rk2[:], rs[:, 0:U], rs[:, 0:U], ALU.mult).then_inc(rk2_ready.sem, 1)
                        pool.wait_ge(rk2_ready.sem, rk2_ready.after(s))
                        pool.wait_ge(am_ready.sem, am_ready.before(s))
                        pool.wait_ge(vecF_in.sem, vecF_in.after(s))
                        nc.gpsimd.tensor_tensor(negc[:], rk2[:], vecF[:, 0, :], ALU.mult).then_inc(c_ready.sem, 1)
                        pool.wait_ge(am_ready.sem, am_ready.after(s))
                        settled()
                        nc.gpsimd.affine_select(out=AM[:, :, 0, :], in_=AM[:, :, 0, :], compare_op=ALU.not_equal, fill=1.0,
                                                base=0, pattern=[[0, U], [-1, P]], channel_multiplier=1
                                                ).then_inc(diag_filled.sem, 1)
                        pool.wait_ge(diag_filled.sem, diag_filled.after(s))
                        pool.wait_ge(y_ready.sem, y_ready.after(s))
                        nc.gpsimd.tensor_tensor(Xm[:], AM[:, :, 0, :],
                                                level0_t[:].rearrange("p (a n) -> p a n", a=1).broadcast_to([P, U, P]),
                                                ALU.mult).then_inc(x0_ready.sem, 1)
                        pool.wait_ge(carried.sem, carried.before(s))
                        nc.gpsimd.tensor_tensor(w_next[:], Ex[:, :, P - 1], negc[:], ALU.mult).then_inc(w_ready.sem, 1)
                        out_factors(s)
                        pool.wait_ge(yw_ready.sem, yw_ready.after(s))
                        pool.wait_ge(w_ready.sem, w_ready.after(s))
                        pool.wait_ge(f_steps.sem, f_steps.after(s))
                        settled()
                        nc.gpsimd.tensor_copy(w[:], w_next[:]).then_inc(carried.sem, 1)
                        settled()
                        nc.gpsimd.tensor_copy(rq[:], rs[:, U:2 * U]).then_inc(carried.sem, 1)
                stage_back(SLOTS)
                out_factors(SLOTS)

            @block.scalar
            def _(act):
                def gate_to_silu(s):
                    act.wait_ge(gate_moved.sem, gate_moved.before(s))
                    act.wait_ge(z_ready.sem, z_ready.before(s))
                    nc.scalar.activation(gate[:], gate_this[:], ACT.Silu).then_inc(gate_silu.sem, 1)

                def keep_gate(s):
                    act.wait_ge(gate_projected.sem, gate_projected.after(s))
                    act.wait_ge(gate_moved.sem, gate_moved.after(s))
                    nc.scalar.activation(gate_next[:], bank[4][:].rearrange("p (u n) -> p u n", u=U), ACT.Copy
                                         ).then_inc(gate_kept.sem, 1)

                def back_1(s):
                    act.wait_ge(qs_ready.sem, qs_ready.after(s))
                    act.wait_ge(vecB_in.sem, vecB_in.after(s))
                    act.wait_ge(o_ready.sem, o_ready.before(s))
                    for u in range(U):
                        last = nc.scalar.activation(QSg[:, u, :], bank[6][:, u * P:(u + 1) * P], ACT.Copy,
                                                    scale=vecB[:, 1, u:u + 1])
                    last.then_inc(qs_scaled.sem, 1)
                    act.wait_ge(y_ready.sem, y_ready.after(s))
                    act.wait_ge(my_ready.sem, my_ready.before(s))
                    act.wait_ge(yw_ready.sem, yw_ready.before(s))
                    nc.scalar.activation(Y[:], bank[5][:].rearrange("p (u n) -> p u n", u=U), ACT.Copy).then_inc(y_copied.sem, 1)

                def back_2(s):
                    act.wait_ge(z_ready.sem, z_ready.after(s))
                    act.wait_ge(f_steps.sem, f_steps.before(s))
                    for u in range(U):
                        last = nc.scalar.activation(Zsq[:, u, :], Z[:, u, :], ACT.Square, accum_out=ssz[:, u:u + 1])
                    last.then_inc(z_squared.sem, 1)

                def back_3(s):
                    act.wait_ge(f_steps.sem, f_steps.after(s))
                    act.wait_ge(z_turned.sem, z_turned.before(s))
                    for u in range(U):
                        last = nc.scalar.activation(Zf[:, u, :], Z[:, u, :], ACT.Copy, scale=f[:, u:u + 1])
                    last.then_inc(z_scaled.sem, 1)

                def back_4(s):
                    act.wait_ge(z_turned.sem, z_turned.after(s))
                    act.wait_ge(out_ready.sem, out_ready.before(s))
                    nc.scalar.activation(ZT[:], bank[7][:].rearrange("p (u n) -> p u n", u=U), ACT.Copy,
                                         scale=onorm[:, 0:1]).then_inc(zt_copied.sem, 1)

                def copy_level(s, l, gi):
                    n = 1 << l
                    i = 2 * (l - 1) + gi
                    act.wait_ge(tx_ready.sem, tx_ready.step(s, i + 1))
                    b = bank[2 + gi]
                    t1, _ = halves(grp(Tm, gi), n)
                    _, x2 = halves(grp(Xm, gi), n)
                    if l < LEVELS - 1:
                        nc.scalar.activation(t1, b[:, 128:256].rearrange("p (u m n) -> p u m n", u=2, n=n), ACT.Copy)
                    nc.scalar.activation(x2, b[:, 256:384].rearrange("p (u m n) -> p u m n", u=2, n=n), ACT.Copy
                                         ).then_inc(tx_copied.sem, 1)

                keep_gate(-1)
                with act.Fori(0, HP) as q:
                    with act.Fori(0, NC) as c:
                        s = q * NC + c
                        gate_to_silu(s)
                        act.wait_ge(convolved.sem, convolved.before(s))
                        act.wait_ge(qs_ready.sem, qs_ready.after(s))
                        act.wait_ge(qk_squared.sem, qk_squared.before(s))
                        nc.scalar.activation(QK[:], conv[:, 0:2, :, :], ACT.Silu).then_inc(qk_silu.sem, 1)
                        nc.scalar.activation(Vt[:], conv[:, 2, :, :], ACT.Silu).then_inc(v_silu.sem, 1)
                        back_1(s)
                        act.wait_ge(decay_ready.sem, decay_ready.after(s))
                        act.wait_ge(w_ready.sem, w_ready.before(s))
                        for u in range(U):
                            last = nc.scalar.activation(Ex[:, u, :], bank[0][:, u * P:(u + 1) * P], ACT.Exp,
                                                        bias=vecF[:, 2, u:u + 1])
                        last.then_inc(exp_ready.sem, 1)
                        act.wait_ge(k_turned.sem, k_turned.after(s))
                        act.wait_ge(su_ready.sem, su_ready.after(s))
                        nc.scalar.activation(Ktok[:], bank[7][:].rearrange("p (u n) -> p u n", u=U), ACT.Copy
                                             ).then_inc(k_copied.sem, 1)
                        back_2(s)
                        for l in range(1, LEVELS):
                            for gi in range(2):
                                copy_level(s, l, gi)
                            if l == 2:
                                back_3(s)
                            if l == 3:
                                back_4(s)
                        keep_gate(s)
                s = SLOTS
                gate_to_silu(s)
                back_1(s)
                back_2(s)
                back_3(s)
                back_4(s)

            @block.vector
            def _(dve):
                tap_count = [0]

                def convolve(s, i):
                    kind, hh = i // 2, i % 2
                    dve.wait_ge(projected.sem, projected.step(s, i + 1))
                    if i == 0:
                        dve.wait_ge(W_ok.sem, s + 2)
                        dve.wait_ge(qk_silu.sem, qk_silu.after(s))
                        dve.wait_ge(v_silu.sem, v_silu.after(s))
                    src = bank[i % 2][:, 0:B * CW].rearrange("p (b n) -> p b n", b=B)
                    out = conv[:, kind, hh::2, :]
                    n = (TAPS - 1) * i
                    nc.vector.tensor_scalar(out, src[:, :, 0:P], cw[:, hh, kind, 0:1], None, ALU.mult).then_inc(taps, 1)
                    for j in range(1, TAPS):
                        dve.wait_ge(taps, (s + 1) * 18 + n + j)
                        ins = nc.vector.scalar_tensor_tensor(out, src[:, :, j:j + P], cw[:, hh, kind, j:j + 1], out,
                                                             ALU.mult, ALU.add)
                        ins.then_inc(*((taps, 1) if j < TAPS - 1 else (convolved.sem, 1)))

                def back_1(s):
                    dve.wait_ge(ks_ready.sem, ks_ready.after(s))
                    dve.wait_ge(vecB_in.sem, vecB_in.after(s))
                    dve.wait_ge(v_scaled.sem, v_scaled.before(s))
                    for u in range(U):
                        nc.vector.scalar_tensor_tensor(RHS[:, u, :], bank[5][:, u * P:(u + 1) * P], vecB[:, 0, u:u + 1],
                                                       Vn[:, u, :], ALU.mult, ALU.add).then_inc(rhs_ready.sem, 1)
                    dve.wait_ge(y_copied.sem, y_copied.after(s))
                    dve.wait_ge(carried.sem, carried.before(s))
                    nc.vector.tensor_tensor(Yw[:], Y[:], w[:].rearrange("p (u a) -> p u a", a=1).broadcast_to([P, U, P]),
                                            ALU.mult).then_inc(yw_ready.sem, 1)
                    dve.wait_ge(su_ready.sem, su_ready.after(s))
                    for u in range(U):
                        last = nc.vector.scalar_tensor_tensor(S[:, u, :], S[:, u, :], vecB[:, 2, u:u + 1],
                                                              bank[5][:, u * P:(u + 1) * P], ALU.mult, ALU.subtract)
                    last.then_inc(s_updated.sem, 1)
                    dve.wait_ge(my_ready.sem, my_ready.after(s))
                    dve.wait_ge(qs_scaled.sem, qs_scaled.after(s))
                    nc.vector.tensor_tensor(O[:], QSg[:], bank[6][:].rearrange("p (u n) -> p u n", u=U),
                                            ALU.subtract).then_inc(o_ready.sem, 1)
                    dve.wait_ge(o_ready.sem, o_ready.after(s))
                    dve.wait_ge(gate_silu.sem, gate_silu.after(s))
                    dve.wait_ge(z_scaled.sem, z_scaled.before(s))
                    nc.vector.tensor_tensor(Z[:], O[:], gate[:], ALU.mult).then_inc(z_ready.sem, 1)

                def back_2(s, acc):
                    dve.wait_ge(out_ready.sem, out_ready.after(s))
                    nc.vector.tensor_tensor(acc, acc, bank[7][:], ALU.add).then_inc(out_added.sem, 1)

                def mask_level(s, l, gi):
                    n = 1 << l
                    i = 2 * l + gi
                    dve.wait_ge(at_ready.sem, at_ready.step(s, i + 1))
                    b = bank[2 + gi]
                    if l == 0:
                        nc.vector.tensor_tensor(grp(Tm, gi), b[:, 0:2 * P].rearrange("p (u n) -> p u n", u=2),
                                                level0[:].rearrange("p (a n) -> p a n", a=1).broadcast_to([P, 2, P]),
                                                ALU.mult).then_inc(masked.sem, 1)
                        return
                    for u in range(2):
                        l1, _ = halves(Lv[:, l - 1, 2 * gi + u:2 * gi + u + 1, :], n)
                        last = nc.vector.tensor_tensor(l1[:, 0], b[:, u * 64:(u + 1) * 64].rearrange("p (m n) -> p m n", n=n),
                                                       level_masks[:, l - 1, :].rearrange("p (m n) -> p m n", n=n), ALU.mult)
                    last.then_inc(masked.sem, 1)

                for i in range(6):
                    convolve(-1, i)
                with dve.Fori(0, HP) as q:
                    with dve.Fori(0, NC) as c:
                        s = q * NC + c
                        back_1(s)
                        dve.wait_ge(ss_ready.sem, ss_ready.after(s))
                        dve.wait_ge(nk_ready.sem, nk_ready.before(s))
                        nc.vector.tensor_scalar(ss[:], bank[1][:, 0:2 * U], L2_EPS, None, ALU.add).then_inc(ss_copied.sem, 1)
                        dve.wait_ge(v_turned.sem, v_turned.after(s))
                        dve.wait_ge(nk_ready.sem, nk_ready.after(s))
                        nc.vector.tensor_tensor(Vn[:], bank[4][:].rearrange("p (u n) -> p u n", u=U),
                                                nk[:].rearrange("p (u a) -> p u a", a=1).broadcast_to([P, U, P]),
                                                ALU.mult).then_inc(v_scaled.sem, 1)
                        dve.wait_ge(exp_ready.sem, exp_ready.after(s))
                        dve.wait_ge(c_ready.sem, c_ready.after(s))
                        dve.wait_ge(my_ready.sem, my_ready.after(s))
                        for u in range(U):
                            dve.wait_ge(kq_ready.sem, kq_ready.step(s, u // 2 + 1))
                            o = (u % 2) * 2 * P
                            nc.vector.scalar_tensor_tensor(
                                AM[:, u, :, :], bank[2 + u // 2][:, o:o + 2 * P].rearrange("p (a n) -> p a n", a=2),
                                negc[:, u:u + 1], Ex[:, u:u + 1, :].broadcast_to([P, 2, P]),
                                ALU.mult, ALU.mult).then_inc(am_ready.sem, 1)
                        for l in range(LEVELS):
                            for gi in range(2):
                                mask_level(s, l, gi)
                            if l >= 1:
                                convolve(s, l - 1)
                        back_2(s, Acc[:, ds(c, 1), :, :].rearrange("p a b d -> p (a b d)"))
                s = SLOTS
                back_1(s)
                back_2(s, Acc[:, 0, :, :].rearrange("p b d -> p (b d)"))

            @block.tensor
            def _(pe):
                def project(s, i):
                    kind, hh = i // 2, i % 2
                    if i == 0:
                        pe.wait_ge(W_ok.sem, s + 2)
                        pe.wait_ge(xc_in.sem, s + 2)
                        pe.wait_ge(exp_ready.sem, exp_ready.after(s))
                    elif i == 1:
                        pe.wait_ge(ss_copied.sem, ss_copied.after(s))
                    else:
                        pe.wait_ge(convolved.sem, convolved.step(s, i - 1))
                    for k in range(KD):
                        last = nc.tensor.matmul(bank[i % 2][:, 0:B * CW].rearrange("p (b n) -> p b n", b=B),
                                                Wp[:, k, kind, hh, :], xc[:, k, :, :], start=(k == 0), stop=(k == KD - 1))
                    last.then_inc(projected.sem, 1)

                def project_gate(s):
                    pe.wait_ge(v_scaled.sem, v_scaled.after(s))
                    for b in range(B):
                        for k in range(KD):
                            last = nc.tensor.matmul(bank[4][:, b * 2 * P:(b + 1) * 2 * P], xc[:, k, b, HALO:CW],
                                                    Wp[:, k, 3, :, :], start=(b == 0 and k == 0), stop=(k == KD - 1),
                                                    skip_group_check=True)
                    last.then_inc(gate_projected.sem, 1)

                def each_unit(dst, lhs, rhs):
                    for u in range(U):
                        last = nc.tensor.matmul(dst[:, u * P:(u + 1) * P], lhs(u), rhs(u), start=True, stop=True)
                    return last

                def back_1(s):
                    pe.wait_ge(s_updated.sem, s_updated.before(s))
                    pe.wait_ge(o_ready.sem, o_ready.before(s))
                    each_unit(bank[5], lambda u: QK[:, 0, u, :], lambda u: S[:, u, :]).then_inc(ks_ready.sem, 1)
                    each_unit(bank[6], lambda u: QK[:, 1, u, :], lambda u: S[:, u, :]).then_inc(qs_ready.sem, 1)

                def back_2(s):
                    pe.wait_ge(rhs_ready.sem, rhs_ready.after(s))
                    pe.wait_ge(tx_copied.sem, tx_copied.before(s))
                    each_unit(bank[5], lambda u: Xm[:, u, :], lambda u: RHS[:, u, :]).then_inc(y_ready.sem, 1)

                def back_3(s):
                    pe.wait_ge(y_copied.sem, y_copied.after(s))
                    pe.wait_ge(qs_scaled.sem, qs_scaled.after(s))
                    each_unit(bank[6], lambda u: AM[:, u, 1, :], lambda u: Y[:, u, :]).then_inc(my_ready.sem, 1)
                    pe.wait_ge(yw_ready.sem, yw_ready.after(s))
                    each_unit(bank[5], lambda u: Ktok[:, u, :], lambda u: Yw[:, u, :]).then_inc(su_ready.sem, 1)

                def turn_z(s, loop=True):
                    if loop:
                        pe.wait_ge(k_copied.sem, k_copied.after(s))
                    pe.wait_ge(z_scaled.sem, z_scaled.after(s))
                    for u in range(U):
                        last = nc.tensor.transpose(bank[7][:, u * P:(u + 1) * P], Zf[:, u, :], ident[:])
                    last.then_inc(z_turned.sem, 1)

                def output(s):
                    pe.wait_ge(zt_copied.sem, zt_copied.after(s))
                    pe.wait_ge(Wo_ok.sem, s + 1)
                    for b in range(B):
                        for hh in range(2):
                            last = nc.tensor.matmul(bank[7][:, b * D:(b + 1) * D], ZT[:, 2 * b + hh, :], Wo[:, hh, :],
                                                    start=(b == 0 and hh == 0), stop=(hh == 1), skip_group_check=True)
                    last.then_inc(out_ready.sem, 1)

                def multiply_at(s, l, gi):
                    b = bank[2 + gi]
                    n = 1 << l
                    if l == 0:
                        pe.wait_ge(diag_filled.sem, diag_filled.after(s))
                        for u in range(2):
                            last = nc.tensor.transpose(b[:, u * P:(u + 1) * P], AM[:, 2 * gi + u, 0, :], ident[:])
                        last.then_inc(at_ready.sem, 1)
                        return
                    if l == 1:
                        pe.wait_ge(masked.sem, masked.step(s, gi + 1))
                    else:
                        pe.wait_ge(tx_copied.sem, tx_copied.step(s, 2 * (l - 2) + gi + 1))
                    t1, _ = halves(grp(Tm, gi), n)
                    for u in range(2):
                        last = nc.tensor.matmul(b[:, u * 64:(u + 1) * 64].rearrange("p (m n) -> p m n", n=n),
                                                AM[:, 2 * gi + u, 0, :], t1[:, u], start=True, stop=True)
                    last.then_inc(at_ready.sem, 1)

                def multiply_tx(s, l, gi):
                    b = bank[2 + gi]
                    n = 1 << l
                    pe.wait_ge(masked.sem, masked.step(s, 2 * l + gi + 1))
                    if l == 1:
                        pe.wait_ge(x0_ready.sem, x0_ready.after(s))
                    _, x2 = halves(grp(Xm, gi), n)
                    l1, _ = halves(grp(Lv[:, l - 1], gi), n)
                    for u in range(2):
                        if l < LEVELS - 1:
                            nc.tensor.matmul(b[:, 128 + u * 64:128 + (u + 1) * 64].rearrange("p (m n) -> p m n", n=n),
                                             Xm[:, 2 * gi + u, :], l1[:, u], start=True, stop=True)
                        last = nc.tensor.matmul(b[:, 256 + u * 64:256 + (u + 1) * 64].rearrange("p (m n) -> p m n", n=n),
                                                Lv[:, l - 1, 2 * gi + u, :], x2[:, u], start=True, stop=True)
                    last.then_inc(tx_ready.sem, 1)

                for i in range(6):
                    project(-1, i)
                project_gate(-1)
                with pe.Fori(0, HP) as q:
                    with pe.Fori(0, NC) as c:
                        s = q * NC + c
                        back_1(s)
                        pe.wait_ge(vecF_in.sem, vecF_in.after(s))
                        pe.wait_ge(convolved.sem, convolved.before(s))
                        nc.tensor.matmul(bank[0][:], ident16[:], causal16[:], start=True, stop=False, skip_group_check=True)
                        for u in range(U):
                            last = nc.tensor.matmul(bank[0][:, u * P:(u + 1) * P], vecF[:, 1, u:u + 1].broadcast_to([P, P]),
                                                    cumsum_mask[:], start=False, stop=True, skip_group_check=True)
                        last.then_inc(decay_ready.sem, 1)
                        back_2(s)
                        pe.wait_ge(qk_silu.sem, qk_silu.after(s))
                        for u in range(U):
                            last = nc.tensor.matmul(bank[2 + u // 2][:, (u % 2) * 2 * P:(u % 2 + 1) * 2 * P]
                                                    .rearrange("p (a n) -> p a n", a=2), QK[:, 0, u, :],
                                                    QK[:, :, u, :], start=True, stop=True)
                            if u % 2:
                                last.then_inc(kq_ready.sem, 1)
                        pe.wait_ge(out_added.sem, out_added.before(s))
                        for u in range(U):
                            last = nc.tensor.transpose(bank[7][:, u * P:(u + 1) * P], QK[:, 0, u, :], ident[:])
                        last.then_inc(k_turned.sem, 1)
                        pe.wait_ge(v_silu.sem, v_silu.after(s))
                        pe.wait_ge(gate_kept.sem, gate_kept.before(s))
                        for u in range(U):
                            last = nc.tensor.transpose(bank[4][:, u * P:(u + 1) * P], Vt[:, u, :], ident[:])
                        last.then_inc(v_turned.sem, 1)
                        pe.wait_ge(qk_squared.sem, qk_squared.after(s))
                        for a in range(2):
                            for u in range(U):
                                last = nc.tensor.matmul(bank[1][:, a * U + u:a * U + u + 1], QKsq[:, a, u, :], ones[:, 0:1],
                                                        start=True, stop=True)
                        last.then_inc(ss_ready.sem, 1)
                        back_3(s)
                        for l in range(LEVELS):
                            for gi in range(2):
                                multiply_at(s, l, gi)
                            if l >= 1:
                                project(s, l - 1)
                                for gi in range(2):
                                    multiply_tx(s, l, gi)
                            if l == 3:
                                turn_z(s)
                            if l == 5:
                                output(s)
                        project_gate(s)
                s = SLOTS
                back_1(s)
                back_2(s)
                back_3(s)
                turn_z(s, loop=False)
                output(s)
        tools.clear()


def int_ffn(nc, tools, bank, XT, Yt, A_gate, A_gs, A_up, A_us, A_down, A_dsc):
    IT = FI // P
    NB = NC * B // 4
    with ExitStack() as ctx:
        def sb(name, shape, dt=F32):
            return tools.sb("ff_" + name, shape, dt, ctx)

        def sem(name):
            return tools.sem("ff_" + name)

        Wi = sb("Wi", [P, 3, KD * FI], I32)
        Wf = sb("Wf", [P, 3, KD * FI])
        gs = sb("gs", [P, IT])
        us = sb("us", [P, IT])
        dsc = sb("dsc", [P, D])
        sg = sb("sg", [P, 2, 4 * P])
        hT = sb("hT", [P, IT, 4 * P])
        w_loaded = [sem(f"w{i}_loaded") for i in range(3)]
        scales_loaded = sem("scales_loaded")
        w_made = sem("w_made")
        gu_ready = PerSlot(sem("gu_ready"), IT)
        g_silu = PerSlot(sem("g_silu"), IT)
        h_ready = PerSlot(sem("h_ready"), IT)
        y_ready = PerSlot(sem("y_ready"), 4)
        y_scaled = PerSlot(sem("y_scaled"), 4)
        Wg = Wf[:, 0, :].rearrange("p (k i) -> p k i", k=KD)
        Wu = Wf[:, 1, :].rearrange("p (k i) -> p k i", k=KD)
        Wd = Wf[:, 2, :].rearrange("p (t d) -> p t d", t=IT)
        Yv = Yt[:].rearrange("p c b d -> p (c b) d")

        with nc.Block() as block:
            @block.sync
            def _(sp):
                for x in (g_silu, h_ready, y_ready, y_scaled, gu_ready):
                    sp.sem_inc(x.sem, x.n)
        with nc.Block() as block:
            @block.sync
            def _(sp):
                sp.dma_start(Wi[:, 0, :].rearrange("p (k i) -> p k i", k=KD), A_gate.rearrange("(k p) i -> p k i", p=P)).then_inc(w_loaded[0], 16)
                sp.dma_start(Wi[:, 1, :].rearrange("p (k i) -> p k i", k=KD), A_up.rearrange("(k p) i -> p k i", p=P)).then_inc(w_loaded[1], 16)
                sp.dma_start(Wi[:, 2, :].rearrange("p (t d) -> p t d", t=IT), A_down.rearrange("(t p) d -> p t d", p=P)).then_inc(w_loaded[2], 16)
                sp.dma_start(gs[:], A_gs).then_inc(scales_loaded, 16)
                sp.dma_start(us[:], A_us).then_inc(scales_loaded, 16)
                sp.dma_start(dsc[:], A_dsc.partition_broadcast(P)).then_inc(scales_loaded, 16)

            @block.tensor
            def _(pe):
                pe.wait_ge(w_made, 2)
                with pe.Fori(0, NB) as n:
                    for i in range(IT):
                        pe.wait_ge(g_silu.sem, g_silu.step(n, i - 1))
                        pe.wait_ge(h_ready.sem, h_ready.step(n, i - 1))
                        for w, bk in ((Wg, bank[i % 2]), (Wu, bank[2 + i % 2])):
                            for k in range(KD):
                                last = nc.tensor.matmul(bk[:], w[:, k, i * P:(i + 1) * P], XT[:, k, ds(n * 4 * P, 4 * P)],
                                                        start=(k == 0), stop=(k == KD - 1))
                        last.then_inc(gu_ready.sem, 1)
                    pe.wait_ge(h_ready.sem, h_ready.after(n))
                    pe.wait_ge(w_made, 3)
                    for j in range(4):
                        pe.wait_ge(y_scaled.sem, y_scaled.step(n, j - 1))
                        for i in range(IT):
                            last = nc.tensor.matmul(bank[4 + j % 2][:, 0:D], hT[:, i, j * P:(j + 1) * P], Wd[:, i, :],
                                                    start=(i == 0), stop=(i == IT - 1))
                        last.then_inc(y_ready.sem, 1)

            @block.scalar
            def _(act):
                act.wait_ge(scales_loaded, 48)
                with act.Fori(0, NB) as n:
                    for i in range(IT):
                        act.wait_ge(gu_ready.sem, gu_ready.step(n, i + 1))
                        act.wait_ge(h_ready.sem, h_ready.step(n, i - 1))
                        nc.scalar.activation(sg[:, i % 2, :], bank[i % 2][:], ACT.Silu, scale=gs[:, i:i + 1]).then_inc(g_silu.sem, 1)

            @block.vector
            def _(dve):
                for i in range(3):
                    dve.wait_ge(w_loaded[i], 16)
                    nc.vector.tensor_scalar(Wf[:, i, :], Wi[:, i, :], -128.0, None, ALU.add).then_inc(w_made, 1)
                dve.wait_ge(scales_loaded, 48)
                with dve.Fori(0, NB) as n:
                    for i in range(IT):
                        dve.wait_ge(g_silu.sem, g_silu.step(n, i + 1))
                        if i == 0:
                            dve.wait_ge(y_ready.sem, y_ready.before(n))
                        nc.vector.scalar_tensor_tensor(hT[:, i, :], bank[2 + i % 2][:], us[:, i:i + 1], sg[:, i % 2, :],
                                                       ALU.mult, ALU.mult).then_inc(h_ready.sem, 1)
                    for j in range(4):
                        dve.wait_ge(y_ready.sem, y_ready.step(n, j + 1))
                        nc.vector.tensor_tensor(Yv[:, ds(n * 4 + j, 1), :].rearrange("p a d -> p (a d)"), bank[4 + j % 2][:, 0:D],
                                                dsc[:], ALU.mult).then_inc(y_scaled.sem, 1)


def attention(nc, tools, PS, bank, ident, ident16, causal16, XT, Yt, A_wq, A_bq, A_cs, A_wv, A_bv, A_wd, A_bd):
    NB = NC * B // 4
    KB = 4
    with ExitStack() as ctx:
        def sb(name, shape, dt=F32):
            return tools.sb("at_" + name, shape, dt, ctx)

        def sem(name):
            return tools.sem("at_" + name)

        QF = sb("QF", [P, 2, KD, B, T])
        V = sb("V", [P, NC, B, D])
        Wdn = sb("Wdn", [P, KD, D])
        bd = sb("bd", [P, D])
        w_loaded = sem("w_loaded")
        with ExitStack() as ctx2:
            Wq = tools.sb("at_Wq", [P, KD, 4, D], F32, ctx2)
            Wv = tools.sb("at_Wv", [P, KD, D], F32, ctx2)
            bq = tools.sb("at_bq", [P, 4, KD], F32, ctx2)
            bv = tools.sb("at_bv", [P, D], F32, ctx2)
            cs = tools.sb("at_cs", [P, 2, T], F32, ctx2)
            qa = tools.sb("at_qa", [P, 2, 2, 4 * P], F32, ctx2)
            qm = tools.sb("at_qm", [P, 2, 2, 4 * P], F32, ctx2)
            qk_ready = PerSlot(sem("qk_ready"), 4)
            biased = PerSlot(sem("biased"), 4)
            rotated = PerSlot(sem("rotated"), 8)
            summed = PerSlot(sem("summed"), 4)
            v_ready = sem("v_ready")
            v_added = sem("v_added")
            with nc.Block() as block:
                @block.sync
                def _(sp):
                    for x in (qk_ready, biased, rotated, summed):
                        sp.sem_inc(x.sem, x.n)
            with nc.Block() as block:
                @block.sync
                def _(sp):
                    for k in range(KD):
                        sp.dma_start(Wq[:, k, :, :], A_wq[:, k * P:(k + 1) * P, :].rearrange("a p n -> p a n")).then_inc(w_loaded, 16)
                        sp.dma_start(Wv[:, k, :], A_wv[k * P:(k + 1) * P, :]).then_inc(w_loaded, 16)
                        sp.dma_start(Wdn[:, k, :], A_wd[k * P:(k + 1) * P, :]).then_inc(w_loaded, 16)
                    sp.dma_start(bq[:], A_bq).then_inc(w_loaded, 16)
                    sp.dma_start(cs[:], A_cs.rearrange("a p t -> p a t")).then_inc(w_loaded, 16)
                    sp.dma_start(bv[:], A_bv.partition_broadcast(P)).then_inc(w_loaded, 16)
                    sp.dma_start(bd[:], A_bd.partition_broadcast(P)).then_inc(w_loaded, 16)

                LOADED = 16 * (3 * KD + 4)

                @block.tensor
                def _(pe):
                    pe.wait_ge(w_loaded, LOADED)
                    with pe.Fori(0, NB) as n:
                        for i in range(4):
                            a, m = i // 2, i % 2
                            pe.wait_ge(biased.sem, biased.step(n, i - 1))
                            for part in range(2):
                                for k in range(KD):
                                    last = nc.tensor.matmul(bank[2 * (i % 2) + part][:], Wq[:, k, 2 * a + part, m * P:(m + 1) * P],
                                                            XT[:, k, ds(n * 4 * P, 4 * P)], start=(k == 0), stop=(k == KD - 1))
                            last.then_inc(qk_ready.sem, 1)
                    for t in range(NC * B):
                        if t >= 2:
                            pe.wait_ge(v_added, t - 1)
                        for k in range(KD):
                            last = nc.tensor.matmul(bank[4 + t % 2][:, 0:D], XT[:, k, t * P:(t + 1) * P], Wv[:, k, :],
                                                    start=(k == 0), stop=(k == KD - 1))
                        last.then_inc(v_ready, 1)

                @block.scalar
                def _(act):
                    act.wait_ge(w_loaded, LOADED)
                    with act.Fori(0, NB) as n:
                        for i in range(4):
                            a, m = i // 2, i % 2
                            act.wait_ge(qk_ready.sem, qk_ready.step(n, i + 1))
                            act.wait_ge(rotated.sem, rotated.step(n, 2 * (i - 1)))
                            for part in range(2):
                                last = nc.scalar.activation(qa[:, i % 2, part, :], bank[2 * (i % 2) + part][:], ACT.Identity,
                                                            bias=bq[:, 2 * a + part, m:m + 1])
                            last.then_inc(biased.sem, 1)

                @block.vector
                def _(dve):
                    dve.wait_ge(w_loaded, LOADED)
                    with dve.Fori(0, NB) as n:
                        for i in range(4):
                            a, m = i // 2, i % 2
                            dve.wait_ge(biased.sem, biased.step(n, i + 1))
                            for part in range(2):
                                for c in range(2):
                                    tab = cs[:, part, ds((n * 2 + c) * P, P)].rearrange("p (a n) -> p a n", a=1).broadcast_to([P, B, P])
                                    last = nc.vector.tensor_tensor(
                                        qm[:, i % 2, part, c * B * P:(c + 1) * B * P].rearrange("p (b n) -> p b n", b=B),
                                        qa[:, i % 2, part, c * B * P:(c + 1) * B * P].rearrange("p (b n) -> p b n", b=B),
                                        tab, ALU.mult)
                                last.then_inc(rotated.sem, 1)
                            dve.wait_ge(rotated.sem, rotated.step(n, 2 * (i + 1)))
                            for c in range(2):
                                last = nc.vector.tensor_tensor(
                                    QF[:, a, m, :, ds((n * 2 + c) * P, P)],
                                    qm[:, i % 2, 0, c * B * P:(c + 1) * B * P].rearrange("p (b n) -> p b n", b=B),
                                    qm[:, i % 2, 1, c * B * P:(c + 1) * B * P].rearrange("p (b n) -> p b n", b=B), ALU.add)
                            last.then_inc(summed.sem, 1)
                    for t in range(NC * B):
                        dve.wait_ge(v_ready, t + 1)
                        nc.vector.tensor_tensor(V[:, t // B, t % B, :], bank[4 + t % 2][:, 0:D], bv[:], ALU.add).then_inc(v_added, 1)

        tiles = [(hh, b, i) for hh in range(2) for b in range(B) for i in range(NC)]
        NT = len(tiles)
        qh = sb("qh", [AD, 2, B, T])
        kh = sb("kh", [AD, 2, B, T])
        mx = sb("mx", [P, 2, 1])
        nb = sb("nb", [P, 2, 1])
        rsum = sb("rsum", [P, 2, 1])
        rinv = sb("rinv", [P, 2, 1])
        Pm = sb("Pm", [P, 2, T])
        PT = sb("PT", [P, 2, NC, P])
        AO = sb("AO", [P, NC, B, D])
        groups = [(t, g) for t, (_, _, i) in enumerate(tiles) for g in range(i // KB + 1)]
        gidx = {tg: n for n, tg in enumerate(groups)}
        NG = len(groups)
        heads_loaded = [sem(f"heads_loaded{i}") for i in range(2)]
        scored = PerSlot(sem("scored"), NT)
        maxed = PerSlot(sem("maxed"), NT)
        biased2 = PerSlot(sem("biased2"), NT)
        exped = PerSlot(sem("exped"), NT)
        turned = PerSlot(sem("turned"), NG)
        moved = [PerSlot(sem(f"moved{e}"), 0) for e in range(2)]
        pv_ready = PerSlot(sem("pv_ready"), NT)
        inverted = PerSlot(sem("inverted"), NT)
        scaled = PerSlot(sem("scaled"), NT)
        moved[0].n = (NG + 1) // 2
        moved[1].n = NG // 2
        assert NG % 2 == 0
        with nc.Block() as block:
            @block.sync
            def _(sp):
                for x in (scored, maxed, biased2, exped, turned, moved[0], moved[1], pv_ready, inverted, scaled):
                    sp.sem_inc(x.sem, x.n)
        with nc.Block() as block:
            @block.sync
            def _(sp):
                for h in range(AH):
                    if h >= 2:
                        sp.wait_ge(scored.sem, scored.step(h // 2 - 1, (h % 2 + 1) * B * NC))
                    r = (h % 8) * AD
                    sp.dma_start(qh[:, h % 2, :, :], QF[r:r + AD, 0, h // 8, :, :]).then_inc(heads_loaded[h % 2], 16)
                    sp.dma_start(kh[:, h % 2, :, :], QF[r:r + AD, 1, h // 8, :, :]).then_inc(heads_loaded[h % 2], 16)

            @block.tensor
            def _(pe):
                def score(g, t):
                    hh, b, i = tiles[t]
                    if b == 0 and i == 0:
                        pe.wait_ge(heads_loaded[hh], (g + 1) * 32)
                    pe.wait_ge(exped.sem, exped.step(g, t - 1))
                    for g4 in range(i // KB + 1):
                        cols = min(KB, i + 1 - g4 * KB) * P
                        diag = g4 == i // KB
                        last = nc.tensor.matmul(PS[:, 2 * (t % 2) + g4, 0:cols], qh[:, hh, b, i * P:(i + 1) * P],
                                                kh[:, hh, b, g4 * KB * P:g4 * KB * P + cols], start=True, stop=not diag,
                                                skip_group_check=True)
                        if diag:
                            last = nc.tensor.matmul(PS[:, 2 * (t % 2) + g4, cols - P:cols], ident16[:], causal16[:],
                                                    start=False, stop=True, skip_group_check=True)
                    last.then_inc(scored.sem, 1)

                def turn(g, t):
                    i = tiles[t][2]
                    pe.wait_ge(exped.sem, exped.step(g, t + 1))
                    for g4 in range(i // KB + 1):
                        n = gidx[(t, g4)]
                        pe.wait_ge(moved[n % 2].sem, moved[n % 2].step(g, n // 2))
                        for kb in range(g4 * KB, min(i + 1, (g4 + 1) * KB)):
                            last = nc.tensor.transpose(bank[4 + n % 2][:, (kb % KB) * P:(kb % KB + 1) * P],
                                                       Pm[:, t % 2, kb * P:(kb + 1) * P], ident[:])
                        last.then_inc(turned.sem, 1)

                def pv(g, t):
                    hh, b, i = tiles[t]
                    for g4 in range(i // KB + 1):
                        n = gidx[(t, g4)]
                        pe.wait_ge(moved[n % 2].sem, moved[n % 2].step(g, n // 2 + 1))
                    pe.wait_ge(scaled.sem, scaled.step(g, t - 1))
                    for kb in range(i + 1):
                        last = nc.tensor.matmul(bank[6 + t % 2][:, 0:AD], PT[:, t % 2, kb, :],
                                                V[:, kb, b, ds((g * 2 + hh) * AD, AD)], start=(kb == 0), stop=(kb == i))
                    last.then_inc(pv_ready.sem, 1)

                with pe.Fori(0, AH // 2) as g:
                    score(g, 0)
                    for t in range(NT):
                        if t + 1 < NT:
                            score(g, t + 1)
                        turn(g, t)
                        if t >= 1:
                            pv(g, t - 1)
                    pv(g, NT - 1)

            def move(eng, g, t, e):
                i = tiles[t][2]
                for g4 in range(i // KB + 1):
                    n = gidx[(t, g4)]
                    if n % 2 != e:
                        continue
                    eng.wait_ge(turned.sem, turned.step(g, n + 1))
                    eng.wait_ge(pv_ready.sem, pv_ready.step(g, t - 1))
                    blocks = min(KB, i + 1 - g4 * KB)
                    dst = PT[:, t % 2, g4 * KB:g4 * KB + blocks, :]
                    src = bank[4 + n % 2][:, 0:blocks * P].rearrange("p (k n) -> p k n", n=P)
                    if e == 0:
                        nc.scalar.activation(dst, src, ACT.Copy).then_inc(moved[0].sem, 1)
                    else:
                        nc.vector.tensor_copy(dst, src).then_inc(moved[1].sem, 1)

            @block.scalar
            def _(act):
                def exp(g, t):
                    width = (tiles[t][2] + 1) * P
                    act.wait_ge(biased2.sem, biased2.step(g, t + 1))
                    act.wait_ge(turned.sem, turned.step(g, gidx[(t - 2, 0)] + tiles[t - 2][2] // KB + 1) if t >= 2
                                else turned.before(g))
                    act.wait_ge(inverted.sem, inverted.step(g, t - 1))
                    nc.scalar.activation(Pm[:, t % 2, 0:width], PS[:, 2 * (t % 2):2 * (t % 2) + 2, :].rearrange("p a n -> p (a n)")[:, 0:width],
                                         ACT.Exp, bias=nb[:, t % 2, :], scale=AD ** -0.5,
                                         accum_out=rsum[:, t % 2, :]).then_inc(exped.sem, 1)

                with act.Fori(0, AH // 2) as g:
                    exp(g, 0)
                    for t in range(NT):
                        if t + 1 < NT:
                            exp(g, t + 1)
                        move(act, g, t, 0)

            @block.vector
            def _(dve):
                def row_max(g, t):
                    width = (tiles[t][2] + 1) * P
                    dve.wait_ge(scored.sem, scored.step(g, t + 1))
                    dve.wait_ge(exped.sem, exped.step(g, t - 1))
                    nc.vector.reduce_max(mx[:, t % 2, :], PS[:, 2 * (t % 2):2 * (t % 2) + 2, :].rearrange("p a n -> p (a n)")[:, 0:width],
                                         axis=AX.X).then_inc(maxed.sem, 1)
                    dve.wait_ge(maxed.sem, maxed.step(g, t + 1))
                    nc.vector.tensor_scalar(nb[:, t % 2, :], mx[:, t % 2, :], -(AD ** -0.5), None, ALU.mult).then_inc(biased2.sem, 1)

                def scale(g, t):
                    hh, b, i = tiles[t]
                    dve.wait_ge(exped.sem, exped.step(g, t + 1))
                    nc.vector.reciprocal(rinv[:, t % 2, :], rsum[:, t % 2, :]).then_inc(inverted.sem, 1)
                    dve.wait_ge(inverted.sem, inverted.step(g, t + 1))
                    dve.wait_ge(pv_ready.sem, pv_ready.step(g, t + 1))
                    nc.vector.tensor_scalar(AO[:, i, b, ds((g * 2 + hh) * AD, AD)], bank[6 + t % 2][:, 0:AD], rinv[:, t % 2, :],
                                            None, ALU.mult).then_inc(scaled.sem, 1)

                with dve.Fori(0, AH // 2) as g:
                    row_max(g, 0)
                    for t in range(NT):
                        if t + 1 < NT:
                            row_max(g, t + 1)
                        move(dve, g, t, 1)
                        if t >= 1:
                            scale(g, t - 1)
                    scale(g, NT - 1)

        AOT = sb("AOT", [P, 2, KD, P])
        ao_turned = sem("ao_turned")
        ao_copied = sem("ao_copied")
        d_ready = sem("d_ready")
        d_added = sem("d_added")
        with nc.Block() as block:
            @block.tensor
            def _(pe):
                def turn(t):
                    if t >= 2:
                        pe.wait_ge(ao_copied, t - 1)
                    for k in range(KD):
                        last = nc.tensor.transpose(bank[t % 2][:, k * P:(k + 1) * P], AO[:, t // B, t % B, k * P:(k + 1) * P], ident[:])
                    last.then_inc(ao_turned, 1)

                turn(0)
                for t in range(NC * B):
                    if t + 1 < NC * B:
                        turn(t + 1)
                    pe.wait_ge(ao_copied, t + 1)
                    if t >= 2:
                        pe.wait_ge(d_added, t - 1)
                    for k in range(KD):
                        last = nc.tensor.matmul(bank[2 + t % 2][:, 0:D], AOT[:, t % 2, k, :], Wdn[:, k, :], start=(k == 0), stop=(k == KD - 1))
                    last.then_inc(d_ready, 1)

            @block.scalar
            def _(act):
                for t in range(NC * B):
                    act.wait_ge(ao_turned, t + 1)
                    if t >= 2:
                        act.wait_ge(d_ready, t - 1)
                    nc.scalar.activation(AOT[:, t % 2, :, :], bank[t % 2][:, 0:D].rearrange("p (k n) -> p k n", k=KD), ACT.Copy).then_inc(ao_copied, 1)

            @block.vector
            def _(dve):
                for t in range(NC * B):
                    dve.wait_ge(d_ready, t + 1)
                    nc.vector.tensor_tensor(Yt[:, t // B, t % B, :], bank[2 + t % 2][:, 0:D], bd[:], ALU.add).then_inc(d_added, 1)


def experts(nc, tools, bank, ident, XT, Yt, A_wr, A_tri, A_w1, A_w3, A_w2):
    NB = NC * B // 4
    NE = NSH + E
    NTL = NC * B
    with ExitStack() as ctx:
        def sb(name, shape, dt=F32):
            return tools.sb("ex_" + name, shape, dt, ctx)

        def sem(name):
            return tools.sem("ex_" + name)

        W1 = sb("W1", [P, KD, NE, EH])
        W3 = sb("W3", [P, KD, NE, EH])
        W2 = sb("W2", [P, NE, D])
        w_loaded = sem("w_loaded")
        cw = sb("cw", [P, NTL, E])
        with ExitStack() as ctx2:
            Wr = tools.sb("ex_Wr", [P, KD, E], F32, ctx2)
            tri = tools.sb("ex_tri", [P, E, E], F32, ctx2)
            lgT = tools.sb("ex_lgT", [E, NTL * P], F32, ctx2)
            mx = tools.sb("ex_mx", [P, NTL, 1], F32, ctx2)
            pr = tools.sb("ex_pr", [P, NTL, E], F32, ctx2)
            den = tools.sb("ex_den", [P, NTL, 1], F32, ctx2)
            above = tools.sb("ex_above", [P, NTL, E, E], F32, ctx2)
            equal = tools.sb("ex_equal", [P, NTL, E, E], F32, ctx2)
            rank = tools.sb("ex_rank", [P, NTL, E, 1], F32, ctx2)
            router_loaded = sem("router_loaded")
            logits = sem("logits")
            logits_copied = sem("logits_copied")
            logits_turned = sem("logits_turned")
            exped = sem("exped")
            steps = sem("router_steps")
            with nc.Block() as block:
                @block.sync
                def _(sp):
                    sp.dma_start(Wr[:], A_wr.rearrange("(k p) e -> p k e", p=P)).then_inc(router_loaded, 16)
                    sp.dma_start(tri[:].rearrange("p e f -> p (e f)"), A_tri.partition_broadcast(P)).then_inc(router_loaded, 16)
                    for k in range(KD):
                        sp.dma_start(W1[:, k, :, :], A_w1[:, k * P:(k + 1) * P, :].rearrange("e p h -> p e h")).then_inc(w_loaded, 16)
                        sp.dma_start(W3[:, k, :, :], A_w3[:, k * P:(k + 1) * P, :].rearrange("e p h -> p e h")).then_inc(w_loaded, 16)
                    sp.dma_start(W2[:], A_w2.rearrange("e p d -> p e d")).then_inc(w_loaded, 16)

                @block.tensor
                def _(pe):
                    pe.wait_ge(router_loaded, 32)
                    for n in range(NB):
                        for k in range(KD):
                            last = nc.tensor.matmul(bank[n][0:E, :], Wr[:, k, :], XT[:, k, n * 4 * P:(n + 1) * 4 * P],
                                                    start=(k == 0), stop=(k == KD - 1))
                        last.then_inc(logits, 1)
                    for t in range(NTL):
                        pe.wait_ge(logits_copied, t // 4 + 1)
                        last = nc.tensor.transpose(bank[4][:, t * E:(t + 1) * E], lgT[:, t * P:(t + 1) * P], ident[0:E, 0:E])
                    last.then_inc(logits_turned, 1)

                lg = bank[4][:, 0:NTL * E].rearrange("p (t e) -> p t e", e=E)

                @block.scalar
                def _(act):
                    for n in range(NB):
                        act.wait_ge(logits, n + 1)
                        nc.scalar.activation(lgT[:, n * 4 * P:(n + 1) * 4 * P], bank[n][0:E, :], ACT.Copy).then_inc(logits_copied, 1)
                    act.wait_ge(steps, 2)
                    nc.scalar.activation(pr[:], pr[:], ACT.Exp).then_inc(exped, 1)

                @block.vector
                def _(dve):
                    def step(n, ins):
                        ins.then_inc(steps, 1)
                        dve.wait_ge(steps, n)

                    dve.wait_ge(logits_turned, 1)
                    dve.wait_ge(router_loaded, 32)
                    over_e = [P, NTL, E]
                    pairs = [P, NTL * E, E]
                    flat = "p t e f -> p (t e) f"
                    step(1, nc.vector.tensor_reduce(mx[:, :, 0], lg, AX.X, ALU.max))
                    step(2, nc.vector.tensor_tensor(pr[:], lg, mx[:].broadcast_to(over_e), ALU.subtract))
                    dve.wait_ge(exped, 1)
                    step(3, nc.vector.tensor_reduce(den[:, :, 0], pr[:], AX.X, ALU.add))
                    step(4, nc.vector.reciprocal(den[:], den[:]))
                    step(5, nc.vector.tensor_tensor(pr[:], pr[:], den[:].broadcast_to(over_e), ALU.mult))
                    for t in range(NTL):
                        pf = pr[:, t:t + 1, :].broadcast_to([P, E, E])
                        pe_ = pr[:, t, :].rearrange("p (e a) -> p e a", a=1).broadcast_to([P, E, E])
                        nc.vector.tensor_tensor(above[:, t, :, :], pf, pe_, ALU.is_gt)
                        last = nc.vector.tensor_tensor(equal[:, t, :, :], pf, pe_, ALU.is_equal)
                    step(6, last)
                    step(7, nc.vector.tensor_tensor(equal[:].rearrange("p t e f -> p t (e f)"), equal[:].rearrange("p t e f -> p t (e f)"),
                                                    tri[:].rearrange("p (a e) f -> p a (e f)", a=1).broadcast_to([P, NTL, E * E]), ALU.mult))
                    step(8, nc.vector.tensor_tensor(above[:], above[:], equal[:], ALU.add))
                    step(9, nc.vector.tensor_reduce(rank[:, :, :, 0], above[:], AX.X, ALU.add))
                    step(10, nc.vector.tensor_scalar(rank[:], rank[:], TOPK - 0.5, TOPK / (TOPK + 1.0), ALU.is_lt, ALU.mult))
                    step(11, nc.vector.tensor_tensor(cw[:], pr[:], rank[:, :, :, 0], ALU.mult))
                    step(12, nc.vector.tensor_reduce(den[:, :, 0], cw[:], AX.X, ALU.add))
                    step(13, nc.vector.tensor_scalar(den[:], den[:], (TOPK + 1.0) / TOPK, None, ALU.mult))
                    step(14, nc.vector.reciprocal(den[:], den[:]))
                    step(15, nc.vector.tensor_tensor(cw[:], cw[:], den[:].broadcast_to(over_e), ALU.mult))

        sg = sb("sg", [P, 2, 4 * P])
        gT = sb("gT", [P, 2, 4 * P])
        h_ready = PerSlot(sem("h_ready"), NE)
        silu = PerSlot(sem("silu"), NE)
        g_ready = PerSlot(sem("g_ready"), NE)
        y_ready = PerSlot(sem("y_ready"), NE)
        y_added = PerSlot(sem("y_added"), NE)
        Yv = Yt[:].rearrange("p c b d -> p (c b) d")
        out_banks = lambda e: (4, 5) if e < NSH or e % 2 else (6, 7)
        with nc.Block() as block:
            @block.sync
            def _(sp):
                for x in (h_ready, silu, g_ready, y_ready, y_added):
                    sp.sem_inc(x.sem, x.n)
        with nc.Block() as block:
            @block.tensor
            def _(pe):
                def up(n, e):
                    pe.wait_ge(silu.sem, silu.step(n, e - 1))
                    pe.wait_ge(g_ready.sem, g_ready.step(n, e - 1))
                    for w, bk in ((W1, bank[e % 2]), (W3, bank[2 + e % 2])):
                        for k in range(KD):
                            last = nc.tensor.matmul(bk[:], w[:, k, e, :], XT[:, k, ds(n * 4 * P, 4 * P)], start=(k == 0), stop=(k == KD - 1))
                    last.then_inc(h_ready.sem, 1)

                def down(n, e):
                    pe.wait_ge(g_ready.sem, g_ready.step(n, e + 1))
                    shared = e < NSH
                    pe.wait_ge(y_added.sem, y_added.before(n) if e <= NSH else y_added.step(n, e - 1))
                    for j in range(4):
                        bk = bank[out_banks(e)[j // 2]]
                        last = nc.tensor.matmul(bk[:, (j % 2) * D:(j % 2 + 1) * D], gT[:, e % 2, j * P:(j + 1) * P], W2[:, e, :],
                                                start=(j % 2 == 0) if not shared else (e == 0 and j % 2 == 0),
                                                stop=not shared or e == NSH - 1, skip_group_check=True)
                    last.then_inc(y_ready.sem, 1)

                pe.wait_ge(w_loaded, 16 * (2 * KD + 1))
                with pe.Fori(0, NB) as n:
                    up(n, 0)
                    for e in range(NE):
                        if e + 1 < NE:
                            up(n, e + 1)
                        down(n, e)

            @block.scalar
            def _(act):
                with act.Fori(0, NB) as n:
                    for e in range(NE):
                        act.wait_ge(h_ready.sem, h_ready.step(n, e + 1))
                        act.wait_ge(g_ready.sem, g_ready.step(n, e - 1))
                        nc.scalar.activation(sg[:, e % 2, :], bank[e % 2][:], ACT.Silu).then_inc(silu.sem, 1)

            @block.vector
            def _(dve):
                def gated(n, e):
                    dve.wait_ge(silu.sem, silu.step(n, e + 1))
                    dve.wait_ge(y_ready.sem, y_ready.step(n, e - 1))
                    nc.vector.tensor_tensor(gT[:, e % 2, :], bank[2 + e % 2][:], sg[:, e % 2, :], ALU.mult).then_inc(g_ready.sem, 1)

                def add(n, e):
                    dve.wait_ge(y_ready.sem, y_ready.step(n, e + 1))
                    if e < NSH - 1:
                        dve.sem_inc(y_added.sem, 1)
                        return
                    dve.wait_ge(y_added.sem, y_added.step(n, e))
                    for j in range(4):
                        src = bank[out_banks(e)[j // 2]][:, (j % 2) * D:(j % 2 + 1) * D]
                        y = Yv[:, ds(n * 4 + j, 1), :].rearrange("p a d -> p (a d)")
                        if e == NSH - 1:
                            last = nc.vector.tensor_scalar(y, src, 1.0 / (TOPK + 1), None, ALU.mult)
                        else:
                            last = nc.vector.scalar_tensor_tensor(y, src, cw[:, ds(n * 4 + j, 1), e - NSH], y, ALU.mult, ALU.add)
                    last.then_inc(y_added.sem, 1)

                with dve.Fori(0, NB) as n:
                    gated(n, 0)
                    for e in range(NE):
                        if e + 1 < NE:
                            gated(n, e + 1)
                        add(n, e)


def two_layers(nc, A, out, stop_after=4):
    with ExitStack() as ctx:
        tools = Tools(nc, ctx)
        PS = ctx.enter_context(nc.psum_tensor("PS", [P, 8, 512], F32))
        bank = [PS[:, i, :] for i in range(8)]
        X = tools.sb("X", [P, NC, B, D])
        Yt = tools.sb("Yt", [P, NC, B, D])
        ident = tools.sb("ident", [P, P])
        cumsum_mask = tools.sb("cumsum_mask", [P, P])
        level0 = tools.sb("level0", [P, P])
        level0_t = tools.sb("level0_t", [P, P])
        level_masks = tools.sb("level_masks", [P, LEVELS - 1, 64])
        causal = tools.sb("causal", [P, U * P])
        causal16 = tools.sb("causal16", [P, U * P], BF16)
        diag16 = tools.sb("diag16", [P, P], BF16)
        ident16 = tools.sb("ident16", [P, P], BF16)
        ones = tools.sb("ones", [P, P])
        half = tools.sb("half", [P, 1])
        consts_loaded = tools.sem("consts_loaded")
        consts_made = tools.sem("consts_made")

        with nc.Block() as block:
            @block.sync
            def _(sp):
                at = 0
                for t, n in ((ident, P), (cumsum_mask, P), (level0, P), (level0_t, P), (level_masks, 64 * (LEVELS - 1)), (causal, U * P)):
                    dst = t[:].rearrange("p a n -> p (a n)") if t is level_masks else t[:]
                    sp.dma_start(dst, A["masks"][:, at:at + n]).then_inc(consts_loaded, 16)
                    at += n

            @block.vector
            def _(dve):
                nc.vector.memset(ones[:], 1.0)
                nc.vector.memset(half[:], -0.5)
                dve.wait_ge(consts_loaded, 16 * 6)
                nc.vector.tensor_copy(ident16[:], ident[:])
                nc.vector.tensor_copy(causal16[:], causal[:])

            @block.gpsimd
            def _(pool):
                pool.wait_ge(consts_loaded, 16 * 6)
                nc.gpsimd.memset(diag16[:], 0.0).then_inc(consts_made, 1)
                pool.wait_ge(consts_made, 1)
                nc.gpsimd.affine_select(out=diag16[:], in_=diag16[:], compare_op=ALU.is_ge, fill=NEG, base=0,
                                        pattern=[[-1, P]], channel_multiplier=1)

        with ExitStack() as c1:
            Xc = tools.sb("Xc", [P, NC + 1, KD, B, CW], F32, c1)

            def put_chunks(act, c, b, src):
                return nc.scalar.activation(Xc[:, c, :, b, HALO:CW], src, ACT.Copy)

            residual_and_norm(nc, tools, "n0", bank, ident, half, X, None, put_chunks, x_in=A["x"])
            with nc.Block() as block:
                @block.gpsimd
                def _(pool):
                    rows = Xc[:].rearrange("p c k b n -> p c (k b) n")
                    nc.gpsimd.memset(rows[:, 0, :, 0:HALO], 0.0)
                    nc.gpsimd.memset(rows[:, NC, :, 0:HALO], 0.0)
                    nc.gpsimd.tensor_copy(rows[:, 1:NC, :, 0:HALO], rows[:, 0:NC - 1, :, P:CW])
                    nc.gpsimd.tensor_copy(rows[:, NC, :, HALO:CW], rows[:, 0, :, HALO:CW])
            cst = (ident, half, cumsum_mask, ones, ident16, causal16, level0, level0_t, level_masks)
            delta_rule(nc, tools, bank, cst, X, Xc, Yt, A["L0_W_qkv"], A["L0_W_ab"], A["conv_w"], A["A_log"], A["dt_bias"],
                       A["o_norm_w"], A["L0_W_o"])

        with ExitStack() as c1:
            XT = tools.sb("XT", [P, KD, NC * B * P], F32, c1)

            def put_tokens(act, c, b, src):
                t = (c * B + b) * P
                return nc.scalar.activation(XT[:, :, t:t + P], src, ACT.Copy)

            plain = lambda c, b: Yt[:, ds(c, 1), b, :]
            rotated = lambda c, b: Yt2[:, ds(c + 1, 1), b, :]
            Yt2 = tools.sb("Yt2", [P, NC + 1, B, D], F32, c1)
            with nc.Block() as block:
                @block.gpsimd
                def _(pool):
                    nc.gpsimd.tensor_copy(Yt2[:, 0:NC, :, :], Yt[:])
                    nc.gpsimd.tensor_copy(Yt2[:, NC, :, :], Yt[:, 0, :, :])
            end = lambda k: (None, out) if stop_after == k else (put_tokens, None)
            put, store = end(1)
            residual_and_norm(nc, tools, "n1", bank, ident, half, X, rotated, put, store=store)
            if stop_after == 1:
                return
            int_ffn(nc, tools, bank, XT, Yt, A["gate_w"], A["gate_s"], A["up_w"], A["up_s"], A["down_w"], A["down_s"])
            put, store = end(2)
            residual_and_norm(nc, tools, "n2", bank, ident, half, X, plain, put, store=store)
            if stop_after == 2:
                return
            attention(nc, tools, PS, bank, ident, ident16, diag16, XT, Yt, A["at_wq"], A["at_bq"], A["at_cs"], A["at_wv"], A["at_bv"],
                      A["L1_W_dense"], A["L1_b_dense"])
            put, store = end(3)
            residual_and_norm(nc, tools, "n3", bank, ident, half, X, plain, put, store=store)
            if stop_after == 3:
                return
            experts(nc, tools, bank, ident, XT, Yt, A["w_router"], A["tri"], A["w1"], A["w3"], A["w2"])
            residual_and_norm(nc, tools, "n4", bank, ident, half, X, plain, None, store=out)


def constants():
    i = np.arange(P)
    r, c = i[:, None], i[None, :]
    parts = [r == c, r <= c]
    level0 = (r == c) | ((r // 2 == c // 2) & (r > c))
    parts += [level0, level0.T]
    for l in range(1, LEVELS):
        n = 1 << l
        first = i[(i // n) % 2 == 0]
        cc = first[None, :]
        parts.append((r == cc) | ((r // (2 * n) == cc // (2 * n)) & ((r // n) % 2 == 1)))
    masks = np.concatenate([p.astype(np.float32) for p in parts] + [np.where(r > c, np.float32(NEG), np.float32(0))] * U, axis=1)
    tri = (i[None, :E] < i[:E, None]).astype(np.float32).reshape(-1)
    rot = AD // 4
    inv = (np.float32(1) / np.float32(10000.0) ** (np.arange(0, rot, 2, dtype=np.float32) / np.float32(rot))).astype(np.float32)
    ang = np.outer(np.arange(T, dtype=np.float32), inv).astype(np.float32)
    cs = np.zeros((2, AD, T), np.float32)
    cs[0] = 1.0
    for d in range(rot):
        cs[0, d] = np.cos(ang[:, d % 2])
        cs[1, d] = np.sin(ang[:, d % 2]) * (-1.0 if d < rot // 2 else 1.0)
    return masks.astype(np.float32), tri, np.tile(cs, (1, P // AD, 1)).astype(np.float32)


def lay_out(a):
    masks, tri, cs = constants()
    rot = AD // 4
    partner = np.arange(AD)
    partner[:rot] = (partner[:rot] + rot // 2) % rot
    w = a["L1_attn_W_qkv"].reshape(D, AH, 3, AD)
    bias = a["L1_attn_b_qkv"].reshape(AH, 3, AD)
    wq = np.stack([w[:, :, 0, :], w[:, :, 0, partner], w[:, :, 1, :], w[:, :, 1, partner]]).reshape(4, D, AH * AD)
    bq = np.stack([bias[:, 0, :], bias[:, 0, partner], bias[:, 1, :], bias[:, 1, partner]]).reshape(4, KD, P).transpose(2, 0, 1)
    quarters = lambda s: s.reshape(D, NSH, EH).transpose(1, 0, 2)
    return {
        "x": a["L0_attn_hidden_states"], "L0_W_qkv": a["L0_attn_W_qkv"], "L0_W_ab": a["L0_attn_W_ab"],
        "conv_w": a["L0_attn_conv_w"], "A_log": a["L0_attn_A_log"], "dt_bias": a["L0_attn_dt_bias"],
        "o_norm_w": a["L0_attn_o_norm_w"], "L0_W_o": a["L0_attn_W_o"],
        "gate_w": a["L0_ffn_gate_w"].T, "gate_s": a["L0_ffn_gate_scale"].reshape(FI // P, P).T,
        "up_w": a["L0_ffn_up_w"].T, "up_s": a["L0_ffn_up_scale"].reshape(FI // P, P).T,
        "down_w": a["L0_ffn_down_w"].T, "down_s": a["L0_ffn_down_scale"],
        "at_wq": wq, "at_bq": bq, "at_cs": cs, "at_wv": w[:, :, 2, :].reshape(D, AH * AD), "at_bv": bias[:, 2, :].reshape(-1),
        "L1_W_dense": a["L1_attn_W_dense"], "L1_b_dense": a["L1_attn_b_dense"],
        "w_router": a["L1_ffn_w_router"],
        "w1": np.concatenate([quarters(a["L1_ffn_ws1"]), a["L1_ffn_we1"]]),
        "w3": np.concatenate([quarters(a["L1_ffn_ws3"]), a["L1_ffn_we3"]]),
        "w2": np.concatenate([a["L1_ffn_ws2"].reshape(NSH, EH, D), a["L1_ffn_we2"]]),
        "masks": masks, "tri": tri,
    }


STOP_AFTER = 4


def kernel(**inputs):
    import concourse.bacc as _bacc
    from concourse.bass_utils import run_bass_kernel_spmd as _run

    nc = _bacc.Bacc("TRN2", target_bir_lowering=False, num_devices=1)
    arrays, aps = {}, {}
    for name, a in lay_out({k: np.asarray(v) for k, v in inputs.items()}).items():
        a = np.ascontiguousarray(a)
        arrays[f"in_{name}"] = a
        aps[name] = nc.dram_tensor(f"in_{name}", a.shape, mybir.dt.from_np(a.dtype), kind="ExternalInput").ap()
    out = nc.dram_tensor("out_0", (B, T, D), F32, kind="ExternalOutput").ap()
    two_layers(nc, aps, out, STOP_AFTER)
    r = _run(nc, [arrays], core_ids=[0])
    return r.results[0]["out_0"]
```

```python
from contextlib import ExitStack

import numpy as np

import concourse.bass as bass
from concourse import mybir

F32 = mybir.dt.float32
BF16 = mybir.dt.bfloat16
I32 = mybir.dt.int32
ALU = mybir.AluOpType
ACT = mybir.ActivationFunctionType
AX = mybir.AxisListType
ds = bass.ds

P = 128
B, T, D = 2, 1024, 256
NC = T // P
KD = D // P
LN_EPS = 1e-5
H, DK = 16, 128
HP = H // 2
U = 2 * B
TAPS = 4
HALO = TAPS - 1
CW = P + HALO
L2_EPS = 1e-6
KINDS = (1, 0, 2)
LEVELS = 7
SLOTS = HP * NC
FI = 1024
AH, AD = 16, 16
E, EH, TOPK = 16, 128, 4
NSH = 4
NEG = -1e30


class PerSlot:

    def __init__(self, sem, n):
        self.sem, self.n = sem, n

    def after(self, s):
        return (s + 2) * self.n

    def step(self, s, k):
        return (s + 1) * self.n + k

    def before(self, s):
        return (s + 1) * self.n


class Counter:

    def __init__(self, sem):
        self.sem, self.v = sem, 0

    def bump(self, k=1):
        self.v += k
        return self.sem, k


class Tools:
    def __init__(self, nc, ctx):
        self.nc, self.ctx, self.phase = nc, ctx, []

    def sb(self, name, shape, dt=F32, ctx=None):
        return (ctx or self.ctx).enter_context(self.nc.sbuf_tensor(name, shape, dt))

    def sem(self, name, ctx=None):
        x = (ctx or self.ctx).enter_context(self.nc.semaphore(name))
        if ctx is not None:
            self.phase.append(x)
        return x

    def clear(self):
        with self.nc.Block() as block:
            @block.sync
            def _(sp):
                for x in self.phase:
                    sp.sem_clear(x)
        self.phase = []


def residual_and_norm(nc, tools, tag, bank, ident, half, X, Y, put, x_in=None, store=None):
    with ExitStack() as ctx:
        stats = tools.sb(tag + "_stats", [P, NC, B, 6], ctx=ctx)
        mv = tools.sb(tag + "_mv", [P, NC, B, 2], ctx=ctx)
        rstd = tools.sb(tag + "_rstd", [P, NC, B, 1], ctx=ctx)
        stats2 = tools.sb(tag + "_stats2", [P, NC, B, 6], ctx=ctx)
        mv2 = tools.sb(tag + "_mv2", [P, NC, B, 2], ctx=ctx)
        rstd2 = tools.sb(tag + "_rstd2", [P, NC, B, 1], ctx=ctx)
        normed = tools.sb(tag + "_normed", [P, B, D], ctx=ctx)
        yn = tools.sb(tag + "_yn", [P, NC, B, D], ctx=ctx) if Y else None
        x_loaded = tools.sem(tag + "_x_loaded")
        y_stats = tools.sem(tag + "_y_stats")
        y_aggr = tools.sem(tag + "_y_aggr")
        y_var = tools.sem(tag + "_y_var")
        y_rstd = tools.sem(tag + "_y_rstd")
        y_normed = tools.sem(tag + "_y_normed")
        x_added = tools.sem(tag + "_x_added")
        x_stats = tools.sem(tag + "_x_stats")
        x_aggr = tools.sem(tag + "_x_aggr")
        x_var = tools.sem(tag + "_x_var")
        x_rstd = tools.sem(tag + "_x_rstd")
        x_normed = tools.sem(tag + "_x_normed")
        transposed = tools.sem(tag + "_transposed")
        laid = tools.sem(tag + "_laid")
        stored = tools.sem(tag + "_stored")

        with nc.Block() as block:
            @block.sync
            def _(sp):
                if x_in is not None:
                    for b in range(B):
                        sp.dma_start(X[:, :, b, :], x_in[b].rearrange("(c p) d -> p c d", p=P)).then_inc(x_loaded, 16)
                if store is not None:
                    sp.wait_ge(x_added, NC * B)
                    for b in range(B):
                        sp.dma_start(store[b].rearrange("(c p) d -> p c d", p=P), X[:, :, b, :]).then_inc(stored, 16)
                    sp.wait_ge(stored, 16 * B)

            @block.vector
            def _(dve):
                if x_in is not None:
                    dve.wait_ge(x_loaded, 16 * B)
                if Y:
                    with dve.Fori(0, NC) as c:
                        for b in range(B):
                            nc.vector.bn_stats(stats[:, ds(c, 1), b, :], Y(c, b)).then_inc(y_stats, 1)
                    for t in range(NC * B):
                        dve.wait_ge(y_stats, t + 1)
                        nc.vector.bn_aggr(mv[:, t // B, t % B, :], stats[:, t // B, t % B, :]).then_inc(y_aggr, 1)
                    dve.wait_ge(y_aggr, NC * B)
                    nc.vector.tensor_scalar(rstd[:, :, :, 0], mv[:, :, :, 1], LN_EPS, None, ALU.add).then_inc(y_var, 1)
                    dve.wait_ge(y_rstd, 1)
                    with dve.Fori(0, NC) as c:
                        for b in range(B):
                            nc.vector.tensor_scalar(yn[:, ds(c, 1), b, :], Y(c, b), mv[:, ds(c, 1), b, 0:1],
                                                    rstd[:, ds(c, 1), b, :], ALU.subtract, ALU.mult).then_inc(y_normed, 1)
                        for b in range(B):
                            dve.wait_ge(y_normed, c * B + b + 1)
                            nc.vector.tensor_tensor(X[:, ds(c, 1), b, :], X[:, ds(c, 1), b, :], yn[:, ds(c, 1), b, :],
                                                    ALU.add).then_inc(x_added, 1)
                if put is None:
                    return
                with dve.Fori(0, NC) as c:
                    for b in range(B):
                        if Y:
                            dve.wait_ge(x_added, c * B + b + 1)
                        nc.vector.bn_stats(stats2[:, ds(c, 1), b, :], X[:, ds(c, 1), b, :]).then_inc(x_stats, 1)
                for t in range(NC * B):
                    dve.wait_ge(x_stats, t + 1)
                    nc.vector.bn_aggr(mv2[:, t // B, t % B, :], stats2[:, t // B, t % B, :]).then_inc(x_aggr, 1)
                dve.wait_ge(x_aggr, NC * B)
                nc.vector.tensor_scalar(rstd2[:, :, :, 0], mv2[:, :, :, 1], LN_EPS, None, ALU.add).then_inc(x_var, 1)
                dve.wait_ge(x_rstd, 1)
                for c in range(NC):
                    for b in range(B):
                        if c >= 1:
                            dve.wait_ge(transposed, (c - 1) * B + b + 1)
                        nc.vector.tensor_scalar(normed[:, b, :], X[:, c, b, :], mv2[:, c, b, 0:1], rstd2[:, c, b, :],
                                                ALU.subtract, ALU.mult).then_inc(x_normed, 1)

            @block.gpsimd
            def _(pool):
                if Y:
                    pool.wait_ge(y_var, 1)
                    nc.gpsimd.tensor_tensor(rstd[:, :, :, 0], rstd[:, :, :, 0],
                                            half[:, 0:1].broadcast_to([P, NC * B]).rearrange("p (c b) -> p c b", b=B),
                                            ALU.pow).then_inc(y_rstd, 1)
                if put is None:
                    return
                pool.wait_ge(x_var, 1)
                nc.gpsimd.tensor_tensor(rstd2[:, :, :, 0], rstd2[:, :, :, 0],
                                        half[:, 0:1].broadcast_to([P, NC * B]).rearrange("p (c b) -> p c b", b=B),
                                        ALU.pow).then_inc(x_rstd, 1)

            @block.tensor
            def _(pe):
                if put is None:
                    return
                for c in range(NC):
                    for b in range(B):
                        t = c * B + b
                        pe.wait_ge(x_normed, t + 1)
                        if t >= 2:
                            pe.wait_ge(laid, t - 1)
                        for k in range(KD):
                            last = nc.tensor.transpose(bank[t % 2][:, k * P:(k + 1) * P], normed[:, b, k * P:(k + 1) * P],
                                                       ident[:])
                        last.then_inc(transposed, 1)

            @block.scalar
            def _(act):
                if put is None:
                    return
                for c in range(NC):
                    for b in range(B):
                        t = c * B + b
                        act.wait_ge(transposed, t + 1)
                        put(act, c, b, bank[t % 2][:, 0:KD * P].rearrange("p (k n) -> p k n", k=KD)).then_inc(laid, 1)


def delta_rule(nc, tools, bank, cst, X, Xc, Acc, A_qkv, A_ab, A_conv, A_alog, A_dt, A_onorm, A_wo):
    ident, half, cumsum_mask, ones, ident16, causal16, level0, level0_t, level_masks = cst
    with ExitStack() as ctx:
        def sb(name, shape, dt=F32):
            return tools.sb("dr_" + name, shape, dt, ctx)

        def sem(name):
            return tools.sem("dr_" + name, ctx)

        Wab = sb("Wab", [P, KD, 2 * H])
        alog = sb("alog", [P, H])
        dtb = sb("dtb", [P, H])
        onorm = sb("onorm", [P, 1])
        z = sb("z", [P, NC * B, H])
        absz = sb("absz", [P, NC * B, H])
        g_all = sb("g_all", [P, NC * B, H])
        nG = sb("nG", [P, NC * B, H])
        eG = sb("eG", [P, NC * B, H])
        eGl = sb("eGl", [P, NC * B, H])
        beta = sb("beta", [P, NC * B, H])
        vecF_all = sb("vecF_all", [P, SLOTS, 3, U])
        vecB_all = sb("vecB_all", [P, SLOTS + 1, 3, U])
        ab_loaded = sem("ab_loaded")
        ab_ready = sem("ab_ready")
        sums_ready = sem("sums_ready")
        alog_exp = sem("alog_exp")
        abs_steps = sem("abs_steps")
        soft_exp = sem("soft_exp")
        soft_ln = sem("soft_ln")
        g_steps = sem("g_steps")
        beta_exp = sem("beta_exp")
        beta_steps = sem("beta_steps")
        G_neg = sem("G_neg")
        G_exp = sem("G_exp")
        firsts_cleared = sem("firsts_cleared")
        spread_done = sem("spread_done")

        with nc.Block() as block:
            @block.sync
            def _(sp):
                sp.dma_start(Wab[:], A_ab[:, 0:2 * H].rearrange("(k p) n -> p k n", p=P)).then_inc(ab_loaded, 16)
                sp.dma_start(alog[:], A_alog.partition_broadcast(P)).then_inc(ab_loaded, 16)
                sp.dma_start(dtb[:], A_dt.partition_broadcast(P)).then_inc(ab_loaded, 16)
                sp.dma_start(onorm[:], A_onorm.rearrange("(p a) -> p a", a=1)).then_inc(ab_loaded, 16)

            @block.tensor
            def _(pe):
                pe.wait_ge(ab_loaded, 64)
                for c in range(NC):
                    for b in range(B):
                        t = (c * B + b) * 2 * H
                        for k in range(KD):
                            last = nc.tensor.matmul(bank[0][:, t:t + 2 * H], Xc[:, c, k, b, HALO:CW], Wab[:, k, :],
                                                    start=(t == 0 and k == 0), stop=(k == KD - 1), skip_group_check=True)
                last.then_inc(ab_ready, 1)
                pe.wait_ge(g_steps, 3)
                gf = g_all[:].rearrange("p t h -> p (t h)")
                nc.tensor.matmul(bank[1][:, 0:NC * B * H], cumsum_mask[:], gf, start=True, stop=True).then_inc(sums_ready, 1)
                nc.tensor.matmul(bank[2][:, 0:NC * B * H], ones[:], gf, start=True, stop=True).then_inc(sums_ready, 1)

            ab = bank[0][:, :].rearrange("p (t n) -> p t n", n=2 * H)
            running = bank[1][:, 0:NC * B * H].rearrange("p (t h) -> p t h", h=H)
            whole = bank[2][:, 0:NC * B * H].rearrange("p (t h) -> p t h", h=H)

            @block.scalar
            def _(act):
                act.wait_ge(ab_loaded, 64)
                nc.scalar.activation(alog[:], alog[:], ACT.Exp).then_inc(alog_exp, 1)
                act.wait_ge(abs_steps, 3)
                nc.scalar.activation(absz[:], absz[:], ACT.Exp).then_inc(soft_exp, 1)
                nc.scalar.activation(beta[:], ab[:, :, H:2 * H], ACT.Exp, scale=-1.0).then_inc(beta_exp, 1)
                act.wait_ge(soft_exp, 1)
                nc.scalar.activation(absz[:], absz[:], ACT.Ln, bias=1.0).then_inc(soft_ln, 1)
                act.wait_ge(sums_ready, 2)
                act.wait_ge(G_neg, 1)
                nc.scalar.activation(eG[:], running, ACT.Exp).then_inc(G_exp, 1)
                nc.scalar.activation(eGl[:], whole, ACT.Exp).then_inc(G_exp, 1)

            @block.vector
            def _(dve):
                dve.wait_ge(ab_ready, 1)
                dve.wait_ge(alog_exp, 1)
                dtb_all = dtb[:].rearrange("p (a h) -> p a h", a=1).broadcast_to([P, NC * B, H])
                alog_all = alog[:].rearrange("p (a h) -> p a h", a=1).broadcast_to([P, NC * B, H])
                nc.vector.tensor_tensor(z[:], ab[:, :, 0:H], dtb_all, ALU.add).then_inc(abs_steps, 1)
                dve.wait_ge(abs_steps, 1)
                nc.vector.tensor_scalar(absz[:], z[:], -1.0, None, ALU.mult).then_inc(abs_steps, 1)
                dve.wait_ge(abs_steps, 2)
                nc.vector.tensor_tensor(absz[:], z[:], absz[:], ALU.min).then_inc(abs_steps, 1)
                dve.wait_ge(soft_ln, 1)
                nc.vector.scalar_tensor_tensor(g_all[:], z[:], 0.0, absz[:], ALU.max, ALU.add).then_inc(g_steps, 1)
                dve.wait_ge(g_steps, 1)
                nc.vector.tensor_tensor(g_all[:], g_all[:], alog_all, ALU.mult).then_inc(g_steps, 1)
                dve.wait_ge(g_steps, 2)
                nc.vector.tensor_scalar(g_all[:], g_all[:], -1.0, None, ALU.mult).then_inc(g_steps, 1)
                dve.wait_ge(beta_exp, 1)
                nc.vector.tensor_scalar(beta[:], beta[:], 1.0, None, ALU.add).then_inc(beta_steps, 1)
                dve.wait_ge(beta_steps, 1)
                nc.vector.reciprocal(beta[:], beta[:]).then_inc(beta_steps, 1)
                dve.wait_ge(beta_steps, 2)
                nc.vector.tensor_scalar(beta[:], beta[:], -2.0, None, ALU.mult).then_inc(beta_steps, 1)
                dve.wait_ge(sums_ready, 1)
                nc.vector.tensor_scalar(nG[:], running, -1.0, None, ALU.mult).then_inc(G_neg, 1)
                dve.wait_ge(G_exp, 2)
                nc.vector.memset(eG[:, 0:B, :], 0.0).then_inc(firsts_cleared, 1)
                nc.vector.memset(eGl[:, 0:B, :], 0.0).then_inc(firsts_cleared, 1)
                nc.vector.memset(vecB_all[:, 0, :, :], 0.0).then_inc(spread_done, 1)

                def spread(dst, src):
                    for b in range(B):
                        for hh in range(2):
                            nc.vector.tensor_copy(
                                dst[:, :, 2 * b + hh].rearrange("p (q c) -> p q c", c=NC),
                                src[:].rearrange("p (c b) h -> p b h c", b=B)[:, b, hh::2, :]).then_inc(spread_done, 1)

                dve.wait_ge(firsts_cleared, 2)
                dve.wait_ge(beta_steps, 3)
                dve.wait_ge(G_neg, 1)
                spread(vecF_all[:, :, 0, :], beta)
                spread(vecF_all[:, :, 1, :], g_all)
                spread(vecF_all[:, :, 2, :], nG)
                spread(vecB_all[:, 1:, 1, :], eG)
                spread(vecB_all[:, 1:, 2, :], eGl)
                dve.wait_ge(spread_done, 1 + 5 * U)
                nc.vector.tensor_scalar(vecB_all[:, 1:, 0, :], vecB_all[:, 1:, 1, :], -1.0, None,
                                        ALU.mult).then_inc(spread_done, 1)

        Wp = sb("Wp", [P, KD, 4, 2, P])
        Wo = sb("Wo", [P, 2, D])
        cw = sb("cw", [P, 2, 3, TAPS])
        xc = sb("xc", [P, KD, B, CW])
        conv = sb("conv", [P, 3, U, P])
        vecF = sb("vecF", [P, 3, U])
        vecB = sb("vecB", [P, 3, U])
        QK = sb("QK", [P, 2, U, P])
        Vt = sb("Vt", [P, U, P])
        QKsq = sb("QKsq", [P, 2, U, P])
        Ktok = sb("Ktok", [P, U, P])
        Vn = sb("Vn", [P, U, P])
        gate_next = sb("gate_next", [P, U, P])
        gate_this = sb("gate_this", [P, U, P])
        gate = sb("gate", [P, U, P])
        ss = sb("ss", [P, 2 * U])
        rs = sb("rs", [P, 2 * U])
        nk = sb("nk", [P, U])
        rk2 = sb("rk2", [P, U])
        negc = sb("negc", [P, U])
        w_next = sb("w_next", [P, U])
        w = sb("w", [P, U])
        rq = sb("rq", [P, U])
        Ex = sb("Ex", [P, U, P])
        AM = sb("AM", [P, U, 2, P])
        Tm = sb("Tm", [P, U, P])
        Xm = sb("Xm", [P, U, P])
        Lv = sb("Lv", [P, LEVELS - 1, U, P])
        RHS = sb("RHS", [P, U, P])
        Y = sb("Y", [P, U, P])
        Yw = sb("Yw", [P, U, P])
        QSg = sb("QSg", [P, U, P])
        O = sb("O", [P, U, P])
        Z = sb("Z", [P, U, P])
        Zsq = sb("Zsq", [P, U, P])
        ssz = sb("ssz", [P, U])
        f1 = sb("f1", [P, U])
        f2 = sb("f2", [P, U])
        f3 = sb("f3", [P, U])
        f4 = sb("f4", [P, U])
        f = sb("f", [P, U])
        Zf = sb("Zf", [P, U, P])
        ZT = sb("ZT", [P, U, P])
        S = sb("S", [P, U, P])
        half_u = half[:, 0:1].broadcast_to([P, 2 * U])

        credited = []

        def per_slot(name, n, credit=True):
            x = PerSlot(sem(name), n)
            if credit:
                credited.append(x)
            return x

        vecF_in = per_slot("vecF_in", 1)
        vecB_in = per_slot("vecB_in", 1)
        xc_in = PerSlot(sem("xc_in"), 1)
        W_ok = PerSlot(sem("W_ok"), 1)
        Wo_ok = PerSlot(sem("Wo_ok"), 1)
        W_dma = sem("W_dma")
        Wo_dma = sem("Wo_dma")
        projected = per_slot("projected", 6, credit=False)
        convolved = per_slot("convolved", 6, credit=False)
        taps = sem("taps")
        gate_projected = per_slot("gate_projected", 1, credit=False)
        gate_kept = per_slot("gate_kept", 1, credit=False)
        gate_moved = per_slot("gate_moved", 1)
        qk_silu = per_slot("qk_silu", 1)
        v_silu = per_slot("v_silu", 1)
        k_turned = per_slot("k_turned", 1)
        k_copied = per_slot("k_copied", 1)
        v_turned = per_slot("v_turned", 1)
        v_scaled = per_slot("v_scaled", 1)
        qk_squared = per_slot("qk_squared", 1)
        ss_ready = per_slot("ss_ready", 1)
        ss_copied = per_slot("ss_copied", 1)
        rs_ready = per_slot("rs_ready", 1)
        nk_ready = per_slot("nk_ready", 1)
        rk2_ready = per_slot("rk2_ready", 1)
        c_ready = per_slot("c_ready", 1)
        kq_ready = per_slot("kq_ready", 2)
        decay_ready = per_slot("decay_ready", 1)
        exp_ready = per_slot("exp_ready", 1)
        am_ready = per_slot("am_ready", U)
        diag_filled = per_slot("diag_filled", 1)
        x0_ready = per_slot("x0_ready", 1)
        w_ready = per_slot("w_ready", 1)
        at_ready = per_slot("at_ready", 2 * LEVELS)
        masked = per_slot("masked", 2 * LEVELS)
        tx_ready = per_slot("tx_ready", 2 * (LEVELS - 1))
        tx_copied = per_slot("tx_copied", 2 * (LEVELS - 1))
        gate_silu = per_slot("gate_silu", 1)
        ks_ready = per_slot("ks_ready", 1)
        qs_ready = per_slot("qs_ready", 1)
        rhs_ready = per_slot("rhs_ready", U)
        qs_scaled = per_slot("qs_scaled", 1)
        y_ready = per_slot("y_ready", 1)
        y_copied = per_slot("y_copied", 1)
        my_ready = per_slot("my_ready", 1)
        yw_ready = per_slot("yw_ready", 1)
        su_ready = per_slot("su_ready", 1)
        s_updated = per_slot("s_updated", 1)
        o_ready = per_slot("o_ready", 1)
        z_ready = per_slot("z_ready", 1)
        z_squared = per_slot("z_squared", 1)
        f_steps = per_slot("f_steps", 5)
        carried = per_slot("carried", 2)
        z_scaled = per_slot("z_scaled", 1)
        z_turned = per_slot("z_turned", 1)
        zt_copied = per_slot("zt_copied", 1)
        out_ready = per_slot("out_ready", 1)
        out_added = per_slot("out_added", 1)
        cleared = sem("cleared")
        settles = sem("settles")

        grp = lambda t, gi: t[:, 2 * gi:2 * gi + 2]

        def halves(ap, n):
            v = ap.rearrange("p u (m two n) -> p u m two n", two=2, n=n)
            return v[:, :, :, 0, :], v[:, :, :, 1, :]

        with nc.Block() as block:
            @block.gpsimd
            def _(pool):
                for t in (QK, Vn, Xm, AM, Ktok, S, gate_this):
                    nc.gpsimd.memset(t[:], 0.0)
                for t in (w, rq, w_next, rs, vecB):
                    nc.gpsimd.memset(t[:], 0.0)
                nc.gpsimd.memset(Acc[:], 0.0)
                for l in range(LEVELS - 1):
                    nc.gpsimd.tensor_copy(Lv[:, l, :, :], ident[:].rearrange("p (a n) -> p a n", a=1).broadcast_to([P, U, P]))
                nc.gpsimd.memset(Wo[:], 0.0).then_inc(cleared, 1)

            @block.sync
            def _(sp):
                for x in credited:
                    sp.sem_inc(x.sem, x.n)
                sp.sem_inc(Wo_ok.sem, 1)

        with nc.Block() as block:
            @block.sync
            def _(sp):
                def load_pair(hp):
                    for k in range(KD):
                        for kind, t in enumerate(KINDS):
                            sp.dma_start(Wp[:, k, kind, :, :], A_qkv[k * P:(k + 1) * P, ds(t * H * DK + hp * 2 * DK, 2 * DK)]
                                         .rearrange("p (h n) -> p h n", h=2)).then_inc(W_dma, 16)
                        sp.dma_start(Wp[:, k, 3, :, :], A_ab[k * P:(k + 1) * P, ds(2 * H + hp * 2 * DK, 2 * DK)]
                                     .rearrange("p (h n) -> p h n", h=2)).then_inc(W_dma, 16)
                    for kind, t in enumerate(KINDS):
                        for hh in range(2):
                            sp.dma_start(cw[:, hh, kind, :], A_conv[ds(t * H * DK + (hp * 2 + hh) * DK, DK), :]).then_inc(W_dma, 16)

                LOADS = 4 * KD + 6
                load_pair(0)
                sp.wait_ge(W_dma, 16 * LOADS)
                sp.sem_inc(W_ok.sem, NC)
                with sp.Fori(0, HP - 1) as q:
                    sp.wait_ge(out_ready.sem, out_ready.after(q * NC))
                    sp.dma_start(Wo[:], A_wo[ds(q * 2 * DK, 2 * DK), :].rearrange("(h p) n -> p h n", p=P)).then_inc(Wo_dma, 16)
                    sp.wait_ge(Wo_dma, (q + 1) * 16)
                    sp.sem_inc(Wo_ok.sem, NC)
                    last = q * NC + NC - 2
                    sp.wait_ge(projected.sem, projected.after(last))
                    sp.wait_ge(gate_projected.sem, gate_projected.after(last))
                    sp.wait_ge(convolved.sem, convolved.after(last))
                    load_pair(q + 1)
                    sp.wait_ge(W_dma, (q + 2) * 16 * LOADS)
                    sp.sem_inc(W_ok.sem, NC)
                q = HP - 1
                sp.sem_inc(W_ok.sem, 1)
                sp.wait_ge(out_ready.sem, out_ready.after(q * NC))
                sp.dma_start(Wo[:], A_wo[ds(q * 2 * DK, 2 * DK), :].rearrange("(h p) n -> p h n", p=P)).then_inc(Wo_dma, 16)
                sp.wait_ge(Wo_dma, (q + 1) * 16)
                sp.sem_inc(Wo_ok.sem, NC)

            @block.gpsimd
            def _(pool):
                def settled():
                    pool.sem_inc(settles, 1)

                def stage_x(c):
                    settled()
                    nc.gpsimd.tensor_copy(xc[:].rearrange("p k b n -> p (k b n)"),
                                          Xc[:, ds(c, 1), :, :, :].rearrange("p a k b n -> p (a k b n)")
                                          ).then_inc(xc_in.sem, 1)

                def stage_back(s):
                    pool.wait_ge(rhs_ready.sem, rhs_ready.before(s))
                    pool.wait_ge(qs_scaled.sem, qs_scaled.before(s))
                    pool.wait_ge(s_updated.sem, s_updated.before(s))
                    settled()
                    nc.gpsimd.tensor_copy(vecB[:], vecB_all[:, ds(s, 1), :, :].rearrange("p a v u -> p (a v) u")
                                          ).then_inc(vecB_in.sem, 1)

                def out_factors(s):
                    pool.wait_ge(z_squared.sem, z_squared.after(s))
                    pool.wait_ge(z_scaled.sem, z_scaled.before(s))
                    nc.gpsimd.tensor_tensor(f1[:], ssz[:], rq[:], ALU.mult).then_inc(f_steps.sem, 1)
                    pool.wait_ge(f_steps.sem, f_steps.step(s, 1))
                    nc.gpsimd.tensor_tensor(f2[:], f1[:], rq[:], ALU.mult).then_inc(f_steps.sem, 1)
                    pool.wait_ge(f_steps.sem, f_steps.step(s, 2))
                    settled()
                    nc.gpsimd.tensor_scalar(f3[:], f2[:], 1.0 / DK, LN_EPS * DK, ALU.mult, ALU.add).then_inc(f_steps.sem, 1)
                    pool.wait_ge(f_steps.sem, f_steps.step(s, 3))
                    nc.gpsimd.tensor_tensor(f4[:], f3[:], half_u[:, 0:U], ALU.pow).then_inc(f_steps.sem, 1)
                    pool.wait_ge(f_steps.sem, f_steps.step(s, 4))
                    nc.gpsimd.tensor_tensor(f[:], f4[:], rq[:], ALU.mult).then_inc(f_steps.sem, 1)

                stage_x(0)
                with pool.Fori(0, HP) as q:
                    with pool.Fori(0, NC) as c:
                        s = q * NC + c
                        stage_back(s)
                        pool.wait_ge(exp_ready.sem, exp_ready.before(s))
                        pool.wait_ge(decay_ready.sem, decay_ready.before(s))
                        settled()
                        nc.gpsimd.tensor_copy(vecF[:], vecF_all[:, ds(s, 1), :, :].rearrange("p a v u -> p (a v) u")
                                              ).then_inc(vecF_in.sem, 1)
                        pool.wait_ge(projected.sem, projected.before(s))
                        pool.wait_ge(gate_projected.sem, gate_projected.before(s))
                        stage_x(c + 1)
                        pool.wait_ge(gate_silu.sem, gate_silu.after(s))
                        pool.wait_ge(gate_kept.sem, gate_kept.before(s))
                        settled()
                        nc.gpsimd.tensor_copy(gate_this[:], gate_next[:]).then_inc(gate_moved.sem, 1)
                        pool.wait_ge(qk_silu.sem, qk_silu.after(s))
                        pool.wait_ge(ss_ready.sem, ss_ready.before(s))
                        nc.gpsimd.tensor_tensor(QKsq[:], QK[:], QK[:], ALU.mult).then_inc(qk_squared.sem, 1)
                        pool.wait_ge(ss_copied.sem, ss_copied.after(s))
                        nc.gpsimd.tensor_tensor(rs[:], ss[:], half_u, ALU.pow).then_inc(rs_ready.sem, 1)
                        pool.wait_ge(rs_ready.sem, rs_ready.after(s))
                        pool.wait_ge(v_scaled.sem, v_scaled.before(s))
                        nc.gpsimd.tensor_tensor(nk[:], ss[:, 0:U], rs[:, 0:U], ALU.mult).then_inc(nk_ready.sem, 1)
                        nc.gpsimd.tensor_tensor(rk2[:], rs[:, 0:U], rs[:, 0:U], ALU.mult).then_inc(rk2_ready.sem, 1)
                        pool.wait_ge(rk2_ready.sem, rk2_ready.after(s))
                        pool.wait_ge(am_ready.sem, am_ready.before(s))
                        pool.wait_ge(vecF_in.sem, vecF_in.after(s))
                        nc.gpsimd.tensor_tensor(negc[:], rk2[:], vecF[:, 0, :], ALU.mult).then_inc(c_ready.sem, 1)
                        pool.wait_ge(am_ready.sem, am_ready.after(s))
                        settled()
                        nc.gpsimd.affine_select(out=AM[:, :, 0, :], in_=AM[:, :, 0, :], compare_op=ALU.not_equal, fill=1.0,
                                                base=0, pattern=[[0, U], [-1, P]], channel_multiplier=1
                                                ).then_inc(diag_filled.sem, 1)
                        pool.wait_ge(diag_filled.sem, diag_filled.after(s))
                        pool.wait_ge(y_ready.sem, y_ready.after(s))
                        nc.gpsimd.tensor_tensor(Xm[:], AM[:, :, 0, :],
                                                level0_t[:].rearrange("p (a n) -> p a n", a=1).broadcast_to([P, U, P]),
                                                ALU.mult).then_inc(x0_ready.sem, 1)
                        pool.wait_ge(carried.sem, carried.before(s))
                        nc.gpsimd.tensor_tensor(w_next[:], Ex[:, :, P - 1], negc[:], ALU.mult).then_inc(w_ready.sem, 1)
                        out_factors(s)
                        pool.wait_ge(yw_ready.sem, yw_ready.after(s))
                        pool.wait_ge(w_ready.sem, w_ready.after(s))
                        pool.wait_ge(f_steps.sem, f_steps.after(s))
                        settled()
                        nc.gpsimd.tensor_copy(w[:], w_next[:]).then_inc(carried.sem, 1)
                        settled()
                        nc.gpsimd.tensor_copy(rq[:], rs[:, U:2 * U]).then_inc(carried.sem, 1)
                stage_back(SLOTS)
                out_factors(SLOTS)

            @block.scalar
            def _(act):
                def gate_to_silu(s):
                    act.wait_ge(gate_moved.sem, gate_moved.before(s))
                    act.wait_ge(z_ready.sem, z_ready.before(s))
                    nc.scalar.activation(gate[:], gate_this[:], ACT.Silu).then_inc(gate_silu.sem, 1)

                def keep_gate(s):
                    act.wait_ge(gate_projected.sem, gate_projected.after(s))
                    act.wait_ge(gate_moved.sem, gate_moved.after(s))
                    nc.scalar.activation(gate_next[:], bank[4][:].rearrange("p (u n) -> p u n", u=U), ACT.Copy
                                         ).then_inc(gate_kept.sem, 1)

                def back_1(s):
                    act.wait_ge(qs_ready.sem, qs_ready.after(s))
                    act.wait_ge(vecB_in.sem, vecB_in.after(s))
                    act.wait_ge(o_ready.sem, o_ready.before(s))
                    for u in range(U):
                        last = nc.scalar.activation(QSg[:, u, :], bank[6][:, u * P:(u + 1) * P], ACT.Copy,
                                                    scale=vecB[:, 1, u:u + 1])
                    last.then_inc(qs_scaled.sem, 1)
                    act.wait_ge(y_ready.sem, y_ready.after(s))
                    act.wait_ge(my_ready.sem, my_ready.before(s))
                    act.wait_ge(yw_ready.sem, yw_ready.before(s))
                    nc.scalar.activation(Y[:], bank[5][:].rearrange("p (u n) -> p u n", u=U), ACT.Copy).then_inc(y_copied.sem, 1)

                def back_2(s):
                    act.wait_ge(z_ready.sem, z_ready.after(s))
                    act.wait_ge(f_steps.sem, f_steps.before(s))
                    for u in range(U):
                        last = nc.scalar.activation(Zsq[:, u, :], Z[:, u, :], ACT.Square, accum_out=ssz[:, u:u + 1])
                    last.then_inc(z_squared.sem, 1)

                def back_3(s):
                    act.wait_ge(f_steps.sem, f_steps.after(s))
                    act.wait_ge(z_turned.sem, z_turned.before(s))
                    for u in range(U):
                        last = nc.scalar.activation(Zf[:, u, :], Z[:, u, :], ACT.Copy, scale=f[:, u:u + 1])
                    last.then_inc(z_scaled.sem, 1)

                def back_4(s):
                    act.wait_ge(z_turned.sem, z_turned.after(s))
                    act.wait_ge(out_ready.sem, out_ready.before(s))
                    nc.scalar.activation(ZT[:], bank[7][:].rearrange("p (u n) -> p u n", u=U), ACT.Copy,
                                         scale=onorm[:, 0:1]).then_inc(zt_copied.sem, 1)

                def copy_level(s, l, gi):
                    n = 1 << l
                    i = 2 * (l - 1) + gi
                    act.wait_ge(tx_ready.sem, tx_ready.step(s, i + 1))
                    b = bank[2 + gi]
                    t1, _ = halves(grp(Tm, gi), n)
                    _, x2 = halves(grp(Xm, gi), n)
                    if l < LEVELS - 1:
                        nc.scalar.activation(t1, b[:, 128:256].rearrange("p (u m n) -> p u m n", u=2, n=n), ACT.Copy)
                    nc.scalar.activation(x2, b[:, 256:384].rearrange("p (u m n) -> p u m n", u=2, n=n), ACT.Copy
                                         ).then_inc(tx_copied.sem, 1)

                keep_gate(-1)
                with act.Fori(0, HP) as q:
                    with act.Fori(0, NC) as c:
                        s = q * NC + c
                        gate_to_silu(s)
                        act.wait_ge(convolved.sem, convolved.before(s))
                        act.wait_ge(qs_ready.sem, qs_ready.after(s))
                        act.wait_ge(qk_squared.sem, qk_squared.before(s))
                        nc.scalar.activation(QK[:], conv[:, 0:2, :, :], ACT.Silu).then_inc(qk_silu.sem, 1)
                        nc.scalar.activation(Vt[:], conv[:, 2, :, :], ACT.Silu).then_inc(v_silu.sem, 1)
                        back_1(s)
                        act.wait_ge(decay_ready.sem, decay_ready.after(s))
                        act.wait_ge(w_ready.sem, w_ready.before(s))
                        for u in range(U):
                            last = nc.scalar.activation(Ex[:, u, :], bank[0][:, u * P:(u + 1) * P], ACT.Exp,
                                                        bias=vecF[:, 2, u:u + 1])
                        last.then_inc(exp_ready.sem, 1)
                        act.wait_ge(k_turned.sem, k_turned.after(s))
                        act.wait_ge(su_ready.sem, su_ready.after(s))
                        nc.scalar.activation(Ktok[:], bank[7][:].rearrange("p (u n) -> p u n", u=U), ACT.Copy
                                             ).then_inc(k_copied.sem, 1)
                        back_2(s)
                        for l in range(1, LEVELS):
                            for gi in range(2):
                                copy_level(s, l, gi)
                            if l == 2:
                                back_3(s)
                            if l == 3:
                                back_4(s)
                        keep_gate(s)
                s = SLOTS
                gate_to_silu(s)
                back_1(s)
                back_2(s)
                back_3(s)
                back_4(s)

            @block.vector
            def _(dve):
                tap_count = [0]

                def convolve(s, i):
                    kind, hh = i // 2, i % 2
                    dve.wait_ge(projected.sem, projected.step(s, i + 1))
                    if i == 0:
                        dve.wait_ge(W_ok.sem, s + 2)
                        dve.wait_ge(qk_silu.sem, qk_silu.after(s))
                        dve.wait_ge(v_silu.sem, v_silu.after(s))
                    src = bank[i % 2][:, 0:B * CW].rearrange("p (b n) -> p b n", b=B)
                    out = conv[:, kind, hh::2, :]
                    n = (TAPS - 1) * i
                    nc.vector.tensor_scalar(out, src[:, :, 0:P], cw[:, hh, kind, 0:1], None, ALU.mult).then_inc(taps, 1)
                    for j in range(1, TAPS):
                        dve.wait_ge(taps, (s + 1) * 18 + n + j)
                        ins = nc.vector.scalar_tensor_tensor(out, src[:, :, j:j + P], cw[:, hh, kind, j:j + 1], out,
                                                             ALU.mult, ALU.add)
                        ins.then_inc(*((taps, 1) if j < TAPS - 1 else (convolved.sem, 1)))

                def back_1(s):
                    dve.wait_ge(ks_ready.sem, ks_ready.after(s))
                    dve.wait_ge(vecB_in.sem, vecB_in.after(s))
                    dve.wait_ge(v_scaled.sem, v_scaled.before(s))
                    for u in range(U):
                        nc.vector.scalar_tensor_tensor(RHS[:, u, :], bank[5][:, u * P:(u + 1) * P], vecB[:, 0, u:u + 1],
                                                       Vn[:, u, :], ALU.mult, ALU.add).then_inc(rhs_ready.sem, 1)
                    dve.wait_ge(y_copied.sem, y_copied.after(s))
                    dve.wait_ge(carried.sem, carried.before(s))
                    nc.vector.tensor_tensor(Yw[:], Y[:], w[:].rearrange("p (u a) -> p u a", a=1).broadcast_to([P, U, P]),
                                            ALU.mult).then_inc(yw_ready.sem, 1)
                    dve.wait_ge(su_ready.sem, su_ready.after(s))
                    for u in range(U):
                        last = nc.vector.scalar_tensor_tensor(S[:, u, :], S[:, u, :], vecB[:, 2, u:u + 1],
                                                              bank[5][:, u * P:(u + 1) * P], ALU.mult, ALU.subtract)
                    last.then_inc(s_updated.sem, 1)
                    dve.wait_ge(my_ready.sem, my_ready.after(s))
                    dve.wait_ge(qs_scaled.sem, qs_scaled.after(s))
                    nc.vector.tensor_tensor(O[:], QSg[:], bank[6][:].rearrange("p (u n) -> p u n", u=U),
                                            ALU.subtract).then_inc(o_ready.sem, 1)
                    dve.wait_ge(o_ready.sem, o_ready.after(s))
                    dve.wait_ge(gate_silu.sem, gate_silu.after(s))
                    dve.wait_ge(z_scaled.sem, z_scaled.before(s))
                    nc.vector.tensor_tensor(Z[:], O[:], gate[:], ALU.mult).then_inc(z_ready.sem, 1)

                def back_2(s, acc):
                    dve.wait_ge(out_ready.sem, out_ready.after(s))
                    nc.vector.tensor_tensor(acc, acc, bank[7][:], ALU.add).then_inc(out_added.sem, 1)

                def mask_level(s, l, gi):
                    n = 1 << l
                    i = 2 * l + gi
                    dve.wait_ge(at_ready.sem, at_ready.step(s, i + 1))
                    b = bank[2 + gi]
                    if l == 0:
                        nc.vector.tensor_tensor(grp(Tm, gi), b[:, 0:2 * P].rearrange("p (u n) -> p u n", u=2),
                                                level0[:].rearrange("p (a n) -> p a n", a=1).broadcast_to([P, 2, P]),
                                                ALU.mult).then_inc(masked.sem, 1)
                        return
                    for u in range(2):
                        l1, _ = halves(Lv[:, l - 1, 2 * gi + u:2 * gi + u + 1, :], n)
                        last = nc.vector.tensor_tensor(l1[:, 0], b[:, u * 64:(u + 1) * 64].rearrange("p (m n) -> p m n", n=n),
                                                       level_masks[:, l - 1, :].rearrange("p (m n) -> p m n", n=n), ALU.mult)
                    last.then_inc(masked.sem, 1)

                for i in range(6):
                    convolve(-1, i)
                with dve.Fori(0, HP) as q:
                    with dve.Fori(0, NC) as c:
                        s = q * NC + c
                        back_1(s)
                        dve.wait_ge(ss_ready.sem, ss_ready.after(s))
                        dve.wait_ge(nk_ready.sem, nk_ready.before(s))
                        nc.vector.tensor_scalar(ss[:], bank[1][:, 0:2 * U], L2_EPS, None, ALU.add).then_inc(ss_copied.sem, 1)
                        dve.wait_ge(v_turned.sem, v_turned.after(s))
                        dve.wait_ge(nk_ready.sem, nk_ready.after(s))
                        nc.vector.tensor_tensor(Vn[:], bank[4][:].rearrange("p (u n) -> p u n", u=U),
                                                nk[:].rearrange("p (u a) -> p u a", a=1).broadcast_to([P, U, P]),
                                                ALU.mult).then_inc(v_scaled.sem, 1)
                        dve.wait_ge(exp_ready.sem, exp_ready.after(s))
                        dve.wait_ge(c_ready.sem, c_ready.after(s))
                        dve.wait_ge(my_ready.sem, my_ready.after(s))
                        for u in range(U):
                            dve.wait_ge(kq_ready.sem, kq_ready.step(s, u // 2 + 1))
                            o = (u % 2) * 2 * P
                            nc.vector.scalar_tensor_tensor(
                                AM[:, u, :, :], bank[2 + u // 2][:, o:o + 2 * P].rearrange("p (a n) -> p a n", a=2),
                                negc[:, u:u + 1], Ex[:, u:u + 1, :].broadcast_to([P, 2, P]),
                                ALU.mult, ALU.mult).then_inc(am_ready.sem, 1)
                        for l in range(LEVELS):
                            for gi in range(2):
                                mask_level(s, l, gi)
                            if l >= 1:
                                convolve(s, l - 1)
                        back_2(s, Acc[:, ds(c, 1), :, :].rearrange("p a b d -> p (a b d)"))
                s = SLOTS
                back_1(s)
                back_2(s, Acc[:, 0, :, :].rearrange("p b d -> p (b d)"))

            @block.tensor
            def _(pe):
                def project(s, i):
                    kind, hh = i // 2, i % 2
                    if i == 0:
                        pe.wait_ge(W_ok.sem, s + 2)
                        pe.wait_ge(xc_in.sem, s + 2)
                        pe.wait_ge(exp_ready.sem, exp_ready.after(s))
                    elif i == 1:
                        pe.wait_ge(ss_copied.sem, ss_copied.after(s))
                    else:
                        pe.wait_ge(convolved.sem, convolved.step(s, i - 1))
                    for k in range(KD):
                        last = nc.tensor.matmul(bank[i % 2][:, 0:B * CW].rearrange("p (b n) -> p b n", b=B),
                                                Wp[:, k, kind, hh, :], xc[:, k, :, :], start=(k == 0), stop=(k == KD - 1))
                    last.then_inc(projected.sem, 1)

                def project_gate(s):
                    pe.wait_ge(v_scaled.sem, v_scaled.after(s))
                    for b in range(B):
                        for k in range(KD):
                            last = nc.tensor.matmul(bank[4][:, b * 2 * P:(b + 1) * 2 * P], xc[:, k, b, HALO:CW],
                                                    Wp[:, k, 3, :, :], start=(b == 0 and k == 0), stop=(k == KD - 1),
                                                    skip_group_check=True)
                    last.then_inc(gate_projected.sem, 1)

                def each_unit(dst, lhs, rhs):
                    for u in range(U):
                        last = nc.tensor.matmul(dst[:, u * P:(u + 1) * P], lhs(u), rhs(u), start=True, stop=True)
                    return last

                def back_1(s):
                    pe.wait_ge(s_updated.sem, s_updated.before(s))
                    pe.wait_ge(o_ready.sem, o_ready.before(s))
                    each_unit(bank[5], lambda u: QK[:, 0, u, :], lambda u: S[:, u, :]).then_inc(ks_ready.sem, 1)
                    each_unit(bank[6], lambda u: QK[:, 1, u, :], lambda u: S[:, u, :]).then_inc(qs_ready.sem, 1)

                def back_2(s):
                    pe.wait_ge(rhs_ready.sem, rhs_ready.after(s))
                    pe.wait_ge(tx_copied.sem, tx_copied.before(s))
                    each_unit(bank[5], lambda u: Xm[:, u, :], lambda u: RHS[:, u, :]).then_inc(y_ready.sem, 1)

                def back_3(s):
                    pe.wait_ge(y_copied.sem, y_copied.after(s))
                    pe.wait_ge(qs_scaled.sem, qs_scaled.after(s))
                    each_unit(bank[6], lambda u: AM[:, u, 1, :], lambda u: Y[:, u, :]).then_inc(my_ready.sem, 1)
                    pe.wait_ge(yw_ready.sem, yw_ready.after(s))
                    each_unit(bank[5], lambda u: Ktok[:, u, :], lambda u: Yw[:, u, :]).then_inc(su_ready.sem, 1)

                def turn_z(s, loop=True):
                    if loop:
                        pe.wait_ge(k_copied.sem, k_copied.after(s))
                    pe.wait_ge(z_scaled.sem, z_scaled.after(s))
                    for u in range(U):
                        last = nc.tensor.transpose(bank[7][:, u * P:(u + 1) * P], Zf[:, u, :], ident[:])
                    last.then_inc(z_turned.sem, 1)

                def output(s):
                    pe.wait_ge(zt_copied.sem, zt_copied.after(s))
                    pe.wait_ge(Wo_ok.sem, s + 1)
                    for b in range(B):
                        for hh in range(2):
                            last = nc.tensor.matmul(bank[7][:, b * D:(b + 1) * D], ZT[:, 2 * b + hh, :], Wo[:, hh, :],
                                                    start=(b == 0 and hh == 0), stop=(hh == 1), skip_group_check=True)
                    last.then_inc(out_ready.sem, 1)

                def multiply_at(s, l, gi):
                    b = bank[2 + gi]
                    n = 1 << l
                    if l == 0:
                        pe.wait_ge(diag_filled.sem, diag_filled.after(s))
                        for u in range(2):
                            last = nc.tensor.transpose(b[:, u * P:(u + 1) * P], AM[:, 2 * gi + u, 0, :], ident[:])
                        last.then_inc(at_ready.sem, 1)
                        return
                    if l == 1:
                        pe.wait_ge(masked.sem, masked.step(s, gi + 1))
                    else:
                        pe.wait_ge(tx_copied.sem, tx_copied.step(s, 2 * (l - 2) + gi + 1))
                    t1, _ = halves(grp(Tm, gi), n)
                    for u in range(2):
                        last = nc.tensor.matmul(b[:, u * 64:(u + 1) * 64].rearrange("p (m n) -> p m n", n=n),
                                                AM[:, 2 * gi + u, 0, :], t1[:, u], start=True, stop=True)
                    last.then_inc(at_ready.sem, 1)

                def multiply_tx(s, l, gi):
                    b = bank[2 + gi]
                    n = 1 << l
                    pe.wait_ge(masked.sem, masked.step(s, 2 * l + gi + 1))
                    if l == 1:
                        pe.wait_ge(x0_ready.sem, x0_ready.after(s))
                    _, x2 = halves(grp(Xm, gi), n)
                    l1, _ = halves(grp(Lv[:, l - 1], gi), n)
                    for u in range(2):
                        if l < LEVELS - 1:
                            nc.tensor.matmul(b[:, 128 + u * 64:128 + (u + 1) * 64].rearrange("p (m n) -> p m n", n=n),
                                             Xm[:, 2 * gi + u, :], l1[:, u], start=True, stop=True)
                        last = nc.tensor.matmul(b[:, 256 + u * 64:256 + (u + 1) * 64].rearrange("p (m n) -> p m n", n=n),
                                                Lv[:, l - 1, 2 * gi + u, :], x2[:, u], start=True, stop=True)
                    last.then_inc(tx_ready.sem, 1)

                for i in range(6):
                    project(-1, i)
                project_gate(-1)
                with pe.Fori(0, HP) as q:
                    with pe.Fori(0, NC) as c:
                        s = q * NC + c
                        back_1(s)
                        pe.wait_ge(vecF_in.sem, vecF_in.after(s))
                        pe.wait_ge(convolved.sem, convolved.before(s))
                        nc.tensor.matmul(bank[0][:], ident16[:], causal16[:], start=True, stop=False, skip_group_check=True)
                        for u in range(U):
                            last = nc.tensor.matmul(bank[0][:, u * P:(u + 1) * P], vecF[:, 1, u:u + 1].broadcast_to([P, P]),
                                                    cumsum_mask[:], start=False, stop=True, skip_group_check=True)
                        last.then_inc(decay_ready.sem, 1)
                        back_2(s)
                        pe.wait_ge(qk_silu.sem, qk_silu.after(s))
                        for u in range(U):
                            last = nc.tensor.matmul(bank[2 + u // 2][:, (u % 2) * 2 * P:(u % 2 + 1) * 2 * P]
                                                    .rearrange("p (a n) -> p a n", a=2), QK[:, 0, u, :],
                                                    QK[:, :, u, :], start=True, stop=True)
                            if u % 2:
                                last.then_inc(kq_ready.sem, 1)
                        pe.wait_ge(out_added.sem, out_added.before(s))
                        for u in range(U):
                            last = nc.tensor.transpose(bank[7][:, u * P:(u + 1) * P], QK[:, 0, u, :], ident[:])
                        last.then_inc(k_turned.sem, 1)
                        pe.wait_ge(v_silu.sem, v_silu.after(s))
                        pe.wait_ge(gate_kept.sem, gate_kept.before(s))
                        for u in range(U):
                            last = nc.tensor.transpose(bank[4][:, u * P:(u + 1) * P], Vt[:, u, :], ident[:])
                        last.then_inc(v_turned.sem, 1)
                        pe.wait_ge(qk_squared.sem, qk_squared.after(s))
                        for a in range(2):
                            for u in range(U):
                                last = nc.tensor.matmul(bank[1][:, a * U + u:a * U + u + 1], QKsq[:, a, u, :], ones[:, 0:1],
                                                        start=True, stop=True)
                        last.then_inc(ss_ready.sem, 1)
                        back_3(s)
                        for l in range(LEVELS):
                            for gi in range(2):
                                multiply_at(s, l, gi)
                            if l >= 1:
                                project(s, l - 1)
                                for gi in range(2):
                                    multiply_tx(s, l, gi)
                            if l == 3:
                                turn_z(s)
                            if l == 5:
                                output(s)
                        project_gate(s)
                s = SLOTS
                back_1(s)
                back_2(s)
                back_3(s)
                turn_z(s, loop=False)
                output(s)
        tools.clear()


def int_ffn(nc, tools, bank, XT, Yt, A_gate, A_gs, A_up, A_us, A_down, A_dsc):
    IT = FI // P
    NB = NC * B // 4
    with ExitStack() as ctx:
        def sb(name, shape, dt=F32):
            return tools.sb("ff_" + name, shape, dt, ctx)

        def sem(name):
            return tools.sem("ff_" + name)

        Wi = sb("Wi", [P, 3, KD * FI], I32)
        Wf = sb("Wf", [P, 3, KD * FI])
        gs = sb("gs", [P, IT])
        us = sb("us", [P, IT])
        dsc = sb("dsc", [P, D])
        sg = sb("sg", [P, 2, 4 * P])
        hT = sb("hT", [P, IT, 4 * P])
        w_loaded = [sem(f"w{i}_loaded") for i in range(3)]
        scales_loaded = sem("scales_loaded")
        w_made = sem("w_made")
        gu_ready = PerSlot(sem("gu_ready"), IT)
        g_silu = PerSlot(sem("g_silu"), IT)
        h_ready = PerSlot(sem("h_ready"), IT)
        y_ready = PerSlot(sem("y_ready"), 4)
        y_scaled = PerSlot(sem("y_scaled"), 4)
        Wg = Wf[:, 0, :].rearrange("p (k i) -> p k i", k=KD)
        Wu = Wf[:, 1, :].rearrange("p (k i) -> p k i", k=KD)
        Wd = Wf[:, 2, :].rearrange("p (t d) -> p t d", t=IT)
        Yv = Yt[:].rearrange("p c b d -> p (c b) d")

        with nc.Block() as block:
            @block.sync
            def _(sp):
                for x in (g_silu, h_ready, y_ready, y_scaled, gu_ready):
                    sp.sem_inc(x.sem, x.n)
        with nc.Block() as block:
            @block.sync
            def _(sp):
                sp.dma_start(Wi[:, 0, :].rearrange("p (k i) -> p k i", k=KD), A_gate.rearrange("(k p) i -> p k i", p=P)).then_inc(w_loaded[0], 16)
                sp.dma_start(Wi[:, 1, :].rearrange("p (k i) -> p k i", k=KD), A_up.rearrange("(k p) i -> p k i", p=P)).then_inc(w_loaded[1], 16)
                sp.dma_start(Wi[:, 2, :].rearrange("p (t d) -> p t d", t=IT), A_down.rearrange("(t p) d -> p t d", p=P)).then_inc(w_loaded[2], 16)
                sp.dma_start(gs[:], A_gs).then_inc(scales_loaded, 16)
                sp.dma_start(us[:], A_us).then_inc(scales_loaded, 16)
                sp.dma_start(dsc[:], A_dsc.partition_broadcast(P)).then_inc(scales_loaded, 16)

            @block.tensor
            def _(pe):
                pe.wait_ge(w_made, 2)
                with pe.Fori(0, NB) as n:
                    for i in range(IT):
                        pe.wait_ge(g_silu.sem, g_silu.step(n, i - 1))
                        pe.wait_ge(h_ready.sem, h_ready.step(n, i - 1))
                        for w, bk in ((Wg, bank[i % 2]), (Wu, bank[2 + i % 2])):
                            for k in range(KD):
                                last = nc.tensor.matmul(bk[:], w[:, k, i * P:(i + 1) * P], XT[:, k, ds(n * 4 * P, 4 * P)],
                                                        start=(k == 0), stop=(k == KD - 1))
                        last.then_inc(gu_ready.sem, 1)
                    pe.wait_ge(h_ready.sem, h_ready.after(n))
                    pe.wait_ge(w_made, 3)
                    for j in range(4):
                        pe.wait_ge(y_scaled.sem, y_scaled.step(n, j - 1))
                        for i in range(IT):
                            last = nc.tensor.matmul(bank[4 + j % 2][:, 0:D], hT[:, i, j * P:(j + 1) * P], Wd[:, i, :],
                                                    start=(i == 0), stop=(i == IT - 1))
                        last.then_inc(y_ready.sem, 1)

            @block.scalar
            def _(act):
                act.wait_ge(scales_loaded, 48)
                with act.Fori(0, NB) as n:
                    for i in range(IT):
                        act.wait_ge(gu_ready.sem, gu_ready.step(n, i + 1))
                        act.wait_ge(h_ready.sem, h_ready.step(n, i - 1))
                        nc.scalar.activation(sg[:, i % 2, :], bank[i % 2][:], ACT.Silu, scale=gs[:, i:i + 1]).then_inc(g_silu.sem, 1)

            @block.vector
            def _(dve):
                for i in range(3):
                    dve.wait_ge(w_loaded[i], 16)
                    nc.vector.tensor_scalar(Wf[:, i, :], Wi[:, i, :], -128.0, None, ALU.add).then_inc(w_made, 1)
                dve.wait_ge(scales_loaded, 48)
                with dve.Fori(0, NB) as n:
                    for i in range(IT):
                        dve.wait_ge(g_silu.sem, g_silu.step(n, i + 1))
                        if i == 0:
                            dve.wait_ge(y_ready.sem, y_ready.before(n))
                        nc.vector.scalar_tensor_tensor(hT[:, i, :], bank[2 + i % 2][:], us[:, i:i + 1], sg[:, i % 2, :],
                                                       ALU.mult, ALU.mult).then_inc(h_ready.sem, 1)
                    for j in range(4):
                        dve.wait_ge(y_ready.sem, y_ready.step(n, j + 1))
                        nc.vector.tensor_tensor(Yv[:, ds(n * 4 + j, 1), :].rearrange("p a d -> p (a d)"), bank[4 + j % 2][:, 0:D],
                                                dsc[:], ALU.mult).then_inc(y_scaled.sem, 1)


def attention(nc, tools, PS, bank, ident, ident16, causal16, diag16, XT, Yt, A_wq, A_bq, A_cs, A_wv, A_bv, A_wd, A_bd):
    NB = NC * B // 4
    KB = 4
    with ExitStack() as ctx:
        def sb(name, shape, dt=F32):
            return tools.sb("at_" + name, shape, dt, ctx)

        def sem(name):
            return tools.sem("at_" + name)

        QP = sb("QP", [P, 3, 2, KD, B, T], BF16)
        V = sb("V", [P, NC, B, AH, AD + 1])
        Wdn = sb("Wdn", [P, KD, D])
        bd = sb("bd", [P, D])
        w_loaded = sem("w_loaded")
        with ExitStack() as ctx2:
            QF = tools.sb("at_QF", [P, 2, KD, B, T], F32, ctx2)
            Wq = tools.sb("at_Wq", [P, KD, 4, D], F32, ctx2)
            Wv = tools.sb("at_Wv", [P, KD, D], F32, ctx2)
            bq = tools.sb("at_bq", [P, 4, KD], F32, ctx2)
            bv = tools.sb("at_bv", [P, D], F32, ctx2)
            cs = tools.sb("at_cs", [P, 2, T], F32, ctx2)
            qa = tools.sb("at_qa", [P, 2, 2, 4 * P], F32, ctx2)
            qm = tools.sb("at_qm", [P, 2, 2, 4 * P], F32, ctx2)
            qk_ready = PerSlot(sem("qk_ready"), 4)
            biased = PerSlot(sem("biased"), 4)
            rotated = PerSlot(sem("rotated"), 8)
            summed = PerSlot(sem("summed"), 4)
            v_ready = sem("v_ready")
            v_added = sem("v_added")
            part_cast = sem("part_cast")
            rest_taken = sem("rest_taken")
            with nc.Block() as block:
                @block.sync
                def _(sp):
                    for x in (qk_ready, biased, rotated, summed):
                        sp.sem_inc(x.sem, x.n)

                @block.gpsimd
                def _(pool):
                    nc.gpsimd.memset(V[:], 1.0)
            with nc.Block() as block:
                @block.sync
                def _(sp):
                    for k in range(KD):
                        sp.dma_start(Wq[:, k, :, :], A_wq[:, k * P:(k + 1) * P, :].rearrange("a p n -> p a n")).then_inc(w_loaded, 16)
                        sp.dma_start(Wv[:, k, :], A_wv[k * P:(k + 1) * P, :]).then_inc(w_loaded, 16)
                        sp.dma_start(Wdn[:, k, :], A_wd[k * P:(k + 1) * P, :]).then_inc(w_loaded, 16)
                    sp.dma_start(bq[:], A_bq).then_inc(w_loaded, 16)
                    sp.dma_start(cs[:], A_cs.rearrange("a p t -> p a t")).then_inc(w_loaded, 16)
                    sp.dma_start(bv[:], A_bv.partition_broadcast(P)).then_inc(w_loaded, 16)
                    sp.dma_start(bd[:], A_bd.partition_broadcast(P)).then_inc(w_loaded, 16)

                LOADED = 16 * (3 * KD + 4)

                @block.tensor
                def _(pe):
                    pe.wait_ge(w_loaded, LOADED)
                    with pe.Fori(0, NB) as n:
                        for i in range(4):
                            a, m = i // 2, i % 2
                            pe.wait_ge(biased.sem, biased.step(n, i - 1))
                            for part in range(2):
                                for k in range(KD):
                                    last = nc.tensor.matmul(bank[2 * (i % 2) + part][:], Wq[:, k, 2 * a + part, m * P:(m + 1) * P],
                                                            XT[:, k, ds(n * 4 * P, 4 * P)], start=(k == 0), stop=(k == KD - 1))
                            last.then_inc(qk_ready.sem, 1)
                    for t in range(NC * B):
                        if t >= 2:
                            pe.wait_ge(v_added, t - 1)
                        for k in range(KD):
                            last = nc.tensor.matmul(bank[4 + t % 2][:, 0:D], XT[:, k, t * P:(t + 1) * P], Wv[:, k, :],
                                                    start=(k == 0), stop=(k == KD - 1))
                        last.then_inc(v_ready, 1)

                @block.scalar
                def _(act):
                    act.wait_ge(w_loaded, LOADED)
                    with act.Fori(0, NB) as n:
                        for i in range(4):
                            a, m = i // 2, i % 2
                            act.wait_ge(qk_ready.sem, qk_ready.step(n, i + 1))
                            act.wait_ge(rotated.sem, rotated.step(n, 2 * (i - 1)))
                            for part in range(2):
                                last = nc.scalar.activation(qa[:, i % 2, part, :], bank[2 * (i % 2) + part][:], ACT.Identity,
                                                            bias=bq[:, 2 * a + part, m:m + 1])
                            last.then_inc(biased.sem, 1)

                @block.vector
                def _(dve):
                    dve.wait_ge(w_loaded, LOADED)
                    with dve.Fori(0, NB) as n:
                        for i in range(4):
                            a, m = i // 2, i % 2
                            dve.wait_ge(biased.sem, biased.step(n, i + 1))
                            for part in range(2):
                                for c in range(2):
                                    tab = cs[:, part, ds((n * 2 + c) * P, P)].rearrange("p (a n) -> p a n", a=1).broadcast_to([P, B, P])
                                    last = nc.vector.tensor_tensor(
                                        qm[:, i % 2, part, c * B * P:(c + 1) * B * P].rearrange("p (b n) -> p b n", b=B),
                                        qa[:, i % 2, part, c * B * P:(c + 1) * B * P].rearrange("p (b n) -> p b n", b=B),
                                        tab, ALU.mult)
                                last.then_inc(rotated.sem, 1)
                            dve.wait_ge(rotated.sem, rotated.step(n, 2 * (i + 1)))
                            for c in range(2):
                                last = nc.vector.tensor_tensor(
                                    QF[:, a, m, :, ds((n * 2 + c) * P, P)],
                                    qm[:, i % 2, 0, c * B * P:(c + 1) * B * P].rearrange("p (b n) -> p b n", b=B),
                                    qm[:, i % 2, 1, c * B * P:(c + 1) * B * P].rearrange("p (b n) -> p b n", b=B), ALU.add)
                            last.then_inc(summed.sem, 1)
                    for t in range(NC * B):
                        dve.wait_ge(v_ready, t + 1)
                        nc.vector.tensor_tensor(V[:, t // B, t % B, :, 0:AD], bank[4 + t % 2][:, 0:D].rearrange("p (h d) -> p h d", d=AD),
                                                bv[:].rearrange("p (h d) -> p h d", d=AD), ALU.add).then_inc(v_added, 1)

            with nc.Block() as block:
                pieces8 = [(a, m, b) for a in range(2) for m in range(KD) for b in range(B)]

                @block.scalar
                def _(act):
                    for n, (a, m, b) in enumerate(pieces8):
                        nc.scalar.activation(QP[:, 0, a, m, b, :], QF[:, a, m, b, :], ACT.Copy).then_inc(part_cast, 1)
                        if n >= 1:
                            act.wait_ge(rest_taken, 2 * n - 1)
                            a, m, b = pieces8[n - 1]
                            nc.scalar.activation(QP[:, 1, a, m, b, :], QF[:, a, m, b, :], ACT.Copy).then_inc(part_cast, 1)
                    a, m, b = pieces8[-1]
                    act.wait_ge(rest_taken, 2 * len(pieces8) - 1)
                    nc.scalar.activation(QP[:, 1, a, m, b, :], QF[:, a, m, b, :], ACT.Copy).then_inc(part_cast, 1)

                @block.vector
                def _(dve):
                    for n, (a, m, b) in enumerate(pieces8):
                        dve.wait_ge(part_cast, max(2 * n, 1))
                        nc.vector.tensor_tensor(QF[:, a, m, b, :], QF[:, a, m, b, :], QP[:, 0, a, m, b, :], ALU.subtract).then_inc(rest_taken, 1)
                        dve.wait_ge(part_cast, min(2 * n + 3, 2 * len(pieces8)))
                        nc.vector.tensor_tensor(QP[:, 2, a, m, b, :], QF[:, a, m, b, :], QP[:, 1, a, m, b, :], ALU.subtract).then_inc(rest_taken, 1)

        TERMS = ((0, 0), (0, 1), (1, 0), (1, 1), (0, 2), (2, 0))
        MR = 3
        ROWS = MR + len(TERMS) * AD
        units = [(hh, b) for hh in range(2) for b in range(B)]
        NU = len(units)
        qs = sb("qs", [ROWS, 2, B, T], BF16)
        ks = sb("ks", [ROWS, 2, B, T], BF16)
        zrow = sb("zrow", [MR, B, T], BF16)
        mx = sb("mx", [P, NC])
        mrest = sb("mrest", [P, NC])
        mp = sb("mp", [P, MR, NC], BF16)
        rinv = sb("rinv", [P, NC, 1])
        first = [kt * NC - kt * (kt - 1) // 2 for kt in range(NC)]
        PT = sb("PT", [P, NC * (NC + 1) // 2, P])
        AO = sb("AO", [P, NC, B, D])
        pieces = [(kt, i, min(4, NC - i)) for kt in range(NC) for i in range(kt, NC, 4)]
        NPC = len(pieces)
        assert NPC % 3 == 0
        heads_loaded = [sem(f"heads_loaded{i}") for i in range(2)]
        LOADS = 1 + 2 * len(TERMS)
        rows_set = sem("rows_set")
        scored = PerSlot(sem("scored"), NC)
        maxed = PerSlot(sem("maxed"), NC)
        max_split = PerSlot(sem("max_split"), 4)
        max_turned = PerSlot(sem("max_turned"), 1)
        max_copied = PerSlot(sem("max_copied"), 1)
        scored_t = PerSlot(sem("scored_t"), NPC)
        exped = PerSlot(sem("exped"), NPC)
        pv_ready = PerSlot(sem("pv_ready"), 1)
        inverted = PerSlot(sem("inverted"), 1)
        scaled = PerSlot(sem("scaled"), 1)
        with nc.Block() as block:
            @block.sync
            def _(sp):
                for x in (scored, maxed, max_split, max_turned, max_copied, scored_t, exped, pv_ready, inverted, scaled):
                    sp.sem_inc(x.sem, x.n)

            @block.gpsimd
            def _(pool):
                nc.gpsimd.memset(zrow[:], 0.0).then_inc(rows_set, 1)
                nc.gpsimd.memset(ks[0:MR, :, :, :], 1.0).then_inc(rows_set, 1)
        with nc.Block() as block:
            @block.sync
            def _(sp):
                for h in range(AH):
                    if h >= 2:
                        sp.wait_ge(scored_t.sem, scored_t.after(2 * (h - 2) + 1))
                    r = (h % 8) * AD
                    loaded = heads_loaded[h % 2]
                    sp.dma_start(qs[0:MR, h % 2, :, :], zrow[:]).then_inc(loaded, 16)
                    for n, parts in enumerate(TERMS):
                        at = MR + n * AD
                        for a, dst in enumerate((qs, ks)):
                            sp.dma_start(dst[at:at + AD, h % 2, :, :], QP[r:r + AD, parts[a], a, h // 8, :, :]).then_inc(loaded, 16)
                sp.sem_inc(heads_loaded[0], 16 * LOADS)

            @block.tensor
            def _(pe):
                def score(s, u, i, loads=None):
                    hh, b = units[u]
                    if b == 0 and i == 0:
                        pe.wait_ge(heads_loaded[hh], loads)
                    if i == 0:
                        pe.wait_ge(max_copied.sem, max_copied.before(s))
                    pe.wait_ge(maxed.sem, maxed.step(s, i - 1))
                    for g4 in range(i // 4 + 1):
                        cols = min(4, i + 1 - g4 * 4) * P
                        diag = g4 == i // 4
                        bk = bank[2 * (i % 2) + g4]
                        last = nc.tensor.matmul(bk[:, 0:cols], qs[:, hh, b, i * P:(i + 1) * P],
                                                ks[:, hh, b, g4 * 4 * P:g4 * 4 * P + cols], start=True, stop=not diag,
                                                skip_group_check=True)
                        if diag:
                            last = nc.tensor.matmul(bk[:, cols - P:cols], ident16[:], diag16[:], start=False, stop=True,
                                                    skip_group_check=True)
                    last.then_inc(scored.sem, 1)

                def turn_max(s, u):
                    pe.wait_ge(max_split.sem, max_split.after(s))
                    for i in range(NC):
                        last = nc.tensor.matmul(bank[i // 4][0:MR, (i % 4) * P:(i % 4 + 1) * P], mp[:, :, i], ident16[:],
                                                start=True, stop=True)
                    last.then_inc(max_turned.sem, 1)

                def score_t(s, u, kt):
                    hh, b = units[u]
                    if kt == 0:
                        pe.wait_ge(max_copied.sem, max_copied.after(s))
                    for n, (k, i, tiles) in enumerate(pieces):
                        if k != kt:
                            continue
                        pe.wait_ge(exped.sem, exped.step(s, n - 2))
                        bk = bank[4 + n % 3]
                        diag = i == kt
                        last = nc.tensor.matmul(bk[:, 0:tiles * P], ks[:, hh, b, kt * P:(kt + 1) * P],
                                                qs[:, hh, b, i * P:(i + tiles) * P], start=True, stop=not diag,
                                                skip_group_check=True)
                        if diag:
                            last = nc.tensor.matmul(bk[:, 0:P], ident16[:], causal16[:, 0:P], start=False, stop=True,
                                                    skip_group_check=True)
                        last.then_inc(scored_t.sem, 1)

                def pv(s, g, u, i):
                    hh, b = units[u]
                    if i == 0:
                        pe.wait_ge(scaled.sem, scaled.before(s))
                    pe.wait_ge(exped.sem, exped.step(s, 1 + max(n for n, p in enumerate(pieces) if p[0] <= i and p[1] <= i)))
                    for kt in range(i + 1):
                        last = nc.tensor.matmul(bank[7][:, i * (AD + 1):(i + 1) * (AD + 1)], PT[:, first[kt] + i - kt, :],
                                                V[:, kt, b, ds(g * 2 + hh, 1), :].rearrange("p a d -> p (a d)"),
                                                start=(kt == 0), stop=(kt == i), skip_group_check=True)
                    if i == NC - 1:
                        last.then_inc(pv_ready.sem, 1)

                for i in range(NC):
                    score(0, 0, i, 16 * LOADS)
                turn_max(0, 0)
                with pe.Fori(0, AH // 2) as g:
                    for u in range(NU):
                        s = g * NU + u
                        nu = (u + 1) % NU
                        loads = (g + 1 + (u + 1) // NU) * 16 * LOADS
                        for i in range(NC):
                            score(s + 1, nu, i, loads)
                            score_t(s, u, i)
                        for i in range(NC // 2):
                            pv(s, g, u, i)
                        turn_max(s + 1, nu)
                        for i in range(NC // 2, NC):
                            pv(s, g, u, i)

            @block.scalar
            def _(act):
                def copy_max(s, u):
                    hh, b = units[u]
                    act.wait_ge(max_turned.sem, max_turned.after(s))
                    nc.scalar.activation(qs[0:MR, hh, b, :], PS[0:MR, 0:2, :].rearrange("p a n -> p (a n)"), ACT.Copy
                                         ).then_inc(max_copied.sem, 1)

                def exps(s):
                    for n, (kt, i, tiles) in enumerate(pieces):
                        act.wait_ge(scored_t.sem, scored_t.step(s, n + 1))
                        at = first[kt] + i - kt
                        nc.scalar.activation(PT[:, at:at + tiles, :], bank[4 + n % 3][:, 0:tiles * P].rearrange("p (a n) -> p a n", n=P),
                                             ACT.Exp, scale=AD ** -0.5).then_inc(exped.sem, 1)

                copy_max(0, 0)
                with act.Fori(0, AH // 2) as g:
                    for u in range(NU):
                        exps(g * NU + u)
                        copy_max(g * NU + u + 1, (u + 1) % NU)

            @block.vector
            def _(dve):
                def row_max(s, i):
                    dve.wait_ge(scored.sem, scored.step(s, i + 1))
                    nc.vector.reduce_max(mx[:, i:i + 1], PS[:, 2 * (i % 2):2 * (i % 2) + 2, :].rearrange("p a n -> p (a n)")[:, 0:(i + 1) * P],
                                         axis=AX.X).then_inc(maxed.sem, 1)

                def split_max(s):
                    dve.wait_ge(maxed.sem, maxed.after(s))
                    dve.wait_ge(max_turned.sem, max_turned.before(s))
                    nc.vector.tensor_scalar(mp[:, 0, :], mx[:], -1.0, None, ALU.mult).then_inc(max_split.sem, 1)
                    dve.wait_ge(max_split.sem, max_split.step(s, 1))
                    nc.vector.scalar_tensor_tensor(mrest[:], mx[:], -1.0, mp[:, 0, :], ALU.mult, ALU.subtract).then_inc(max_split.sem, 1)
                    dve.wait_ge(max_split.sem, max_split.step(s, 2))
                    nc.vector.tensor_copy(mp[:, 1, :], mrest[:]).then_inc(max_split.sem, 1)
                    dve.wait_ge(max_split.sem, max_split.step(s, 3))
                    nc.vector.tensor_tensor(mp[:, 2, :], mrest[:], mp[:, 1, :], ALU.subtract).then_inc(max_split.sem, 1)

                def divide(s, g, u):
                    hh, b = units[u]
                    o = bank[7][:, 0:NC * (AD + 1)].rearrange("p (i d) -> p i d", d=AD + 1)
                    dve.wait_ge(pv_ready.sem, pv_ready.after(s))
                    nc.vector.reciprocal(rinv[:], o[:, :, AD:AD + 1]).then_inc(inverted.sem, 1)
                    dve.wait_ge(inverted.sem, inverted.after(s))
                    nc.vector.tensor_tensor(AO[:, :, b, ds((g * 2 + hh) * AD, AD)], o[:, :, 0:AD], rinv[:].broadcast_to([P, NC, AD]),
                                            ALU.mult).then_inc(scaled.sem, 1)

                for i in range(NC):
                    row_max(0, i)
                split_max(0)
                with dve.Fori(0, AH // 2) as g:
                    for u in range(NU):
                        s = g * NU + u
                        for i in range(NC):
                            row_max(s + 1, i)
                        split_max(s + 1)
                        divide(s, g, u)

        AOT = sb("AOT", [P, 2, KD, P])
        ao_turned = sem("ao_turned")
        ao_copied = sem("ao_copied")
        d_ready = sem("d_ready")
        d_added = sem("d_added")
        with nc.Block() as block:
            @block.tensor
            def _(pe):
                def turn(t):
                    if t >= 2:
                        pe.wait_ge(ao_copied, t - 1)
                    for k in range(KD):
                        last = nc.tensor.transpose(bank[t % 2][:, k * P:(k + 1) * P], AO[:, t // B, t % B, k * P:(k + 1) * P], ident[:])
                    last.then_inc(ao_turned, 1)

                turn(0)
                for t in range(NC * B):
                    if t + 1 < NC * B:
                        turn(t + 1)
                    pe.wait_ge(ao_copied, t + 1)
                    if t >= 2:
                        pe.wait_ge(d_added, t - 1)
                    for k in range(KD):
                        last = nc.tensor.matmul(bank[2 + t % 2][:, 0:D], AOT[:, t % 2, k, :], Wdn[:, k, :], start=(k == 0), stop=(k == KD - 1))
                    last.then_inc(d_ready, 1)

            @block.scalar
            def _(act):
                for t in range(NC * B):
                    act.wait_ge(ao_turned, t + 1)
                    if t >= 2:
                        act.wait_ge(d_ready, t - 1)
                    nc.scalar.activation(AOT[:, t % 2, :, :], bank[t % 2][:, 0:D].rearrange("p (k n) -> p k n", k=KD), ACT.Copy).then_inc(ao_copied, 1)

            @block.vector
            def _(dve):
                for t in range(NC * B):
                    dve.wait_ge(d_ready, t + 1)
                    nc.vector.tensor_tensor(Yt[:, t // B, t % B, :], bank[2 + t % 2][:, 0:D], bd[:], ALU.add).then_inc(d_added, 1)


def experts(nc, tools, bank, ident, XT, Yt, A_wr, A_tri, A_w1, A_w3, A_w2):
    NB = NC * B // 4
    NE = NSH + E
    NTL = NC * B
    with ExitStack() as ctx:
        def sb(name, shape, dt=F32):
            return tools.sb("ex_" + name, shape, dt, ctx)

        def sem(name):
            return tools.sem("ex_" + name)

        W1 = sb("W1", [P, KD, NE, EH])
        W3 = sb("W3", [P, KD, NE, EH])
        W2 = sb("W2", [P, NE, D])
        w_loaded = sem("w_loaded")
        cw = sb("cw", [P, NTL, E])
        with ExitStack() as ctx2:
            Wr = tools.sb("ex_Wr", [P, KD, E], F32, ctx2)
            tri = tools.sb("ex_tri", [P, E, E], F32, ctx2)
            lgT = tools.sb("ex_lgT", [E, NTL * P], F32, ctx2)
            mx = tools.sb("ex_mx", [P, NTL, 1], F32, ctx2)
            pr = tools.sb("ex_pr", [P, NTL, E], F32, ctx2)
            den = tools.sb("ex_den", [P, NTL, 1], F32, ctx2)
            above = tools.sb("ex_above", [P, NTL, E, E], F32, ctx2)
            equal = tools.sb("ex_equal", [P, NTL, E, E], F32, ctx2)
            rank = tools.sb("ex_rank", [P, NTL, E, 1], F32, ctx2)
            router_loaded = sem("router_loaded")
            logits = sem("logits")
            logits_copied = sem("logits_copied")
            logits_turned = sem("logits_turned")
            exped = sem("exped")
            steps = sem("router_steps")
            with nc.Block() as block:
                @block.sync
                def _(sp):
                    sp.dma_start(Wr[:], A_wr.rearrange("(k p) e -> p k e", p=P)).then_inc(router_loaded, 16)
                    sp.dma_start(tri[:].rearrange("p e f -> p (e f)"), A_tri.partition_broadcast(P)).then_inc(router_loaded, 16)
                    for k in range(KD):
                        sp.dma_start(W1[:, k, :, :], A_w1[:, k * P:(k + 1) * P, :].rearrange("e p h -> p e h")).then_inc(w_loaded, 16)
                        sp.dma_start(W3[:, k, :, :], A_w3[:, k * P:(k + 1) * P, :].rearrange("e p h -> p e h")).then_inc(w_loaded, 16)
                    sp.dma_start(W2[:], A_w2.rearrange("e p d -> p e d")).then_inc(w_loaded, 16)

                @block.tensor
                def _(pe):
                    pe.wait_ge(router_loaded, 32)
                    for n in range(NB):
                        for k in range(KD):
                            last = nc.tensor.matmul(bank[n][0:E, :], Wr[:, k, :], XT[:, k, n * 4 * P:(n + 1) * 4 * P],
                                                    start=(k == 0), stop=(k == KD - 1))
                        last.then_inc(logits, 1)
                    for t in range(NTL):
                        pe.wait_ge(logits_copied, t // 4 + 1)
                        last = nc.tensor.transpose(bank[4][:, t * E:(t + 1) * E], lgT[:, t * P:(t + 1) * P], ident[0:E, 0:E])
                    last.then_inc(logits_turned, 1)

                lg = bank[4][:, 0:NTL * E].rearrange("p (t e) -> p t e", e=E)

                @block.scalar
                def _(act):
                    for n in range(NB):
                        act.wait_ge(logits, n + 1)
                        nc.scalar.activation(lgT[:, n * 4 * P:(n + 1) * 4 * P], bank[n][0:E, :], ACT.Copy).then_inc(logits_copied, 1)
                    act.wait_ge(steps, 2)
                    nc.scalar.activation(pr[:], pr[:], ACT.Exp).then_inc(exped, 1)

                @block.vector
                def _(dve):
                    def step(n, ins):
                        ins.then_inc(steps, 1)
                        dve.wait_ge(steps, n)

                    dve.wait_ge(logits_turned, 1)
                    dve.wait_ge(router_loaded, 32)
                    over_e = [P, NTL, E]
                    pairs = [P, NTL * E, E]
                    flat = "p t e f -> p (t e) f"
                    step(1, nc.vector.tensor_reduce(mx[:, :, 0], lg, AX.X, ALU.max))
                    step(2, nc.vector.tensor_tensor(pr[:], lg, mx[:].broadcast_to(over_e), ALU.subtract))
                    dve.wait_ge(exped, 1)
                    step(3, nc.vector.tensor_reduce(den[:, :, 0], pr[:], AX.X, ALU.add))
                    step(4, nc.vector.reciprocal(den[:], den[:]))
                    step(5, nc.vector.tensor_tensor(pr[:], pr[:], den[:].broadcast_to(over_e), ALU.mult))
                    for t in range(NTL):
                        pf = pr[:, t:t + 1, :].broadcast_to([P, E, E])
                        pe_ = pr[:, t, :].rearrange("p (e a) -> p e a", a=1).broadcast_to([P, E, E])
                        nc.vector.tensor_tensor(above[:, t, :, :], pf, pe_, ALU.is_gt)
                        last = nc.vector.tensor_tensor(equal[:, t, :, :], pf, pe_, ALU.is_equal)
                    step(6, last)
                    step(7, nc.vector.tensor_tensor(equal[:].rearrange("p t e f -> p t (e f)"), equal[:].rearrange("p t e f -> p t (e f)"),
                                                    tri[:].rearrange("p (a e) f -> p a (e f)", a=1).broadcast_to([P, NTL, E * E]), ALU.mult))
                    step(8, nc.vector.tensor_tensor(above[:], above[:], equal[:], ALU.add))
                    step(9, nc.vector.tensor_reduce(rank[:, :, :, 0], above[:], AX.X, ALU.add))
                    step(10, nc.vector.tensor_scalar(rank[:], rank[:], TOPK - 0.5, TOPK / (TOPK + 1.0), ALU.is_lt, ALU.mult))
                    step(11, nc.vector.tensor_tensor(cw[:], pr[:], rank[:, :, :, 0], ALU.mult))
                    step(12, nc.vector.tensor_reduce(den[:, :, 0], cw[:], AX.X, ALU.add))
                    step(13, nc.vector.tensor_scalar(den[:], den[:], (TOPK + 1.0) / TOPK, None, ALU.mult))
                    step(14, nc.vector.reciprocal(den[:], den[:]))
                    step(15, nc.vector.tensor_tensor(cw[:], cw[:], den[:].broadcast_to(over_e), ALU.mult))

        sg = sb("sg", [P, 2, 4 * P])
        gT = sb("gT", [P, 2, 4 * P])
        h_ready = PerSlot(sem("h_ready"), NE)
        silu = PerSlot(sem("silu"), NE)
        g_ready = PerSlot(sem("g_ready"), NE)
        y_ready = PerSlot(sem("y_ready"), NE)
        y_added = PerSlot(sem("y_added"), NE)
        Yv = Yt[:].rearrange("p c b d -> p (c b) d")
        out_banks = lambda e: (4, 5) if e < NSH or e % 2 else (6, 7)
        with nc.Block() as block:
            @block.sync
            def _(sp):
                for x in (h_ready, silu, g_ready, y_ready, y_added):
                    sp.sem_inc(x.sem, x.n)
        with nc.Block() as block:
            @block.tensor
            def _(pe):
                def up(n, e):
                    pe.wait_ge(silu.sem, silu.step(n, e - 1))
                    pe.wait_ge(g_ready.sem, g_ready.step(n, e - 1))
                    for w, bk in ((W1, bank[e % 2]), (W3, bank[2 + e % 2])):
                        for k in range(KD):
                            last = nc.tensor.matmul(bk[:], w[:, k, e, :], XT[:, k, ds(n * 4 * P, 4 * P)], start=(k == 0), stop=(k == KD - 1))
                    last.then_inc(h_ready.sem, 1)

                def down(n, e):
                    pe.wait_ge(g_ready.sem, g_ready.step(n, e + 1))
                    shared = e < NSH
                    pe.wait_ge(y_added.sem, y_added.before(n) if e <= NSH else y_added.step(n, e - 1))
                    for j in range(4):
                        bk = bank[out_banks(e)[j // 2]]
                        last = nc.tensor.matmul(bk[:, (j % 2) * D:(j % 2 + 1) * D], gT[:, e % 2, j * P:(j + 1) * P], W2[:, e, :],
                                                start=(j % 2 == 0) if not shared else (e == 0 and j % 2 == 0),
                                                stop=not shared or e == NSH - 1, skip_group_check=True)
                    last.then_inc(y_ready.sem, 1)

                pe.wait_ge(w_loaded, 16 * (2 * KD + 1))
                with pe.Fori(0, NB) as n:
                    up(n, 0)
                    for e in range(NE):
                        if e + 1 < NE:
                            up(n, e + 1)
                        down(n, e)

            @block.scalar
            def _(act):
                with act.Fori(0, NB) as n:
                    for e in range(NE):
                        act.wait_ge(h_ready.sem, h_ready.step(n, e + 1))
                        act.wait_ge(g_ready.sem, g_ready.step(n, e - 1))
                        nc.scalar.activation(sg[:, e % 2, :], bank[e % 2][:], ACT.Silu).then_inc(silu.sem, 1)

            @block.vector
            def _(dve):
                def gated(n, e):
                    dve.wait_ge(silu.sem, silu.step(n, e + 1))
                    dve.wait_ge(y_ready.sem, y_ready.step(n, e - 1))
                    nc.vector.tensor_tensor(gT[:, e % 2, :], bank[2 + e % 2][:], sg[:, e % 2, :], ALU.mult).then_inc(g_ready.sem, 1)

                def add(n, e):
                    dve.wait_ge(y_ready.sem, y_ready.step(n, e + 1))
                    if e < NSH - 1:
                        dve.sem_inc(y_added.sem, 1)
                        return
                    dve.wait_ge(y_added.sem, y_added.step(n, e))
                    for j in range(4):
                        src = bank[out_banks(e)[j // 2]][:, (j % 2) * D:(j % 2 + 1) * D]
                        y = Yv[:, ds(n * 4 + j, 1), :].rearrange("p a d -> p (a d)")
                        if e == NSH - 1:
                            last = nc.vector.tensor_scalar(y, src, 1.0 / (TOPK + 1), None, ALU.mult)
                        else:
                            last = nc.vector.scalar_tensor_tensor(y, src, cw[:, ds(n * 4 + j, 1), e - NSH], y, ALU.mult, ALU.add)
                    last.then_inc(y_added.sem, 1)

                with dve.Fori(0, NB) as n:
                    gated(n, 0)
                    for e in range(NE):
                        if e + 1 < NE:
                            gated(n, e + 1)
                        add(n, e)


def two_layers(nc, A, out):
    with ExitStack() as ctx:
        tools = Tools(nc, ctx)
        PS = ctx.enter_context(nc.psum_tensor("PS", [P, 8, 512], F32))
        bank = [PS[:, i, :] for i in range(8)]
        X = tools.sb("X", [P, NC, B, D])
        Yt = tools.sb("Yt", [P, NC, B, D])
        ident = tools.sb("ident", [P, P])
        cumsum_mask = tools.sb("cumsum_mask", [P, P])
        level0 = tools.sb("level0", [P, P])
        level0_t = tools.sb("level0_t", [P, P])
        level_masks = tools.sb("level_masks", [P, LEVELS - 1, 64])
        causal = tools.sb("causal", [P, U * P])
        causal16 = tools.sb("causal16", [P, U * P], BF16)
        diag16 = tools.sb("diag16", [P, P], BF16)
        ident16 = tools.sb("ident16", [P, P], BF16)
        ones = tools.sb("ones", [P, P])
        half = tools.sb("half", [P, 1])
        consts_loaded = tools.sem("consts_loaded")
        consts_made = tools.sem("consts_made")

        with nc.Block() as block:
            @block.sync
            def _(sp):
                at = 0
                for t, n in ((ident, P), (cumsum_mask, P), (level0, P), (level0_t, P), (level_masks, 64 * (LEVELS - 1)), (causal, U * P)):
                    dst = t[:].rearrange("p a n -> p (a n)") if t is level_masks else t[:]
                    sp.dma_start(dst, A["masks"][:, at:at + n]).then_inc(consts_loaded, 16)
                    at += n

            @block.vector
            def _(dve):
                nc.vector.memset(ones[:], 1.0)
                nc.vector.memset(half[:], -0.5)
                dve.wait_ge(consts_loaded, 16 * 6)
                nc.vector.tensor_copy(ident16[:], ident[:])
                nc.vector.tensor_copy(causal16[:], causal[:])

            @block.gpsimd
            def _(pool):
                pool.wait_ge(consts_loaded, 16 * 6)
                nc.gpsimd.memset(diag16[:], 0.0).then_inc(consts_made, 1)
                pool.wait_ge(consts_made, 1)
                nc.gpsimd.affine_select(out=diag16[:], in_=diag16[:], compare_op=ALU.is_ge, fill=NEG, base=0,
                                        pattern=[[-1, P]], channel_multiplier=1)

        with ExitStack() as c1:
            Xc = tools.sb("Xc", [P, NC + 1, KD, B, CW], F32, c1)

            def put_chunks(act, c, b, src):
                return nc.scalar.activation(Xc[:, c, :, b, HALO:CW], src, ACT.Copy)

            residual_and_norm(nc, tools, "n0", bank, ident, half, X, None, put_chunks, x_in=A["x"])
            with nc.Block() as block:
                @block.gpsimd
                def _(pool):
                    rows = Xc[:].rearrange("p c k b n -> p c (k b) n")
                    nc.gpsimd.memset(rows[:, 0, :, 0:HALO], 0.0)
                    nc.gpsimd.memset(rows[:, NC, :, 0:HALO], 0.0)
                    nc.gpsimd.tensor_copy(rows[:, 1:NC, :, 0:HALO], rows[:, 0:NC - 1, :, P:CW])
                    nc.gpsimd.tensor_copy(rows[:, NC, :, HALO:CW], rows[:, 0, :, HALO:CW])
            cst = (ident, half, cumsum_mask, ones, ident16, causal16, level0, level0_t, level_masks)
            delta_rule(nc, tools, bank, cst, X, Xc, Yt, A["L0_W_qkv"], A["L0_W_ab"], A["conv_w"], A["A_log"], A["dt_bias"],
                       A["o_norm_w"], A["L0_W_o"])

        with ExitStack() as c1:
            XT = tools.sb("XT", [P, KD, NC * B * P], F32, c1)

            def put_tokens(act, c, b, src):
                t = (c * B + b) * P
                return nc.scalar.activation(XT[:, :, t:t + P], src, ACT.Copy)

            plain = lambda c, b: Yt[:, ds(c, 1), b, :]
            rotated = lambda c, b: Yt2[:, ds(c + 1, 1), b, :]
            with ExitStack() as c2:
                Yt2 = tools.sb("Yt2", [P, NC + 1, B, D], F32, c2)
                with nc.Block() as block:
                    @block.gpsimd
                    def _(pool):
                        nc.gpsimd.tensor_copy(Yt2[:, 0:NC, :, :], Yt[:])
                        nc.gpsimd.tensor_copy(Yt2[:, NC, :, :], Yt[:, 0, :, :])
                residual_and_norm(nc, tools, "n1", bank, ident, half, X, rotated, put_tokens)
            int_ffn(nc, tools, bank, XT, Yt, A["gate_w"], A["gate_s"], A["up_w"], A["up_s"], A["down_w"], A["down_s"])
            residual_and_norm(nc, tools, "n2", bank, ident, half, X, plain, put_tokens)
            attention(nc, tools, PS, bank, ident, ident16, causal16, diag16, XT, Yt, A["at_wq"], A["at_bq"], A["at_cs"], A["at_wv"], A["at_bv"],
                      A["L1_W_dense"], A["L1_b_dense"])
            residual_and_norm(nc, tools, "n3", bank, ident, half, X, plain, put_tokens)
            experts(nc, tools, bank, ident, XT, Yt, A["w_router"], A["tri"], A["w1"], A["w3"], A["w2"])
            residual_and_norm(nc, tools, "n4", bank, ident, half, X, plain, None, store=out)


def constants():
    i = np.arange(P)
    r, c = i[:, None], i[None, :]
    parts = [r == c, r <= c]
    level0 = (r == c) | ((r // 2 == c // 2) & (r > c))
    parts += [level0, level0.T]
    for l in range(1, LEVELS):
        n = 1 << l
        first = i[(i // n) % 2 == 0]
        cc = first[None, :]
        parts.append((r == cc) | ((r // (2 * n) == cc // (2 * n)) & ((r // n) % 2 == 1)))
    masks = np.concatenate([p.astype(np.float32) for p in parts] + [np.where(r > c, np.float32(NEG), np.float32(0))] * U, axis=1)
    tri = (i[None, :E] < i[:E, None]).astype(np.float32).reshape(-1)
    rot = AD // 4
    inv = (np.float32(1) / np.float32(10000.0) ** (np.arange(0, rot, 2, dtype=np.float32) / np.float32(rot))).astype(np.float32)
    ang = np.outer(np.arange(T, dtype=np.float32), inv).astype(np.float32)
    cs = np.zeros((2, AD, T), np.float32)
    cs[0] = 1.0
    for d in range(rot):
        cs[0, d] = np.cos(ang[:, d % 2])
        cs[1, d] = np.sin(ang[:, d % 2]) * (-1.0 if d < rot // 2 else 1.0)
    return masks.astype(np.float32), tri, np.tile(cs, (1, P // AD, 1)).astype(np.float32)


def lay_out(a):
    masks, tri, cs = constants()
    rot = AD // 4
    partner = np.arange(AD)
    partner[:rot] = (partner[:rot] + rot // 2) % rot
    w = a["L1_attn_W_qkv"].reshape(D, AH, 3, AD)
    bias = a["L1_attn_b_qkv"].reshape(AH, 3, AD)
    wq = np.stack([w[:, :, 0, :], w[:, :, 0, partner], w[:, :, 1, :], w[:, :, 1, partner]]).reshape(4, D, AH * AD)
    bq = np.stack([bias[:, 0, :], bias[:, 0, partner], bias[:, 1, :], bias[:, 1, partner]]).reshape(4, KD, P).transpose(2, 0, 1)
    quarters = lambda s: s.reshape(D, NSH, EH).transpose(1, 0, 2)
    return {
        "x": a["L0_attn_hidden_states"], "L0_W_qkv": a["L0_attn_W_qkv"], "L0_W_ab": a["L0_attn_W_ab"],
        "conv_w": a["L0_attn_conv_w"], "A_log": a["L0_attn_A_log"], "dt_bias": a["L0_attn_dt_bias"],
        "o_norm_w": a["L0_attn_o_norm_w"], "L0_W_o": a["L0_attn_W_o"],
        "gate_w": a["L0_ffn_gate_w"].T, "gate_s": a["L0_ffn_gate_scale"].reshape(FI // P, P).T,
        "up_w": a["L0_ffn_up_w"].T, "up_s": a["L0_ffn_up_scale"].reshape(FI // P, P).T,
        "down_w": a["L0_ffn_down_w"].T, "down_s": a["L0_ffn_down_scale"],
        "at_wq": wq, "at_bq": bq, "at_cs": cs, "at_wv": w[:, :, 2, :].reshape(D, AH * AD), "at_bv": bias[:, 2, :].reshape(-1),
        "L1_W_dense": a["L1_attn_W_dense"], "L1_b_dense": a["L1_attn_b_dense"],
        "w_router": a["L1_ffn_w_router"],
        "w1": np.concatenate([quarters(a["L1_ffn_ws1"]), a["L1_ffn_we1"]]),
        "w3": np.concatenate([quarters(a["L1_ffn_ws3"]), a["L1_ffn_we3"]]),
        "w2": np.concatenate([a["L1_ffn_ws2"].reshape(NSH, EH, D), a["L1_ffn_we2"]]),
        "masks": masks, "tri": tri,
    }


def kernel(**inputs):
    import concourse.bacc as _bacc
    from concourse.bass_utils import run_bass_kernel_spmd as _run

    nc = _bacc.Bacc("TRN2", target_bir_lowering=False, num_devices=1)
    arrays, aps = {}, {}
    for name, a in lay_out({k: np.asarray(v) for k, v in inputs.items()}).items():
        a = np.ascontiguousarray(a)
        arrays[f"in_{name}"] = a
        aps[name] = nc.dram_tensor(f"in_{name}", a.shape, mybir.dt.from_np(a.dtype), kind="ExternalInput").ap()
    out = nc.dram_tensor("out_0", (B, T, D), F32, kind="ExternalOutput").ap()
    two_layers(nc, aps, out)
    r = _run(nc, [arrays], core_ids=[0])
    return r.results[0]["out_0"]
```

```python
from contextlib import ExitStack

import numpy as np

import concourse.bass as bass
from concourse import mybir

F32 = mybir.dt.float32
BF16 = mybir.dt.bfloat16
I32 = mybir.dt.int32
ALU = mybir.AluOpType
ACT = mybir.ActivationFunctionType
AX = mybir.AxisListType
ds = bass.ds

P = 128
B, T, D = 2, 1024, 256
NC = T // P
KD = D // P
LN_EPS = 1e-5
H, DK = 16, 128
HP = H // 2
U = 2 * B
TAPS = 4
HALO = TAPS - 1
CW = P + HALO
L2_EPS = 1e-6
KINDS = (1, 0, 2)
LEVELS = 7
SLOTS = HP * NC
FI = 1024
AH, AD = 16, 16
E, EH, TOPK = 16, 128, 4
NSH = 4
NEG = -1e30


class PerSlot:

    def __init__(self, sem, n, lead=1):
        self.sem, self.n, self.lead = sem, n, lead

    def after(self, s):
        return (s + self.lead + 1) * self.n

    def step(self, s, k):
        return (s + self.lead) * self.n + k

    def before(self, s):
        return (s + self.lead) * self.n


class Counter:

    def __init__(self, sem):
        self.sem, self.v = sem, 0

    def bump(self, k=1):
        self.v += k
        return self.sem, k


class Tools:
    def __init__(self, nc, ctx):
        self.nc, self.ctx, self.phase = nc, ctx, []

    def sb(self, name, shape, dt=F32, ctx=None):
        return (ctx or self.ctx).enter_context(self.nc.sbuf_tensor(name, shape, dt))

    def sem(self, name, ctx=None):
        x = (ctx or self.ctx).enter_context(self.nc.semaphore(name))
        if ctx is not None:
            self.phase.append(x)
        return x

    def clear(self):
        with self.nc.Block() as block:
            @block.sync
            def _(sp):
                for x in self.phase:
                    sp.sem_clear(x)
        self.phase = []


def residual_and_norm(nc, tools, tag, bank, ident, half, X, Y, put, x_in=None, store=None, loads_ahead=None):
    DEPTH = 4
    AHEAD = 2
    with ExitStack() as ctx:
        stats = tools.sb(tag + "_stats", [P, NC, B, 6], ctx=ctx)
        mv = tools.sb(tag + "_mv", [P, NC, B, 2], ctx=ctx)
        rstd = tools.sb(tag + "_rstd", [P, NC, B, 1], ctx=ctx)
        stats2 = tools.sb(tag + "_stats2", [P, NC, B, 6], ctx=ctx)
        mv2 = tools.sb(tag + "_mv2", [P, NC, B, 2], ctx=ctx)
        rstd2 = tools.sb(tag + "_rstd2", [P, NC, B, 1], ctx=ctx)
        normed = tools.sb(tag + "_normed", [P, DEPTH, D], ctx=ctx)
        yn = tools.sb(tag + "_yn", [P, NC, B, D], ctx=ctx) if Y else None
        x_loaded = tools.sem(tag + "_x_loaded")
        y_stats = tools.sem(tag + "_y_stats")
        y_aggr = tools.sem(tag + "_y_aggr")
        y_var = tools.sem(tag + "_y_var")
        y_rstd = tools.sem(tag + "_y_rstd")
        y_normed = tools.sem(tag + "_y_normed")
        x_added = tools.sem(tag + "_x_added")
        x_stats = tools.sem(tag + "_x_stats")
        x_aggr = tools.sem(tag + "_x_aggr")
        x_var = tools.sem(tag + "_x_var")
        x_rstd = tools.sem(tag + "_x_rstd")
        x_normed = tools.sem(tag + "_x_normed")
        transposed = tools.sem(tag + "_transposed")
        laid = tools.sem(tag + "_laid")
        stored = tools.sem(tag + "_stored")

        with nc.Block() as block:
            @block.sync
            def _(sp):
                if loads_ahead is not None:
                    loads_ahead(sp)
                if x_in is not None:
                    for b in range(B):
                        sp.dma_start(X[:, :, b, :], x_in[b].rearrange("(c p) d -> p c d", p=P)).then_inc(x_loaded, 16)
                if store is not None:
                    sp.wait_ge(x_added, NC * B)
                    for b in range(B):
                        sp.dma_start(store[b].rearrange("(c p) d -> p c d", p=P), X[:, :, b, :]).then_inc(stored, 16)
                    sp.wait_ge(stored, 16 * B)

            @block.vector
            def _(dve):
                if x_in is not None:
                    dve.wait_ge(x_loaded, 16 * B)
                if Y:
                    for t in range(NC * B):
                        nc.vector.bn_stats(stats[:, t // B, t % B, :], Y(t // B, t % B)).then_inc(y_stats, 1)
                    for t in range(NC * B):
                        dve.wait_ge(y_stats, t + 1)
                        nc.vector.bn_aggr(mv[:, t // B, t % B, :], stats[:, t // B, t % B, :]).then_inc(y_aggr, 1)
                    dve.wait_ge(y_aggr, NC * B)
                    nc.vector.tensor_scalar(rstd[:, :, :, 0], mv[:, :, :, 1], LN_EPS, None, ALU.add).then_inc(y_var, 1)
                    dve.wait_ge(y_rstd, 1)
                for t in range(NC * B + AHEAD):
                    if Y and t < NC * B:
                        c, b = t // B, t % B
                        nc.vector.tensor_scalar(yn[:, c, b, :], Y(c, b), mv[:, c, b, 0:1], rstd[:, c, b, :],
                                                ALU.subtract, ALU.mult).then_inc(y_normed, 1)
                    if put is not None and t >= AHEAD:
                        c, b = (t - AHEAD) // B, (t - AHEAD) % B
                        if Y:
                            dve.wait_ge(x_added, t - AHEAD + 1)
                        nc.vector.bn_stats(stats2[:, c, b, :], X[:, c, b, :]).then_inc(x_stats, 1)
                if put is None:
                    return
                for t in range(NC * B):
                    dve.wait_ge(x_stats, t + 1)
                    nc.vector.bn_aggr(mv2[:, t // B, t % B, :], stats2[:, t // B, t % B, :]).then_inc(x_aggr, 1)
                dve.wait_ge(x_aggr, NC * B)
                nc.vector.tensor_scalar(rstd2[:, :, :, 0], mv2[:, :, :, 1], LN_EPS, None, ALU.add).then_inc(x_var, 1)
                dve.wait_ge(x_rstd, 1)
                for t in range(NC * B):
                    c, b = t // B, t % B
                    if t >= DEPTH:
                        dve.wait_ge(transposed, t - DEPTH + 1)
                    nc.vector.tensor_scalar(normed[:, t % DEPTH, :], X[:, c, b, :], mv2[:, c, b, 0:1], rstd2[:, c, b, :],
                                            ALU.subtract, ALU.mult).then_inc(x_normed, 1)

            @block.gpsimd
            def _(pool):
                if Y:
                    pool.wait_ge(y_var, 1)
                    nc.gpsimd.tensor_tensor(rstd[:, :, :, 0], rstd[:, :, :, 0],
                                            half[:, 0:1].broadcast_to([P, NC * B]).rearrange("p (c b) -> p c b", b=B),
                                            ALU.pow).then_inc(y_rstd, 1)
                    for t in range(NC * B):
                        pool.wait_ge(y_normed, t + 1)
                        nc.gpsimd.tensor_tensor(X[:, t // B, t % B, :], X[:, t // B, t % B, :], yn[:, t // B, t % B, :],
                                                ALU.add).then_inc(x_added, 1)
                if put is None:
                    return
                pool.wait_ge(x_var, 1)
                nc.gpsimd.tensor_tensor(rstd2[:, :, :, 0], rstd2[:, :, :, 0],
                                        half[:, 0:1].broadcast_to([P, NC * B]).rearrange("p (c b) -> p c b", b=B),
                                        ALU.pow).then_inc(x_rstd, 1)

            @block.tensor
            def _(pe):
                if put is None:
                    return
                for c in range(NC):
                    for b in range(B):
                        t = c * B + b
                        pe.wait_ge(x_normed, t + 1)
                        if t >= DEPTH:
                            pe.wait_ge(laid, t - DEPTH + 1)
                        for k in range(KD):
                            last = nc.tensor.transpose(bank[t % DEPTH][:, k * P:(k + 1) * P], normed[:, t % DEPTH, k * P:(k + 1) * P],
                                                       ident[:])
                        last.then_inc(transposed, 1)

            @block.scalar
            def _(act):
                if put is None:
                    return
                for c in range(NC):
                    for b in range(B):
                        t = c * B + b
                        act.wait_ge(transposed, t + 1)
                        put(act, c, b, bank[t % DEPTH][:, 0:KD * P].rearrange("p (k n) -> p k n", k=KD)).then_inc(laid, 1)


def delta_rule(nc, tools, bank, cst, X, Xc, Acc, A_qkv, A_ab, A_conv, A_alog, A_dt, A_onorm, A_wo):
    ident, half, cumsum_mask, ones, ident16, causal16, level0, level0_t, level_masks = cst
    with ExitStack() as ctx:
        def sb(name, shape, dt=F32):
            return tools.sb("dr_" + name, shape, dt, ctx)

        def sem(name):
            return tools.sem("dr_" + name, ctx)

        Wab = sb("Wab", [P, KD, 2 * H])
        alog = sb("alog", [P, H])
        dtb = sb("dtb", [P, H])
        onorm = sb("onorm", [P, 1])
        z = sb("z", [P, NC * B, H])
        absz = sb("absz", [P, NC * B, H])
        g_all = sb("g_all", [P, NC * B, H])
        nG = sb("nG", [P, NC * B, H])
        eG = sb("eG", [P, NC * B, H])
        eGl = sb("eGl", [P, NC * B, H])
        beta = sb("beta", [P, NC * B, H])
        vecF_all = sb("vecF_all", [P, SLOTS + 1, 3, U])
        vecB_all = sb("vecB_all", [P, SLOTS + 1, 3, U])
        ab_loaded = sem("ab_loaded")
        ab_ready = sem("ab_ready")
        sums_ready = sem("sums_ready")
        alog_exp = sem("alog_exp")
        abs_steps = sem("abs_steps")
        soft_exp = sem("soft_exp")
        soft_ln = sem("soft_ln")
        g_steps = sem("g_steps")
        beta_exp = sem("beta_exp")
        beta_steps = sem("beta_steps")
        G_neg = sem("G_neg")
        G_exp = sem("G_exp")
        firsts_cleared = sem("firsts_cleared")
        spread_done = sem("spread_done")

        with nc.Block() as block:
            @block.sync
            def _(sp):
                sp.dma_start(Wab[:], A_ab[:, 0:2 * H].rearrange("(k p) n -> p k n", p=P)).then_inc(ab_loaded, 16)
                sp.dma_start(alog[:], A_alog.partition_broadcast(P)).then_inc(ab_loaded, 16)
                sp.dma_start(dtb[:], A_dt.partition_broadcast(P)).then_inc(ab_loaded, 16)
                sp.dma_start(onorm[:], A_onorm.rearrange("(p a) -> p a", a=1)).then_inc(ab_loaded, 16)

            @block.tensor
            def _(pe):
                pe.wait_ge(ab_loaded, 64)
                for c in range(NC):
                    for b in range(B):
                        t = (c * B + b) * 2 * H
                        for k in range(KD):
                            last = nc.tensor.matmul(bank[0][:, t:t + 2 * H], Xc[:, c, k, b, HALO:CW], Wab[:, k, :],
                                                    start=(t == 0 and k == 0), stop=(k == KD - 1), skip_group_check=True)
                last.then_inc(ab_ready, 1)
                pe.wait_ge(g_steps, 3)
                gf = g_all[:].rearrange("p t h -> p (t h)")
                nc.tensor.matmul(bank[1][:, 0:NC * B * H], cumsum_mask[:], gf, start=True, stop=True).then_inc(sums_ready, 1)
                nc.tensor.matmul(bank[2][:, 0:NC * B * H], ones[:], gf, start=True, stop=True).then_inc(sums_ready, 1)

            ab = bank[0][:, :].rearrange("p (t n) -> p t n", n=2 * H)
            running = bank[1][:, 0:NC * B * H].rearrange("p (t h) -> p t h", h=H)
            whole = bank[2][:, 0:NC * B * H].rearrange("p (t h) -> p t h", h=H)

            @block.scalar
            def _(act):
                act.wait_ge(ab_loaded, 64)
                nc.scalar.activation(alog[:], alog[:], ACT.Exp).then_inc(alog_exp, 1)
                act.wait_ge(abs_steps, 3)
                nc.scalar.activation(absz[:], absz[:], ACT.Exp).then_inc(soft_exp, 1)
                nc.scalar.activation(beta[:], ab[:, :, H:2 * H], ACT.Exp, scale=-1.0).then_inc(beta_exp, 1)
                act.wait_ge(soft_exp, 1)
                nc.scalar.activation(absz[:], absz[:], ACT.Ln, bias=1.0).then_inc(soft_ln, 1)
                act.wait_ge(sums_ready, 2)
                act.wait_ge(G_neg, 1)
                nc.scalar.activation(eG[:], running, ACT.Exp).then_inc(G_exp, 1)
                nc.scalar.activation(eGl[:], whole, ACT.Exp).then_inc(G_exp, 1)

            @block.vector
            def _(dve):
                dve.wait_ge(ab_ready, 1)
                dve.wait_ge(alog_exp, 1)
                dtb_all = dtb[:].rearrange("p (a h) -> p a h", a=1).broadcast_to([P, NC * B, H])
                alog_all = alog[:].rearrange("p (a h) -> p a h", a=1).broadcast_to([P, NC * B, H])
                nc.vector.tensor_tensor(z[:], ab[:, :, 0:H], dtb_all, ALU.add).then_inc(abs_steps, 1)
                dve.wait_ge(abs_steps, 1)
                nc.vector.tensor_scalar(absz[:], z[:], -1.0, None, ALU.mult).then_inc(abs_steps, 1)
                dve.wait_ge(abs_steps, 2)
                nc.vector.tensor_tensor(absz[:], z[:], absz[:], ALU.min).then_inc(abs_steps, 1)
                dve.wait_ge(soft_ln, 1)
                nc.vector.scalar_tensor_tensor(g_all[:], z[:], 0.0, absz[:], ALU.max, ALU.add).then_inc(g_steps, 1)
                dve.wait_ge(g_steps, 1)
                nc.vector.tensor_tensor(g_all[:], g_all[:], alog_all, ALU.mult).then_inc(g_steps, 1)
                dve.wait_ge(g_steps, 2)
                nc.vector.tensor_scalar(g_all[:], g_all[:], -1.0, None, ALU.mult).then_inc(g_steps, 1)
                dve.wait_ge(beta_exp, 1)
                nc.vector.tensor_scalar(beta[:], beta[:], 1.0, None, ALU.add).then_inc(beta_steps, 1)
                dve.wait_ge(beta_steps, 1)
                nc.vector.reciprocal(beta[:], beta[:]).then_inc(beta_steps, 1)
                dve.wait_ge(beta_steps, 2)
                nc.vector.tensor_scalar(beta[:], beta[:], -2.0, None, ALU.mult).then_inc(beta_steps, 1)
                dve.wait_ge(sums_ready, 1)
                nc.vector.tensor_scalar(nG[:], running, -1.0, None, ALU.mult).then_inc(G_neg, 1)
                dve.wait_ge(G_exp, 2)
                nc.vector.memset(eG[:, 0:B, :], 0.0).then_inc(firsts_cleared, 1)
                nc.vector.memset(eGl[:, 0:B, :], 0.0).then_inc(firsts_cleared, 1)
                nc.vector.memset(vecB_all[:, 0, :, :], 0.0).then_inc(spread_done, 1)
                nc.vector.memset(vecF_all[:, SLOTS, :, :], 0.0).then_inc(spread_done, 1)

                def spread(dst, src):
                    for b in range(B):
                        for hh in range(2):
                            nc.vector.tensor_copy(
                                dst[:, :, 2 * b + hh].rearrange("p (q c) -> p q c", c=NC),
                                src[:].rearrange("p (c b) h -> p b h c", b=B)[:, b, hh::2, :]).then_inc(spread_done, 1)

                dve.wait_ge(firsts_cleared, 2)
                dve.wait_ge(beta_steps, 3)
                dve.wait_ge(G_neg, 1)
                spread(vecF_all[:, :SLOTS, 0, :], beta)
                spread(vecF_all[:, :SLOTS, 1, :], g_all)
                spread(vecF_all[:, :SLOTS, 2, :], nG)
                spread(vecB_all[:, 1:, 1, :], eG)
                spread(vecB_all[:, 1:, 2, :], eGl)
                dve.wait_ge(spread_done, 2 + 5 * U)
                nc.vector.tensor_scalar(vecB_all[:, 1:, 0, :], vecB_all[:, 1:, 1, :], -1.0, None,
                                        ALU.mult).then_inc(spread_done, 1)

        Wp = sb("Wp", [P, KD, 3, 2, P])
        Wg = sb("Wg", [P, KD, 2, P])
        Wo = sb("Wo", [P, 2, D])
        cw = sb("cw", [P, 2, 3, TAPS])
        xc = sb("xc", [P, KD, B, CW])
        xg = sb("xg", [P, KD, B, P])
        conv = sb("conv", [P, 3, U, P])
        vecF = sb("vecF", [P, 3, U])
        vecB = sb("vecB", [P, 3, U])
        QK = sb("QK", [P, 2, 2, U, P])
        Vt = sb("Vt", [P, U, P])
        QKsq = sb("QKsq", [P, 2, U, P])
        Ktok = sb("Ktok", [P, 2, U, P])
        Vn = sb("Vn", [P, 2, U, P])
        gate = sb("gate", [P, U, P])
        ss = sb("ss", [P, 2 * U])
        rs = sb("rs", [P, 2 * U])
        nk = sb("nk", [P, U])
        rk2 = sb("rk2", [P, U])
        negc = sb("negc", [P, U])
        w = sb("w", [P, 2, U])
        rq = sb("rq", [P, 2, U])
        Ex = sb("Ex", [P, U, P])
        AM = sb("AM", [P, 2, U, 2, P])
        Tm = sb("Tm", [P, U, P])
        Xm = sb("Xm", [P, 2, U, P])
        Lv = sb("Lv", [P, LEVELS - 1, U, P])
        RHS = sb("RHS", [P, U, P])
        Y = sb("Y", [P, U, P])
        Yw = sb("Yw", [P, U, P])
        QSg = sb("QSg", [P, U, P])
        O = sb("O", [P, U, P])
        Z = sb("Z", [P, U, P])
        Zsq = sb("Zsq", [P, U, P])
        ssz = sb("ssz", [P, U])
        f1 = sb("f1", [P, U])
        f2 = sb("f2", [P, U])
        f3 = sb("f3", [P, U])
        f4 = sb("f4", [P, U])
        f = sb("f", [P, U])
        Zf = sb("Zf", [P, U, P])
        ZT = sb("ZT", [P, U, P])
        S = sb("S", [P, U, P])
        half_u = half[:, 0:1].broadcast_to([P, 2 * U])

        credited = []

        def per_slot(name, n, first):
            x = PerSlot(sem(name), n, lead=2)
            if first > -2:
                credited.append((x.sem, (first + 2) * n))
            return x

        xc_in = per_slot("xc_in", 1, -2)
        W_ok = per_slot("W_ok", 1, -2)
        W_dma = sem("W_dma")
        projected = per_slot("projected", 6, -2)
        convolved = per_slot("convolved", 6, -2)
        taps = per_slot("taps", 6 * (TAPS - 1), -2)
        vecF_in = per_slot("vecF_in", 1, -1)
        qk_silu = per_slot("qk_silu", 1, -1)
        v_silu = per_slot("v_silu", 1, -1)
        k_turned = per_slot("k_turned", 1, -1)
        k_copied = per_slot("k_copied", 1, -1)
        v_turned = per_slot("v_turned", 1, -1)
        v_scaled = per_slot("v_scaled", 1, -1)
        qk_squared = per_slot("qk_squared", 1, -1)
        ss_ready = per_slot("ss_ready", 1, -1)
        ss_copied = per_slot("ss_copied", 1, -1)
        rs_ready = per_slot("rs_ready", 1, -1)
        nk_ready = per_slot("nk_ready", 1, -1)
        rk2_ready = per_slot("rk2_ready", 1, -1)
        c_ready = per_slot("c_ready", 1, -1)
        kq_ready = per_slot("kq_ready", 2, -1)
        decay_ready = per_slot("decay_ready", 1, -1)
        exp_ready = per_slot("exp_ready", 1, -1)
        am_ready = per_slot("am_ready", U, -1)
        diag_filled = per_slot("diag_filled", 1, -1)
        x0_ready = per_slot("x0_ready", 1, -1)
        w_ready = per_slot("w_ready", 1, -1)
        rq_kept = per_slot("rq_kept", 1, -1)
        at_ready = per_slot("at_ready", 2 * LEVELS, 0)
        masked = per_slot("masked", 2 * LEVELS, 0)
        tx_ready = per_slot("tx_ready", 2 * (LEVELS - 1), 0)
        tx_copied = per_slot("tx_copied", 2 * (LEVELS - 1), 0)
        xg_in = per_slot("xg_in", 1, 0)
        Wg_dma = sem("Wg_dma")
        Wg_ok = per_slot("Wg_ok", 1, 0)
        gate_projected = per_slot("gate_projected", 1, 0)
        vecB_in = per_slot("vecB_in", 1, 0)
        Wo_dma = sem("Wo_dma")
        Wo_ok = per_slot("Wo_ok", 1, 0)
        gate_silu = per_slot("gate_silu", 1, 0)
        ks_ready = per_slot("ks_ready", 1, 0)
        qs_ready = per_slot("qs_ready", 1, 0)
        rhs_ready = per_slot("rhs_ready", U, 0)
        qs_scaled = per_slot("qs_scaled", 1, 0)
        y_ready = per_slot("y_ready", 1, 0)
        y_copied = per_slot("y_copied", 1, 0)
        my_ready = per_slot("my_ready", 1, 0)
        yw_ready = per_slot("yw_ready", 1, 0)
        su_ready = per_slot("su_ready", 1, 0)
        s_updated = per_slot("s_updated", 1, 0)
        o_ready = per_slot("o_ready", 1, 0)
        z_ready = per_slot("z_ready", 1, 0)
        z_squared = per_slot("z_squared", 1, 0)
        f_steps = per_slot("f_steps", 5, 0)
        z_scaled = per_slot("z_scaled", 1, 0)
        z_turned = per_slot("z_turned", 1, 0)
        zt_copied = per_slot("zt_copied", 1, 0)
        out_ready = per_slot("out_ready", 1, 0)
        out_added = per_slot("out_added", 1, 0)
        cleared = sem("cleared")
        settles = sem("settles")

        grp = lambda t, gi: t[:, 2 * gi:2 * gi + 2]

        def halves(ap, n):
            v = ap.rearrange("p u (m two n) -> p u m two n", two=2, n=n)
            return v[:, :, :, 0, :], v[:, :, :, 1, :]

        with nc.Block() as block:
            @block.gpsimd
            def _(pool):
                for t in (QK, Vn, Xm, AM, Ktok, w, rq):
                    nc.gpsimd.memset(t[:, 1], 0.0)
                for t in (S, vecB):
                    nc.gpsimd.memset(t[:], 0.0)
                nc.gpsimd.memset(Acc[:], 0.0)
                for l in range(LEVELS - 1):
                    nc.gpsimd.tensor_copy(Lv[:, l, :, :], ident[:].rearrange("p (a n) -> p a n", a=1).broadcast_to([P, U, P]))
                nc.gpsimd.memset(Wo[:], 0.0).then_inc(cleared, 1)

            @block.sync
            def _(sp):
                for x, v in credited:
                    sp.sem_inc(x, v)
                sp.sem_inc(Wo_ok.sem, 1)

        with nc.Block() as block:
            @block.sync
            def _(sp):
                def load_pair(hp):
                    for k in range(KD):
                        for kind, t in enumerate(KINDS):
                            sp.dma_start(Wp[:, k, kind, :, :], A_qkv[k * P:(k + 1) * P, ds(t * H * DK + hp * 2 * DK, 2 * DK)]
                                         .rearrange("p (h n) -> p h n", h=2)).then_inc(W_dma, 16)
                    for kind, t in enumerate(KINDS):
                        for hh in range(2):
                            sp.dma_start(cw[:, hh, kind, :], A_conv[ds(t * H * DK + (hp * 2 + hh) * DK, DK), :]).then_inc(W_dma, 16)

                def load_gate_and_out(q):
                    sp.wait_ge(gate_projected.sem, gate_projected.before(q * NC))
                    for k in range(KD):
                        sp.dma_start(Wg[:, k, :, :], A_ab[k * P:(k + 1) * P, ds(2 * H + q * 2 * DK, 2 * DK)]
                                     .rearrange("p (h n) -> p h n", h=2)).then_inc(Wg_dma, 16)
                    sp.wait_ge(Wg_dma, (q + 1) * 16 * KD)
                    sp.sem_inc(Wg_ok.sem, NC)
                    sp.wait_ge(out_ready.sem, out_ready.after(q * NC))
                    sp.dma_start(Wo[:], A_wo[ds(q * 2 * DK, 2 * DK), :].rearrange("(h p) n -> p h n", p=P)).then_inc(Wo_dma, 16)
                    sp.wait_ge(Wo_dma, (q + 1) * 16)
                    sp.sem_inc(Wo_ok.sem, NC)

                LOADS = 3 * KD + 6
                load_pair(0)
                sp.wait_ge(W_dma, 16 * LOADS)
                sp.sem_inc(W_ok.sem, NC)
                with sp.Fori(0, HP - 1) as q:
                    load_gate_and_out(q)
                    last = q * NC + NC - 3
                    sp.wait_ge(projected.sem, projected.after(last))
                    sp.wait_ge(convolved.sem, convolved.after(last))
                    load_pair(q + 1)
                    sp.wait_ge(W_dma, (q + 2) * 16 * LOADS)
                    sp.sem_inc(W_ok.sem, NC)
                sp.sem_inc(W_ok.sem, 2)
                load_gate_and_out(HP - 1)

            @block.gpsimd
            def _(pool):
                def settled():
                    pool.sem_inc(settles, 1)

                def stage_x(s, c):
                    pool.wait_ge(projected.sem, projected.before(s))
                    settled()
                    nc.gpsimd.tensor_copy(xc[:].rearrange("p k b n -> p (k b n)"),
                                          Xc[:, ds(c, 1), :, :, :].rearrange("p a k b n -> p (a k b n)")
                                          ).then_inc(xc_in.sem, 1)

                def stage_gate(s, c):
                    pool.wait_ge(gate_projected.sem, gate_projected.before(s))
                    settled()
                    nc.gpsimd.tensor_copy(xg[:].rearrange("p k b n -> p (k b) n"),
                                          Xc[:, ds(c, 1), :, :, HALO:CW].rearrange("p a k b n -> p (a k b) n")
                                          ).then_inc(xg_in.sem, 1)

                def stage_back(s):
                    pool.wait_ge(rhs_ready.sem, rhs_ready.before(s))
                    pool.wait_ge(qs_scaled.sem, qs_scaled.before(s))
                    pool.wait_ge(s_updated.sem, s_updated.before(s))
                    settled()
                    nc.gpsimd.tensor_copy(vecB[:], vecB_all[:, ds(s, 1), :, :].rearrange("p a v u -> p (a v) u")
                                          ).then_inc(vecB_in.sem, 1)

                def stage_front(s):
                    pool.wait_ge(exp_ready.sem, exp_ready.before(s))
                    pool.wait_ge(decay_ready.sem, decay_ready.before(s))
                    settled()
                    nc.gpsimd.tensor_copy(vecF[:], vecF_all[:, ds(s + 1, 1), :, :].rearrange("p a v u -> p (a v) u")
                                          ).then_inc(vecF_in.sem, 1)

                def norms(s, par):
                    pool.wait_ge(qk_silu.sem, qk_silu.after(s))
                    pool.wait_ge(ss_ready.sem, ss_ready.before(s))
                    nc.gpsimd.tensor_tensor(QKsq[:], QK[:, par], QK[:, par], ALU.mult).then_inc(qk_squared.sem, 1)
                    pool.wait_ge(ss_copied.sem, ss_copied.after(s))
                    nc.gpsimd.tensor_tensor(rs[:], ss[:], half_u, ALU.pow).then_inc(rs_ready.sem, 1)
                    pool.wait_ge(rs_ready.sem, rs_ready.after(s))
                    pool.wait_ge(v_scaled.sem, v_scaled.before(s))
                    nc.gpsimd.tensor_tensor(nk[:], ss[:, 0:U], rs[:, 0:U], ALU.mult).then_inc(nk_ready.sem, 1)
                    nc.gpsimd.tensor_tensor(rk2[:], rs[:, 0:U], rs[:, 0:U], ALU.mult).then_inc(rk2_ready.sem, 1)
                    pool.wait_ge(rk2_ready.sem, rk2_ready.after(s))
                    pool.wait_ge(am_ready.sem, am_ready.before(s))
                    pool.wait_ge(vecF_in.sem, vecF_in.after(s))
                    nc.gpsimd.tensor_tensor(negc[:], rk2[:], vecF[:, 0, :], ALU.mult).then_inc(c_ready.sem, 1)

                def weights(s, par):
                    pool.wait_ge(exp_ready.sem, exp_ready.after(s))
                    pool.wait_ge(c_ready.sem, c_ready.after(s))
                    pool.wait_ge(yw_ready.sem, yw_ready.after(s))
                    nc.gpsimd.tensor_tensor(w[:, par], Ex[:, :, P - 1], negc[:], ALU.mult).then_inc(w_ready.sem, 1)

                def starts(s, par):
                    pool.wait_ge(am_ready.sem, am_ready.after(s))
                    settled()
                    nc.gpsimd.affine_select(out=AM[:, par, :, 0, :], in_=AM[:, par, :, 0, :], compare_op=ALU.not_equal, fill=1.0,
                                            base=0, pattern=[[0, U], [-1, P]], channel_multiplier=1
                                            ).then_inc(diag_filled.sem, 1)
                    pool.wait_ge(diag_filled.sem, diag_filled.after(s))
                    pool.wait_ge(y_ready.sem, y_ready.after(s))
                    nc.gpsimd.tensor_tensor(Xm[:, par], AM[:, par, :, 0, :],
                                            level0_t[:].rearrange("p (a n) -> p a n", a=1).broadcast_to([P, U, P]),
                                            ALU.mult).then_inc(x0_ready.sem, 1)

                def keep_rq(s, par):
                    pool.wait_ge(rs_ready.sem, rs_ready.after(s))
                    pool.wait_ge(f_steps.sem, f_steps.after(s))
                    settled()
                    nc.gpsimd.tensor_copy(rq[:, par], rs[:, U:2 * U]).then_inc(rq_kept.sem, 1)

                def out_factors(s, par):
                    pool.wait_ge(z_squared.sem, z_squared.after(s))
                    pool.wait_ge(rq_kept.sem, rq_kept.before(s))
                    pool.wait_ge(z_scaled.sem, z_scaled.before(s))
                    nc.gpsimd.tensor_tensor(f1[:], ssz[:], rq[:, par], ALU.mult).then_inc(f_steps.sem, 1)
                    pool.wait_ge(f_steps.sem, f_steps.step(s, 1))
                    nc.gpsimd.tensor_tensor(f2[:], f1[:], rq[:, par], ALU.mult).then_inc(f_steps.sem, 1)
                    pool.wait_ge(f_steps.sem, f_steps.step(s, 2))
                    settled()
                    nc.gpsimd.tensor_scalar(f3[:], f2[:], 1.0 / DK, LN_EPS * DK, ALU.mult, ALU.add).then_inc(f_steps.sem, 1)
                    pool.wait_ge(f_steps.sem, f_steps.step(s, 3))
                    nc.gpsimd.tensor_tensor(f4[:], f3[:], half_u[:, 0:U], ALU.pow).then_inc(f_steps.sem, 1)
                    pool.wait_ge(f_steps.sem, f_steps.step(s, 4))
                    nc.gpsimd.tensor_tensor(f[:], f4[:], rq[:, par], ALU.mult).then_inc(f_steps.sem, 1)

                stage_x(-2, 0)
                stage_front(-1)
                stage_x(-1, 1)
                norms(-1, 0)
                weights(-1, 0)
                starts(-1, 0)
                keep_rq(-1, 0)
                with pool.Fori(0, HP) as q:
                    with pool.Fori(0, NC // 2) as cc:
                        for par in range(2):
                            c = cc * 2 + par
                            s = q * NC + c
                            other = 1 - par
                            stage_back(s)
                            stage_front(s)
                            stage_x(s, c + 2)
                            stage_gate(s, c)
                            norms(s, other)
                            weights(s, other)
                            out_factors(s, other)
                            starts(s, other)
                            keep_rq(s, other)
                stage_back(SLOTS)
                out_factors(SLOTS, 1)

            @block.scalar
            def _(act):
                def gate_to_silu(s):
                    act.wait_ge(gate_projected.sem, gate_projected.before(s))
                    act.wait_ge(v_scaled.sem, v_scaled.before(s))
                    act.wait_ge(z_ready.sem, z_ready.before(s))
                    nc.scalar.activation(gate[:], bank[4][:].rearrange("p (u n) -> p u n", u=U), ACT.Silu).then_inc(gate_silu.sem, 1)

                def qkv_to_silu(s, par):
                    act.wait_ge(convolved.sem, convolved.before(s))
                    act.wait_ge(qs_ready.sem, qs_ready.after(s))
                    nc.scalar.activation(QK[:, par], conv[:, 0:2, :, :], ACT.Silu).then_inc(qk_silu.sem, 1)
                    act.wait_ge(v_turned.sem, v_turned.before(s))
                    nc.scalar.activation(Vt[:], conv[:, 2, :, :], ACT.Silu).then_inc(v_silu.sem, 1)

                def exp_decays(s):
                    act.wait_ge(decay_ready.sem, decay_ready.after(s))
                    act.wait_ge(w_ready.sem, w_ready.before(s))
                    for u in range(U):
                        last = nc.scalar.activation(Ex[:, u, :], bank[0][:, u * P:(u + 1) * P], ACT.Exp,
                                                    bias=vecF[:, 2, u:u + 1])
                    last.then_inc(exp_ready.sem, 1)

                def copy_k(s, par):
                    act.wait_ge(k_turned.sem, k_turned.after(s))
                    act.wait_ge(su_ready.sem, su_ready.after(s))
                    nc.scalar.activation(Ktok[:, par], bank[7][:].rearrange("p (u n) -> p u n", u=U), ACT.Copy
                                         ).then_inc(k_copied.sem, 1)

                def scale_qs(s):
                    act.wait_ge(qs_ready.sem, qs_ready.after(s))
                    act.wait_ge(vecB_in.sem, vecB_in.after(s))
                    act.wait_ge(o_ready.sem, o_ready.before(s))
                    for u in range(U):
                        last = nc.scalar.activation(QSg[:, u, :], bank[6][:, u * P:(u + 1) * P], ACT.Copy,
                                                    scale=vecB[:, 1, u:u + 1])
                    last.then_inc(qs_scaled.sem, 1)

                def copy_y(s):
                    act.wait_ge(y_ready.sem, y_ready.after(s))
                    act.wait_ge(my_ready.sem, my_ready.before(s))
                    act.wait_ge(yw_ready.sem, yw_ready.before(s))
                    nc.scalar.activation(Y[:], bank[5][:].rearrange("p (u n) -> p u n", u=U), ACT.Copy).then_inc(y_copied.sem, 1)

                def square_z(s):
                    act.wait_ge(z_ready.sem, z_ready.after(s))
                    act.wait_ge(f_steps.sem, f_steps.before(s))
                    for u in range(U):
                        last = nc.scalar.activation(Zsq[:, u, :], Z[:, u, :], ACT.Square, accum_out=ssz[:, u:u + 1])
                    last.then_inc(z_squared.sem, 1)

                def scale_z(s):
                    act.wait_ge(f_steps.sem, f_steps.after(s))
                    act.wait_ge(z_turned.sem, z_turned.before(s))
                    for u in range(U):
                        last = nc.scalar.activation(Zf[:, u, :], Z[:, u, :], ACT.Copy, scale=f[:, u:u + 1])
                    last.then_inc(z_scaled.sem, 1)

                def copy_zt(s):
                    act.wait_ge(z_turned.sem, z_turned.after(s))
                    act.wait_ge(out_ready.sem, out_ready.before(s))
                    nc.scalar.activation(ZT[:], bank[7][:].rearrange("p (u n) -> p u n", u=U), ACT.Copy,
                                         scale=onorm[:, 0:1]).then_inc(zt_copied.sem, 1)

                def copy_level(s, par, l):
                    n = 1 << l
                    for gi in range(2):
                        act.wait_ge(tx_ready.sem, tx_ready.step(s, 2 * (l - 1) + gi + 1))
                        b = bank[2 + gi]
                        t1, _ = halves(grp(Tm, gi), n)
                        _, x2 = halves(grp(Xm[:, par], gi), n)
                        if l < LEVELS - 1:
                            nc.scalar.activation(t1, b[:, 128:256].rearrange("p (u m n) -> p u m n", u=2, n=n), ACT.Copy)
                        nc.scalar.activation(x2, b[:, 256:384].rearrange("p (u m n) -> p u m n", u=2, n=n), ACT.Copy
                                             ).then_inc(tx_copied.sem, 1)

                qkv_to_silu(-1, 0)
                exp_decays(-1)
                copy_k(-1, 0)
                with act.Fori(0, HP) as q:
                    with act.Fori(0, NC // 2) as cc:
                        for par in range(2):
                            s = q * NC + cc * 2 + par
                            other = 1 - par
                            gate_to_silu(s)
                            qkv_to_silu(s, other)
                            scale_qs(s)
                            copy_level(s, par, 1)
                            copy_y(s)
                            exp_decays(s)
                            copy_level(s, par, 2)
                            copy_k(s, other)
                            copy_level(s, par, 3)
                            square_z(s)
                            copy_level(s, par, 4)
                            scale_z(s)
                            copy_level(s, par, 5)
                            copy_zt(s)
                            copy_level(s, par, 6)
                s = SLOTS
                gate_to_silu(s)
                scale_qs(s)
                copy_y(s)
                square_z(s)
                scale_z(s)
                copy_zt(s)

            @block.vector
            def _(dve):
                def convolve(s, i):
                    kind, hh = i // 2, i % 2
                    dve.wait_ge(projected.sem, projected.step(s, i + 1))
                    if i == 0:
                        dve.wait_ge(W_ok.sem, W_ok.after(s))
                        dve.wait_ge(qk_silu.sem, qk_silu.after(s))
                        dve.wait_ge(v_silu.sem, v_silu.after(s))
                    src = bank[i % 2][:, 0:B * CW].rearrange("p (b n) -> p b n", b=B)
                    out = conv[:, kind, hh::2, :]
                    n = (TAPS - 1) * i
                    nc.vector.tensor_scalar(out, src[:, :, 0:P], cw[:, hh, kind, 0:1], None, ALU.mult).then_inc(taps.sem, 1)
                    for j in range(1, TAPS):
                        dve.wait_ge(taps.sem, taps.step(s, n + j))
                        ins = nc.vector.scalar_tensor_tensor(out, src[:, :, j:j + P], cw[:, hh, kind, j:j + 1], out,
                                                             ALU.mult, ALU.add)
                        ins.then_inc((taps if j < TAPS - 1 else convolved).sem, 1)

                def right_sides(s, par):
                    dve.wait_ge(ks_ready.sem, ks_ready.after(s))
                    dve.wait_ge(vecB_in.sem, vecB_in.after(s))
                    dve.wait_ge(v_scaled.sem, v_scaled.before(s))
                    for u in range(U):
                        nc.vector.scalar_tensor_tensor(RHS[:, u, :], bank[5][:, u * P:(u + 1) * P], vecB[:, 0, u:u + 1],
                                                       Vn[:, par, u, :], ALU.mult, ALU.add).then_inc(rhs_ready.sem, 1)

                def weigh_y(s, par):
                    dve.wait_ge(y_copied.sem, y_copied.after(s))
                    dve.wait_ge(w_ready.sem, w_ready.before(s))
                    nc.vector.tensor_tensor(Yw[:], Y[:], w[:, par].rearrange("p (u a) -> p u a", a=1).broadcast_to([P, U, P]),
                                            ALU.mult).then_inc(yw_ready.sem, 1)

                def update_state(s):
                    dve.wait_ge(su_ready.sem, su_ready.after(s))
                    for u in range(U):
                        last = nc.vector.scalar_tensor_tensor(S[:, u, :], S[:, u, :], vecB[:, 2, u:u + 1],
                                                              bank[5][:, u * P:(u + 1) * P], ALU.mult, ALU.subtract)
                    last.then_inc(s_updated.sem, 1)

                def sum_o(s):
                    dve.wait_ge(my_ready.sem, my_ready.after(s))
                    dve.wait_ge(qs_scaled.sem, qs_scaled.after(s))
                    nc.vector.tensor_tensor(O[:], QSg[:], bank[6][:].rearrange("p (u n) -> p u n", u=U),
                                            ALU.subtract).then_inc(o_ready.sem, 1)

                def gate_o(s):
                    dve.wait_ge(o_ready.sem, o_ready.after(s))
                    dve.wait_ge(gate_silu.sem, gate_silu.after(s))
                    dve.wait_ge(z_scaled.sem, z_scaled.before(s))
                    nc.vector.tensor_tensor(Z[:], O[:], gate[:], ALU.mult).then_inc(z_ready.sem, 1)

                def add_out(s, acc):
                    dve.wait_ge(out_ready.sem, out_ready.after(s))
                    nc.vector.tensor_tensor(acc, acc, bank[7][:], ALU.add).then_inc(out_added.sem, 1)

                def copy_norms(s):
                    dve.wait_ge(ss_ready.sem, ss_ready.after(s))
                    dve.wait_ge(nk_ready.sem, nk_ready.before(s))
                    nc.vector.tensor_scalar(ss[:], bank[1][:, 0:2 * U], L2_EPS, None, ALU.add).then_inc(ss_copied.sem, 1)

                def scale_v(s, par):
                    dve.wait_ge(v_turned.sem, v_turned.after(s))
                    dve.wait_ge(nk_ready.sem, nk_ready.after(s))
                    nc.vector.tensor_tensor(Vn[:, par], bank[4][:].rearrange("p (u n) -> p u n", u=U),
                                            nk[:].rearrange("p (u a) -> p u a", a=1).broadcast_to([P, U, P]),
                                            ALU.mult).then_inc(v_scaled.sem, 1)

                def make_am(s, par):
                    dve.wait_ge(exp_ready.sem, exp_ready.after(s))
                    dve.wait_ge(c_ready.sem, c_ready.after(s))
                    dve.wait_ge(my_ready.sem, my_ready.after(s))
                    for u in range(U):
                        dve.wait_ge(kq_ready.sem, kq_ready.step(s, u // 2 + 1))
                        o = (u % 2) * 2 * P
                        nc.vector.scalar_tensor_tensor(
                            AM[:, par, u, :, :], bank[5 + u // 2][:, o:o + 2 * P].rearrange("p (a n) -> p a n", a=2),
                            negc[:, u:u + 1], Ex[:, u:u + 1, :].broadcast_to([P, 2, P]),
                            ALU.mult, ALU.mult).then_inc(am_ready.sem, 1)

                def mask_level(s, l):
                    n = 1 << l
                    for gi in range(2):
                        dve.wait_ge(at_ready.sem, at_ready.step(s, 2 * l + gi + 1))
                        b = bank[2 + gi]
                        if l == 0:
                            nc.vector.tensor_tensor(grp(Tm, gi), b[:, 0:2 * P].rearrange("p (u n) -> p u n", u=2),
                                                    level0[:].rearrange("p (a n) -> p a n", a=1).broadcast_to([P, 2, P]),
                                                    ALU.mult).then_inc(masked.sem, 1)
                            continue
                        for u in range(2):
                            l1, _ = halves(Lv[:, l - 1, 2 * gi + u:2 * gi + u + 1, :], n)
                            last = nc.vector.tensor_tensor(l1[:, 0], b[:, u * 64:(u + 1) * 64].rearrange("p (m n) -> p m n", n=n),
                                                           level_masks[:, l - 1, :].rearrange("p (m n) -> p m n", n=n), ALU.mult)
                        last.then_inc(masked.sem, 1)

                for i in range(6):
                    convolve(-2, i)
                copy_norms(-1)
                scale_v(-1, 0)
                make_am(-1, 0)
                for i in range(6):
                    convolve(-1, i)
                with dve.Fori(0, HP) as q:
                    with dve.Fori(0, NC // 2) as cc:
                        for par in range(2):
                            c = cc * 2 + par
                            s = q * NC + c
                            other = 1 - par
                            mask_level(s, 0)
                            right_sides(s, other)
                            mask_level(s, 1)
                            weigh_y(s, other)
                            mask_level(s, 2)
                            copy_norms(s)
                            update_state(s)
                            sum_o(s)
                            gate_o(s)
                            mask_level(s, 3)
                            scale_v(s, other)
                            convolve(s, 0)
                            convolve(s, 1)
                            mask_level(s, 4)
                            make_am(s, other)
                            convolve(s, 2)
                            mask_level(s, 5)
                            convolve(s, 3)
                            convolve(s, 4)
                            mask_level(s, 6)
                            convolve(s, 5)
                            add_out(s, Acc[:, ds(c, 1), :, :].rearrange("p a b d -> p (a b d)"))
                s = SLOTS
                right_sides(s, 1)
                weigh_y(s, 1)
                update_state(s)
                sum_o(s)
                gate_o(s)
                add_out(s, Acc[:, 0, :, :].rearrange("p b d -> p (b d)"))

            @block.tensor
            def _(pe):
                def project(s, i):
                    kind, hh = i // 2, i % 2
                    if i == 0:
                        pe.wait_ge(W_ok.sem, W_ok.after(s))
                        pe.wait_ge(xc_in.sem, xc_in.after(s))
                        pe.wait_ge(exp_ready.sem, exp_ready.after(s))
                    elif i == 1:
                        pe.wait_ge(ss_copied.sem, ss_copied.after(s))
                    else:
                        pe.wait_ge(convolved.sem, convolved.step(s, i - 1))
                    for k in range(KD):
                        last = nc.tensor.matmul(bank[i % 2][:, 0:B * CW].rearrange("p (b n) -> p b n", b=B),
                                                Wp[:, k, kind, hh, :], xc[:, k, :, :], start=(k == 0), stop=(k == KD - 1))
                    last.then_inc(projected.sem, 1)

                def project_gate(s):
                    pe.wait_ge(v_scaled.sem, v_scaled.after(s))
                    pe.wait_ge(xg_in.sem, xg_in.after(s))
                    pe.wait_ge(Wg_ok.sem, Wg_ok.after(s))
                    for b in range(B):
                        for k in range(KD):
                            last = nc.tensor.matmul(bank[4][:, b * 2 * P:(b + 1) * 2 * P], xg[:, k, b, :],
                                                    Wg[:, k, :, :], start=(b == 0 and k == 0), stop=(k == KD - 1),
                                                    skip_group_check=True)
                    last.then_inc(gate_projected.sem, 1)

                def each_unit(dst, lhs, rhs):
                    for u in range(U):
                        last = nc.tensor.matmul(dst[:, u * P:(u + 1) * P], lhs(u), rhs(u), start=True, stop=True)
                    return last

                def sum_decays(s):
                    pe.wait_ge(vecF_in.sem, vecF_in.after(s))
                    pe.wait_ge(convolved.sem, convolved.before(s))
                    nc.tensor.matmul(bank[0][:], ident16[:], causal16[:], start=True, stop=False, skip_group_check=True)
                    for u in range(U):
                        last = nc.tensor.matmul(bank[0][:, u * P:(u + 1) * P], vecF[:, 1, u:u + 1].broadcast_to([P, P]),
                                                cumsum_mask[:], start=False, stop=True, skip_group_check=True)
                    last.then_inc(decay_ready.sem, 1)

                def turn_k(s, par):
                    pe.wait_ge(qk_silu.sem, qk_silu.after(s))
                    pe.wait_ge(out_added.sem, out_added.before(s))
                    for u in range(U):
                        last = nc.tensor.transpose(bank[7][:, u * P:(u + 1) * P], QK[:, par, 0, u, :], ident[:])
                    last.then_inc(k_turned.sem, 1)

                def turn_v(s):
                    pe.wait_ge(v_silu.sem, v_silu.after(s))
                    pe.wait_ge(gate_silu.sem, gate_silu.after(s))
                    for u in range(U):
                        last = nc.tensor.transpose(bank[4][:, u * P:(u + 1) * P], Vt[:, u, :], ident[:])
                    last.then_inc(v_turned.sem, 1)

                def sum_squares(s):
                    pe.wait_ge(qk_squared.sem, qk_squared.after(s))
                    for a in range(2):
                        for u in range(U):
                            last = nc.tensor.matmul(bank[1][:, a * U + u:a * U + u + 1], QKsq[:, a, u, :], ones[:, 0:1],
                                                    start=True, stop=True)
                    last.then_inc(ss_ready.sem, 1)

                def multiply_kq(s, par):
                    pe.wait_ge(s_updated.sem, s_updated.after(s))
                    pe.wait_ge(o_ready.sem, o_ready.after(s))
                    for u in range(U):
                        last = nc.tensor.matmul(bank[5 + u // 2][:, (u % 2) * 2 * P:(u % 2 + 1) * 2 * P]
                                                .rearrange("p (a n) -> p a n", a=2), QK[:, par, 0, u, :],
                                                QK[:, par, :, u, :], start=True, stop=True)
                        if u % 2:
                            last.then_inc(kq_ready.sem, 1)

                def meet_state(s, par):
                    pe.wait_ge(am_ready.sem, am_ready.before(s))
                    pe.wait_ge(s_updated.sem, s_updated.before(s))
                    each_unit(bank[5], lambda u: QK[:, par, 0, u, :], lambda u: S[:, u, :]).then_inc(ks_ready.sem, 1)
                    each_unit(bank[6], lambda u: QK[:, par, 1, u, :], lambda u: S[:, u, :]).then_inc(qs_ready.sem, 1)

                def solve(s, par):
                    pe.wait_ge(rhs_ready.sem, rhs_ready.after(s))
                    pe.wait_ge(tx_copied.sem, tx_copied.before(s))
                    each_unit(bank[5], lambda u: Xm[:, par, u, :], lambda u: RHS[:, u, :]).then_inc(y_ready.sem, 1)

                def apply_y(s, par):
                    pe.wait_ge(y_copied.sem, y_copied.after(s))
                    pe.wait_ge(qs_scaled.sem, qs_scaled.after(s))
                    each_unit(bank[6], lambda u: AM[:, par, u, 1, :], lambda u: Y[:, u, :]).then_inc(my_ready.sem, 1)
                    pe.wait_ge(yw_ready.sem, yw_ready.after(s))
                    each_unit(bank[5], lambda u: Ktok[:, par, u, :], lambda u: Yw[:, u, :]).then_inc(su_ready.sem, 1)

                def turn_z(s, k_copies):
                    pe.wait_ge(k_copied.sem, k_copies)
                    pe.wait_ge(z_scaled.sem, z_scaled.after(s))
                    for u in range(U):
                        last = nc.tensor.transpose(bank[7][:, u * P:(u + 1) * P], Zf[:, u, :], ident[:])
                    last.then_inc(z_turned.sem, 1)

                def output(s):
                    pe.wait_ge(zt_copied.sem, zt_copied.after(s))
                    pe.wait_ge(Wo_ok.sem, Wo_ok.after(s))
                    for b in range(B):
                        for hh in range(2):
                            last = nc.tensor.matmul(bank[7][:, b * D:(b + 1) * D], ZT[:, 2 * b + hh, :], Wo[:, hh, :],
                                                    start=(b == 0 and hh == 0), stop=(hh == 1), skip_group_check=True)
                    last.then_inc(out_ready.sem, 1)

                def turn_a(s, par):
                    pe.wait_ge(diag_filled.sem, diag_filled.before(s))
                    pe.wait_ge(tx_copied.sem, tx_copied.before(s))
                    for gi in range(2):
                        for u in range(2):
                            last = nc.tensor.transpose(bank[2 + gi][:, u * P:(u + 1) * P], AM[:, par, 2 * gi + u, 0, :], ident[:])
                        last.then_inc(at_ready.sem, 1)

                def multiply_at(s, par, l):
                    n = 1 << l
                    for gi in range(2):
                        if l == 1:
                            pe.wait_ge(masked.sem, masked.step(s, gi + 1))
                        else:
                            pe.wait_ge(tx_copied.sem, tx_copied.step(s, 2 * (l - 2) + gi + 1))
                        t1, _ = halves(grp(Tm, gi), n)
                        for u in range(2):
                            last = nc.tensor.matmul(bank[2 + gi][:, u * 64:(u + 1) * 64].rearrange("p (m n) -> p m n", n=n),
                                                    AM[:, par, 2 * gi + u, 0, :], t1[:, u], start=True, stop=True)
                        last.then_inc(at_ready.sem, 1)

                def multiply_tx(s, par, l):
                    n = 1 << l
                    if l == 1:
                        pe.wait_ge(x0_ready.sem, x0_ready.before(s))
                    for gi in range(2):
                        b = bank[2 + gi]
                        pe.wait_ge(masked.sem, masked.step(s, 2 * l + gi + 1))
                        _, x2 = halves(grp(Xm[:, par], gi), n)
                        l1, _ = halves(grp(Lv[:, l - 1], gi), n)
                        for u in range(2):
                            if l < LEVELS - 1:
                                nc.tensor.matmul(b[:, 128 + u * 64:128 + (u + 1) * 64].rearrange("p (m n) -> p m n", n=n),
                                                 Xm[:, par, 2 * gi + u, :], l1[:, u], start=True, stop=True)
                            last = nc.tensor.matmul(b[:, 256 + u * 64:256 + (u + 1) * 64].rearrange("p (m n) -> p m n", n=n),
                                                    Lv[:, l - 1, 2 * gi + u, :], x2[:, u], start=True, stop=True)
                        last.then_inc(tx_ready.sem, 1)

                for i in range(6):
                    project(-2, i)
                sum_decays(-1)
                turn_k(-1, 0)
                turn_v(-1)
                sum_squares(-1)
                multiply_kq(-1, 0)
                for i in range(6):
                    project(-1, i)
                with pe.Fori(0, HP) as q:
                    with pe.Fori(0, NC // 2) as cc:
                        for par in range(2):
                            s = q * NC + cc * 2 + par
                            other = 1 - par
                            meet_state(s, other)
                            turn_a(s, par)
                            sum_decays(s)
                            multiply_at(s, par, 1)
                            solve(s, other)
                            turn_k(s, other)
                            multiply_tx(s, par, 1)
                            turn_v(s)
                            multiply_at(s, par, 2)
                            apply_y(s, other)
                            sum_squares(s)
                            multiply_tx(s, par, 2)
                            project(s, 0)
                            multiply_at(s, par, 3)
                            project(s, 1)
                            multiply_tx(s, par, 3)
                            multiply_kq(s, other)
                            multiply_at(s, par, 4)
                            project(s, 2)
                            multiply_tx(s, par, 4)
                            project(s, 3)
                            multiply_at(s, par, 5)
                            turn_z(s, k_copied.after(s))
                            multiply_tx(s, par, 5)
                            project(s, 4)
                            multiply_at(s, par, 6)
                            output(s)
                            multiply_tx(s, par, 6)
                            project(s, 5)
                            project_gate(s)
                s = SLOTS
                meet_state(s, 1)
                solve(s, 1)
                apply_y(s, 1)
                turn_z(s, k_copied.before(s))
                output(s)
        tools.clear()


class FfnWeights:
    def __init__(self, tools, ctx, A_gate, A_gs, A_up, A_us, A_down, A_dsc):
        self.A = A_gate, A_gs, A_up, A_us, A_down, A_dsc
        self.Wi = tools.sb("ff_Wi", [P, 3, KD * FI], I32, ctx)
        self.gs = tools.sb("ff_gs", [P, FI // P], F32, ctx)
        self.us = tools.sb("ff_us", [P, FI // P], F32, ctx)
        self.dsc = tools.sb("ff_dsc", [P, D], F32, ctx)
        self.w_loaded = [tools.sem(f"ff_w{i}_loaded") for i in range(3)]
        self.scales_loaded = tools.sem("ff_scales_loaded")

    def load(self, sp):
        A_gate, A_gs, A_up, A_us, A_down, A_dsc = self.A
        Wi = self.Wi
        sp.dma_start(Wi[:, 0, :].rearrange("p (k i) -> p k i", k=KD), A_gate.rearrange("(k p) i -> p k i", p=P)).then_inc(self.w_loaded[0], 16)
        sp.dma_start(Wi[:, 1, :].rearrange("p (k i) -> p k i", k=KD), A_up.rearrange("(k p) i -> p k i", p=P)).then_inc(self.w_loaded[1], 16)
        sp.dma_start(Wi[:, 2, :].rearrange("p (t d) -> p t d", t=FI // P), A_down.rearrange("(t p) d -> p t d", p=P)).then_inc(self.w_loaded[2], 16)
        sp.dma_start(self.gs[:], A_gs).then_inc(self.scales_loaded, 16)
        sp.dma_start(self.us[:], A_us).then_inc(self.scales_loaded, 16)
        sp.dma_start(self.dsc[:], A_dsc.partition_broadcast(P)).then_inc(self.scales_loaded, 16)


def int_ffn(nc, tools, bank, XT, Yt, weights):
    IT = FI // P
    NB = NC * B // 4
    with ExitStack() as ctx:
        def sb(name, shape, dt=F32):
            return tools.sb("ff_" + name, shape, dt, ctx)

        def sem(name):
            return tools.sem("ff_" + name)

        Wi, gs, us, dsc = weights.Wi, weights.gs, weights.us, weights.dsc
        w_loaded, scales_loaded = weights.w_loaded, weights.scales_loaded
        Wf = sb("Wf", [P, 3, KD * FI])
        sg = sb("sg", [P, 2, 4 * P])
        hT = sb("hT", [P, IT, 4 * P])
        w_made = sem("w_made")
        gu_ready = PerSlot(sem("gu_ready"), IT)
        g_silu = PerSlot(sem("g_silu"), IT)
        h_ready = PerSlot(sem("h_ready"), IT)
        y_ready = PerSlot(sem("y_ready"), 4)
        y_scaled = PerSlot(sem("y_scaled"), 4)
        Wg = Wf[:, 0, :].rearrange("p (k i) -> p k i", k=KD)
        Wu = Wf[:, 1, :].rearrange("p (k i) -> p k i", k=KD)
        Wd = Wf[:, 2, :].rearrange("p (t d) -> p t d", t=IT)
        Yv = Yt[:].rearrange("p c b d -> p (c b) d")

        with nc.Block() as block:
            @block.sync
            def _(sp):
                for x in (g_silu, h_ready, y_ready, y_scaled, gu_ready):
                    sp.sem_inc(x.sem, x.n)
        with nc.Block() as block:
            @block.tensor
            def _(pe):
                pe.wait_ge(w_made, 2)
                with pe.Fori(0, NB) as n:
                    for i in range(IT):
                        pe.wait_ge(g_silu.sem, g_silu.step(n, i - 1))
                        pe.wait_ge(h_ready.sem, h_ready.step(n, i - 1))
                        for w, bk in ((Wg, bank[i % 2]), (Wu, bank[2 + i % 2])):
                            for k in range(KD):
                                last = nc.tensor.matmul(bk[:], w[:, k, i * P:(i + 1) * P], XT[:, k, ds(n * 4 * P, 4 * P)],
                                                        start=(k == 0), stop=(k == KD - 1))
                        last.then_inc(gu_ready.sem, 1)
                    pe.wait_ge(h_ready.sem, h_ready.after(n))
                    pe.wait_ge(w_made, 3)
                    for j in range(4):
                        pe.wait_ge(y_scaled.sem, y_scaled.step(n, j - 1))
                        for i in range(IT):
                            last = nc.tensor.matmul(bank[4 + j % 2][:, 0:D], hT[:, i, j * P:(j + 1) * P], Wd[:, i, :],
                                                    start=(i == 0), stop=(i == IT - 1))
                        last.then_inc(y_ready.sem, 1)

            @block.scalar
            def _(act):
                act.wait_ge(scales_loaded, 48)
                with act.Fori(0, NB) as n:
                    for i in range(IT):
                        act.wait_ge(gu_ready.sem, gu_ready.step(n, i + 1))
                        act.wait_ge(h_ready.sem, h_ready.step(n, i - 1))
                        nc.scalar.activation(sg[:, i % 2, :], bank[i % 2][:], ACT.Silu, scale=gs[:, i:i + 1]).then_inc(g_silu.sem, 1)

            @block.vector
            def _(dve):
                for i in range(3):
                    dve.wait_ge(w_loaded[i], 16)
                    nc.vector.tensor_scalar(Wf[:, i, :], Wi[:, i, :], -128.0, None, ALU.add).then_inc(w_made, 1)
                dve.wait_ge(scales_loaded, 48)
                with dve.Fori(0, NB) as n:
                    for i in range(IT):
                        dve.wait_ge(g_silu.sem, g_silu.step(n, i + 1))
                        if i == 0:
                            dve.wait_ge(y_ready.sem, y_ready.before(n))
                        nc.vector.scalar_tensor_tensor(hT[:, i, :], bank[2 + i % 2][:], us[:, i:i + 1], sg[:, i % 2, :],
                                                       ALU.mult, ALU.mult).then_inc(h_ready.sem, 1)
                    for j in range(4):
                        dve.wait_ge(y_ready.sem, y_ready.step(n, j + 1))
                        nc.vector.tensor_tensor(Yv[:, ds(n * 4 + j, 1), :].rearrange("p a d -> p (a d)"), bank[4 + j % 2][:, 0:D],
                                                dsc[:], ALU.mult).then_inc(y_scaled.sem, 1)


class AttentionWeights:
    LOADED = 16 * (3 * KD + 4)

    def __init__(self, tools, ctx, A_wq, A_bq, A_cs, A_wv, A_bv, A_wd, A_bd):
        self.A = A_wq, A_bq, A_cs, A_wv, A_bv, A_wd, A_bd
        self.Wq = tools.sb("at_Wq", [P, KD, 4, D], F32, ctx)
        self.Wv = tools.sb("at_Wv", [P, KD, D], F32, ctx)
        self.Wdn = tools.sb("at_Wdn", [P, KD, D], F32, ctx)
        self.bq = tools.sb("at_bq", [P, 4, KD], F32, ctx)
        self.cs = tools.sb("at_cs", [P, 2, T], F32, ctx)
        self.bv = tools.sb("at_bv", [P, D], F32, ctx)
        self.bd = tools.sb("at_bd", [P, D], F32, ctx)
        self.loaded = tools.sem("at_w_loaded")

    def load(self, sp):
        A_wq, A_bq, A_cs, A_wv, A_bv, A_wd, A_bd = self.A
        for k in range(KD):
            sp.dma_start(self.Wq[:, k, :, :], A_wq[:, k * P:(k + 1) * P, :].rearrange("a p n -> p a n")).then_inc(self.loaded, 16)
            sp.dma_start(self.Wv[:, k, :], A_wv[k * P:(k + 1) * P, :]).then_inc(self.loaded, 16)
            sp.dma_start(self.Wdn[:, k, :], A_wd[k * P:(k + 1) * P, :]).then_inc(self.loaded, 16)
        sp.dma_start(self.bq[:], A_bq).then_inc(self.loaded, 16)
        sp.dma_start(self.cs[:], A_cs.rearrange("a p t -> p a t")).then_inc(self.loaded, 16)
        sp.dma_start(self.bv[:], A_bv.partition_broadcast(P)).then_inc(self.loaded, 16)
        sp.dma_start(self.bd[:], A_bd.partition_broadcast(P)).then_inc(self.loaded, 16)


def attention(nc, tools, PS, bank, ident16, causal16, diag16, XT, Yt, weights):
    NB = NC * B // 4
    with ExitStack() as ctx:
        def sb(name, shape, dt=F32):
            return tools.sb("at_" + name, shape, dt, ctx)

        def sem(name):
            return tools.sem("at_" + name)

        QP = sb("QP", [P, 3, 2, KD, B, T], BF16)
        V = sb("V", [P, NC, B, AH, AD])
        Wq, Wv, Wdn, bq, cs, bv, bd = (weights.Wq, weights.Wv, weights.Wdn, weights.bq, weights.cs, weights.bv, weights.bd)
        w_loaded, LOADED = weights.loaded, weights.LOADED
        with ExitStack() as ctx2:
            QF = tools.sb("at_QF", [P, 2, KD, B, T], F32, ctx2)
            qa = tools.sb("at_qa", [P, 2, 2, 4 * P], F32, ctx2)
            qm = tools.sb("at_qm", [P, 2, 2, 4 * P], F32, ctx2)
            qk_ready = PerSlot(sem("qk_ready"), 4)
            biased = PerSlot(sem("biased"), 4)
            rotated = PerSlot(sem("rotated"), 8)
            summed = PerSlot(sem("summed"), 4)
            v_ready = sem("v_ready")
            v_added = sem("v_added")
            part_cast = sem("part_cast")
            rest_taken = sem("rest_taken")
            with nc.Block() as block:
                @block.sync
                def _(sp):
                    for x in (qk_ready, biased, rotated, summed):
                        sp.sem_inc(x.sem, x.n)
            with nc.Block() as block:
                @block.tensor
                def _(pe):
                    pe.wait_ge(w_loaded, LOADED)
                    with pe.Fori(0, NB) as n:
                        for i in range(4):
                            a, m = i // 2, i % 2
                            pe.wait_ge(biased.sem, biased.step(n, i - 1))
                            for part in range(2):
                                for k in range(KD):
                                    last = nc.tensor.matmul(bank[2 * (i % 2) + part][:], Wq[:, k, 2 * a + part, m * P:(m + 1) * P],
                                                            XT[:, k, ds(n * 4 * P, 4 * P)], start=(k == 0), stop=(k == KD - 1))
                            last.then_inc(qk_ready.sem, 1)
                    for t in range(NC * B):
                        if t >= 2:
                            pe.wait_ge(v_added, t - 1)
                        for k in range(KD):
                            last = nc.tensor.matmul(bank[4 + t % 2][:, 0:D], XT[:, k, t * P:(t + 1) * P], Wv[:, k, :],
                                                    start=(k == 0), stop=(k == KD - 1))
                        last.then_inc(v_ready, 1)

                @block.scalar
                def _(act):
                    act.wait_ge(w_loaded, LOADED)
                    with act.Fori(0, NB) as n:
                        for i in range(4):
                            a, m = i // 2, i % 2
                            act.wait_ge(qk_ready.sem, qk_ready.step(n, i + 1))
                            act.wait_ge(rotated.sem, rotated.step(n, 2 * (i - 1)))
                            for part in range(2):
                                last = nc.scalar.activation(qa[:, i % 2, part, :], bank[2 * (i % 2) + part][:], ACT.Identity,
                                                            bias=bq[:, 2 * a + part, m:m + 1])
                            last.then_inc(biased.sem, 1)

                @block.vector
                def _(dve):
                    dve.wait_ge(w_loaded, LOADED)
                    with dve.Fori(0, NB) as n:
                        for i in range(4):
                            a, m = i // 2, i % 2
                            dve.wait_ge(biased.sem, biased.step(n, i + 1))
                            for part in range(2):
                                for c in range(2):
                                    tab = cs[:, part, ds((n * 2 + c) * P, P)].rearrange("p (a n) -> p a n", a=1).broadcast_to([P, B, P])
                                    last = nc.vector.tensor_tensor(
                                        qm[:, i % 2, part, c * B * P:(c + 1) * B * P].rearrange("p (b n) -> p b n", b=B),
                                        qa[:, i % 2, part, c * B * P:(c + 1) * B * P].rearrange("p (b n) -> p b n", b=B),
                                        tab, ALU.mult)
                                last.then_inc(rotated.sem, 1)
                            dve.wait_ge(rotated.sem, rotated.step(n, 2 * (i + 1)))
                            for c in range(2):
                                last = nc.vector.tensor_tensor(
                                    QF[:, a, m, :, ds((n * 2 + c) * P, P)],
                                    qm[:, i % 2, 0, c * B * P:(c + 1) * B * P].rearrange("p (b n) -> p b n", b=B),
                                    qm[:, i % 2, 1, c * B * P:(c + 1) * B * P].rearrange("p (b n) -> p b n", b=B), ALU.add)
                            last.then_inc(summed.sem, 1)
                    for t in range(NC * B):
                        dve.wait_ge(v_ready, t + 1)
                        nc.vector.tensor_tensor(V[:, t // B, t % B, :, 0:AD], bank[4 + t % 2][:, 0:D].rearrange("p (h d) -> p h d", d=AD),
                                                bv[:].rearrange("p (h d) -> p h d", d=AD), ALU.add).then_inc(v_added, 1)

            with nc.Block() as block:
                pieces8 = [(a, m, b) for a in range(2) for m in range(KD) for b in range(B)]

                @block.scalar
                def _(act):
                    for n, (a, m, b) in enumerate(pieces8):
                        nc.scalar.activation(QP[:, 0, a, m, b, :], QF[:, a, m, b, :], ACT.Copy).then_inc(part_cast, 1)
                        if n >= 1:
                            act.wait_ge(rest_taken, 2 * n - 1)
                            a, m, b = pieces8[n - 1]
                            nc.scalar.activation(QP[:, 1, a, m, b, :], QF[:, a, m, b, :], ACT.Copy).then_inc(part_cast, 1)
                    a, m, b = pieces8[-1]
                    act.wait_ge(rest_taken, 2 * len(pieces8) - 1)
                    nc.scalar.activation(QP[:, 1, a, m, b, :], QF[:, a, m, b, :], ACT.Copy).then_inc(part_cast, 1)

                @block.vector
                def _(dve):
                    for n, (a, m, b) in enumerate(pieces8):
                        dve.wait_ge(part_cast, max(2 * n, 1))
                        nc.vector.tensor_tensor(QF[:, a, m, b, :], QF[:, a, m, b, :], QP[:, 0, a, m, b, :], ALU.subtract).then_inc(rest_taken, 1)
                        dve.wait_ge(part_cast, min(2 * n + 3, 2 * len(pieces8)))
                        nc.vector.tensor_tensor(QP[:, 2, a, m, b, :], QF[:, a, m, b, :], QP[:, 1, a, m, b, :], ALU.subtract).then_inc(rest_taken, 1)

        TERMS = ((0, 0), (0, 1), (1, 0), (1, 1), (0, 2), (2, 0))
        MR = 3
        ROWS = MR + len(TERMS) * AD
        units = [(hh, b) for hh in range(2) for b in range(B)]
        NU = len(units)
        LAG = 4
        qs = sb("qs", [ROWS, 2, B, T], BF16)
        ks = sb("ks", [ROWS, 2, B, T], BF16)
        zrow = sb("zrow", [MR, B, T], BF16)
        mx = sb("mx", [P, NC])
        mrest = sb("mrest", [P, NC])
        mp = sb("mp", [P, MR, NC], BF16)
        ONES = 32
        Vu = sb("Vu", [P, 2, NC, ONES + AD])
        OT = sb("OT", [ONES + AD, 2, T])
        first = [kt * NC - kt * (kt - 1) // 2 for kt in range(NC)]
        PT = sb("PT", [P, NC * (NC + 1) // 2, P])
        AOT = XT[:].rearrange("p k (b t) -> p k b t", b=B)
        sums = sb("sums", [P, KD, B, T])
        pieces = [(kt, i, 4 - i % 4) for kt in range(NC) for i in sorted({kt} | {j for j in range(0, NC, 4) if j > kt})]
        NPC = len(pieces)
        assert NPC % 2 == 0
        heads_loaded = [sem(f"heads_loaded{i}") for i in range(2)]
        LOADS = 1 + 2 * len(TERMS)
        rows_set = sem("rows_set")
        scored = PerSlot(sem("scored"), NC)
        maxed = PerSlot(sem("maxed"), NC)
        max_split = PerSlot(sem("max_split"), 4)
        max_turned = PerSlot(sem("max_turned"), 1)
        max_copied = PerSlot(sem("max_copied"), 1)
        scored_t = PerSlot(sem("scored_t"), NPC)
        exped = PerSlot(sem("exped"), NPC)
        pv_ready = PerSlot(sem("pv_ready"), 1)
        v_staged = PerSlot(sem("v_staged"), 1)
        stored = [sem(f"stored{i}") for i in range(2)]
        settles = sem("settles")
        kept = PerSlot(sem("kept"), 1)
        with nc.Block() as block:
            @block.sync
            def _(sp):
                for x in (scored, maxed, max_split, max_turned, max_copied, scored_t, exped, pv_ready, kept, v_staged):
                    sp.sem_inc(x.sem, x.n)
                for x in stored:
                    sp.sem_inc(x, 2 * 16)

            @block.gpsimd
            def _(pool):
                nc.gpsimd.memset(zrow[:], 0.0).then_inc(rows_set, 1)
                nc.gpsimd.memset(ks[0:MR, :, :, :], 1.0).then_inc(rows_set, 1)
                nc.gpsimd.memset(Vu[:, :, :, 0:ONES], 0.0).then_inc(rows_set, 1)
                nc.gpsimd.memset(Vu[:, :, :, ONES:], 1.0).then_inc(rows_set, 1)
        with nc.Block() as block:
            @block.sync
            def _(sp):
                def store_head(h):
                    for b in range(B):
                        s = B * h + b
                        sp.wait_ge(kept.sem, kept.after(s))
                        r = (h % 8) * AD
                        sp.dma_start(AOT[r:r + AD, h // 8, b, :], OT[0:AD, s % 2, :]).then_inc(stored[s % 2], 16)
                        sp.dma_start(sums[r:r + AD, h // 8, b, :], OT[ONES:, s % 2, :]).then_inc(stored[s % 2], 16)

                for h in range(AH):
                    if h >= 2:
                        sp.wait_ge(scored_t.sem, scored_t.after(2 * (h - 2) + 1))
                    r = (h % 8) * AD
                    loaded = heads_loaded[h % 2]
                    sp.dma_start(qs[0:MR, h % 2, :, :], zrow[:]).then_inc(loaded, 16)
                    for n, parts in enumerate(TERMS):
                        at = MR + n * AD
                        for a, dst in enumerate((qs, ks)):
                            sp.dma_start(dst[at:at + AD, h % 2, :, :], QP[r:r + AD, parts[a], a, h // 8, :, :]).then_inc(loaded, 16)
                    if h >= 2:
                        store_head(h - 2)
                sp.sem_inc(heads_loaded[0], 16 * LOADS)
                for h in range(AH - 2, AH):
                    store_head(h)
                for x in stored:
                    sp.wait_ge(x, 2 * 16 * (1 + B * AH // 2))

            @block.gpsimd
            def _(pool):
                with pool.Fori(0, AH // 2) as g:
                    for u, (hh, b) in enumerate(units):
                        s = g * NU + u
                        pool.wait_ge(pv_ready.sem, pv_ready.before(s - 1))
                        pool.sem_inc(settles, 1)
                        nc.gpsimd.tensor_copy(Vu[:, u % 2, :, 0:AD],
                                              V[:, :, b, ds(g * 2 + hh, 1), :].rearrange("p c a d -> p c (a d)")).then_inc(v_staged.sem, 1)

            @block.tensor
            def _(pe):
                def score(s, u, i, loads=None):
                    hh, b = units[u]
                    if b == 0 and i == 0:
                        pe.wait_ge(heads_loaded[hh], loads)
                    if i == 0:
                        pe.wait_ge(max_copied.sem, max_copied.before(s))
                    pe.wait_ge(maxed.sem, maxed.step(s, i - 1))
                    for g4 in range(i // 4 + 1):
                        cols = min(4, i + 1 - g4 * 4) * P
                        diag = g4 == i // 4
                        bk = bank[2 * (i % 2) + g4]
                        last = nc.tensor.matmul(bk[:, 0:cols], qs[:, hh, b, i * P:(i + 1) * P],
                                                ks[:, hh, b, g4 * 4 * P:g4 * 4 * P + cols], start=True, stop=not diag,
                                                skip_group_check=True)
                        if diag:
                            last = nc.tensor.matmul(bk[:, cols - P:cols], ident16[:], diag16[:], start=False, stop=True,
                                                    skip_group_check=True)
                    last.then_inc(scored.sem, 1)

                def turn_max(s, u):
                    pe.wait_ge(max_split.sem, max_split.after(s))
                    for i in range(NC):
                        last = nc.tensor.matmul(bank[i // 4][0:MR, (i % 4) * P:(i % 4 + 1) * P], mp[:, :, i], ident16[:],
                                                start=True, stop=True)
                    last.then_inc(max_turned.sem, 1)

                def score_t(s, u, kt):
                    hh, b = units[u]
                    if kt == 0:
                        pe.wait_ge(max_copied.sem, max_copied.after(s))
                    for n, (k, i, tiles) in enumerate(pieces):
                        if k != kt:
                            continue
                        pe.wait_ge(exped.sem, exped.step(s, n - 1))
                        bk = bank[4 + n % 2]
                        diag = i == kt
                        last = nc.tensor.matmul(bk[:, 0:tiles * P], ks[:, hh, b, kt * P:(kt + 1) * P],
                                                qs[:, hh, b, i * P:(i + tiles) * P], start=True, stop=not diag,
                                                skip_group_check=True)
                        if diag:
                            last = nc.tensor.matmul(bk[:, 0:P], ident16[:], causal16[:, 0:P], start=False, stop=True,
                                                    skip_group_check=True)
                        last.then_inc(scored_t.sem, 1)

                def pv(s, u, kt):
                    if kt == 0:
                        pe.wait_ge(v_staged.sem, v_staged.after(s))
                        pe.wait_ge(kept.sem, kept.before(s))
                    for n, (k, i, tiles) in enumerate(pieces):
                        if k != kt:
                            continue
                        pe.wait_ge(exped.sem, exped.step(s, n + 1))
                        at = first[kt] + i - kt
                        last = nc.tensor.matmul(bank[6 + i // 4][0:ONES + AD, (i % 4) * P:(i % 4 + tiles) * P], Vu[:, u % 2, kt, :],
                                                PT[:, at:at + tiles, :].rearrange("p a n -> p (a n)"), start=(kt == 0),
                                                stop=(i + tiles == kt // 4 * 4 + 4 and kt % 4 == 3), skip_group_check=True)
                    if kt == NC - 1:
                        last.then_inc(pv_ready.sem, 1)

                for i in range(NC):
                    score(0, 0, i, 16 * LOADS)
                turn_max(0, 0)
                with pe.Fori(0, AH // 2) as g:
                    for u in range(NU):
                        s = g * NU + u
                        nu = (u + 1) % NU
                        loads = (g + 1 + (u + 1) // NU) * 16 * LOADS
                        score(s + 1, nu, 0, loads)
                        for i in range(NC):
                            if i + 1 < NC:
                                score(s + 1, nu, i + 1, loads)
                            score_t(s, u, i)
                            if i >= LAG:
                                pv(s, u, i - LAG)
                        pv(s, u, NC - LAG)
                        turn_max(s + 1, nu)
                        for i in range(NC - LAG + 1, NC):
                            pv(s, u, i)

            @block.scalar
            def _(act):
                def exps(s):
                    for n, (kt, i, tiles) in enumerate(pieces):
                        act.wait_ge(scored_t.sem, scored_t.step(s, n + 1))
                        at = first[kt] + i - kt
                        nc.scalar.activation(PT[:, at:at + tiles, :], bank[4 + n % 2][:, 0:tiles * P].rearrange("p (a n) -> p a n", n=P),
                                             ACT.Exp, scale=AD ** -0.5).then_inc(exped.sem, 1)

                with act.Fori(0, AH // 2) as g:
                    for u in range(NU):
                        exps(g * NU + u)

            @block.vector
            def _(dve):
                def row_max(s, i):
                    dve.wait_ge(scored.sem, scored.step(s, i + 1))
                    nc.vector.reduce_max(mx[:, i:i + 1], PS[:, 2 * (i % 2):2 * (i % 2) + 2, :].rearrange("p a n -> p (a n)")[:, 0:(i + 1) * P],
                                         axis=AX.X).then_inc(maxed.sem, 1)

                def split_max(s):
                    dve.wait_ge(maxed.sem, maxed.after(s))
                    dve.wait_ge(max_turned.sem, max_turned.before(s))
                    nc.vector.tensor_scalar(mp[:, 0, :], mx[:], -1.0, None, ALU.mult).then_inc(max_split.sem, 1)
                    dve.wait_ge(max_split.sem, max_split.step(s, 1))
                    nc.vector.scalar_tensor_tensor(mrest[:], mx[:], -1.0, mp[:, 0, :], ALU.mult, ALU.subtract).then_inc(max_split.sem, 1)
                    dve.wait_ge(max_split.sem, max_split.step(s, 2))
                    nc.vector.tensor_copy(mp[:, 1, :], mrest[:]).then_inc(max_split.sem, 1)
                    dve.wait_ge(max_split.sem, max_split.step(s, 3))
                    nc.vector.tensor_tensor(mp[:, 2, :], mrest[:], mp[:, 1, :], ALU.subtract).then_inc(max_split.sem, 1)

                def copy_max(s, u):
                    hh, b = units[u]
                    dve.wait_ge(max_turned.sem, max_turned.after(s))
                    nc.vector.tensor_copy(qs[0:MR, hh, b, :], PS[0:MR, 0:2, :].rearrange("p a n -> p (a n)")).then_inc(max_copied.sem, 1)

                def keep_out(s, g, u):
                    dve.wait_ge(pv_ready.sem, pv_ready.after(s))
                    dve.wait_ge(stored[u % 2], 2 * 16 * (1 + g * (NU // 2) + u // 2))
                    nc.vector.tensor_copy(OT[:, u % 2, :], PS[0:ONES + AD, 6:8, :].rearrange("p a n -> p (a n)")).then_inc(kept.sem, 1)

                for i in range(NC):
                    row_max(0, i)
                split_max(0)
                copy_max(0, 0)
                with dve.Fori(0, AH // 2) as g:
                    for u in range(NU):
                        s = g * NU + u
                        for i in range(NC):
                            row_max(s + 1, i)
                        split_max(s + 1)
                        copy_max(s + 1, (u + 1) % NU)
                        keep_out(s, g, u)

        inverted = sem("inverted")
        divided = sem("divided")
        d_ready = sem("d_ready")
        d_added = sem("d_added")
        with nc.Block() as block:
            @block.tensor
            def _(pe):
                for t in range(NC * B):
                    if t % (4 * B) == 0:
                        pe.wait_ge(divided, (t // (4 * B) + 1) * B)
                    if t >= 2:
                        pe.wait_ge(d_added, t - 1)
                    c, b = t // B, t % B
                    for k in range(KD):
                        last = nc.tensor.matmul(bank[t % 2][:, 0:D], AOT[:, k, b, c * P:(c + 1) * P], Wdn[:, k, :], start=(k == 0), stop=(k == KD - 1))
                    last.then_inc(d_ready, 1)

            @block.vector
            def _(dve):
                for n in range(2 * B):
                    part = (slice(None), slice(None), n % B, slice(n // B * 4 * P, (n // B + 1) * 4 * P))
                    nc.vector.reciprocal(sums[part], sums[part]).then_inc(inverted, 1)
                    dve.wait_ge(inverted, n + 1)
                    nc.vector.tensor_tensor(AOT[part], AOT[part], sums[part], ALU.mult).then_inc(divided, 1)
                for t in range(NC * B):
                    dve.wait_ge(d_ready, t + 1)
                    nc.vector.tensor_tensor(Yt[:, t // B, t % B, :], bank[t % 2][:, 0:D], bd[:], ALU.add).then_inc(d_added, 1)


class ExpertWeights:
    NE = NSH + E

    def __init__(self, tools, ctx, A_wr, A_tri, A_w1, A_w3, A_w2):
        self.A = A_wr, A_tri, A_w1, A_w3, A_w2
        self.W1 = tools.sb("ex_W1", [P, KD, self.NE, EH], F32, ctx)
        self.W3 = tools.sb("ex_W3", [P, KD, self.NE, EH], F32, ctx)
        self.W2 = tools.sb("ex_W2", [P, self.NE, D], F32, ctx)
        self.Wr = tools.sb("ex_Wr", [P, KD, E], F32, ctx)
        self.tri = tools.sb("ex_tri", [P, E, E], F32, ctx)
        self.router_loaded = tools.sem("ex_router_loaded")
        self.w_loaded = tools.sem("ex_w_loaded")

    def load(self, sp):
        A_wr, A_tri, A_w1, A_w3, A_w2 = self.A
        sp.dma_start(self.Wr[:], A_wr.rearrange("(k p) e -> p k e", p=P)).then_inc(self.router_loaded, 16)
        sp.dma_start(self.tri[:].rearrange("p e f -> p (e f)"), A_tri.partition_broadcast(P)).then_inc(self.router_loaded, 16)
        for k in range(KD):
            sp.dma_start(self.W1[:, k, :, :], A_w1[:, k * P:(k + 1) * P, :].rearrange("e p h -> p e h")).then_inc(self.w_loaded, 16)
            sp.dma_start(self.W3[:, k, :, :], A_w3[:, k * P:(k + 1) * P, :].rearrange("e p h -> p e h")).then_inc(self.w_loaded, 16)
        sp.dma_start(self.W2[:], A_w2.rearrange("e p d -> p e d")).then_inc(self.w_loaded, 16)


def experts(nc, tools, bank, ident, XT, Yt, weights):
    NB = NC * B // 4
    NE = NSH + E
    NTL = NC * B
    with ExitStack() as ctx:
        def sb(name, shape, dt=F32):
            return tools.sb("ex_" + name, shape, dt, ctx)

        def sem(name):
            return tools.sem("ex_" + name)

        W1, W3, W2, Wr, tri = weights.W1, weights.W3, weights.W2, weights.Wr, weights.tri
        w_loaded, router_loaded = weights.w_loaded, weights.router_loaded
        cw = sb("cw", [P, NTL, E])
        with ExitStack() as ctx2:
            lgT = tools.sb("ex_lgT", [E, NTL * P], F32, ctx2)
            mx = tools.sb("ex_mx", [P, NTL, 1], F32, ctx2)
            pr = tools.sb("ex_pr", [P, NTL, E], F32, ctx2)
            den = tools.sb("ex_den", [P, NTL, 1], F32, ctx2)
            above = tools.sb("ex_above", [P, NTL, E, E], F32, ctx2)
            equal = tools.sb("ex_equal", [P, NTL, E, E], F32, ctx2)
            rank = tools.sb("ex_rank", [P, NTL, E, 1], F32, ctx2)
            logits = sem("logits")
            logits_copied = sem("logits_copied")
            logits_turned = sem("logits_turned")
            exped = sem("exped")
            steps = sem("router_steps")
            with nc.Block() as block:
                @block.tensor
                def _(pe):
                    pe.wait_ge(router_loaded, 32)
                    for n in range(NB):
                        for k in range(KD):
                            last = nc.tensor.matmul(bank[n][0:E, :], Wr[:, k, :], XT[:, k, n * 4 * P:(n + 1) * 4 * P],
                                                    start=(k == 0), stop=(k == KD - 1))
                        last.then_inc(logits, 1)
                    for t in range(NTL):
                        pe.wait_ge(logits_copied, t // 4 + 1)
                        last = nc.tensor.transpose(bank[4][:, t * E:(t + 1) * E], lgT[:, t * P:(t + 1) * P], ident[0:E, 0:E])
                    last.then_inc(logits_turned, 1)

                lg = bank[4][:, 0:NTL * E].rearrange("p (t e) -> p t e", e=E)

                @block.scalar
                def _(act):
                    for n in range(NB):
                        act.wait_ge(logits, n + 1)
                        nc.scalar.activation(lgT[:, n * 4 * P:(n + 1) * 4 * P], bank[n][0:E, :], ACT.Copy).then_inc(logits_copied, 1)
                    act.wait_ge(steps, 2)
                    nc.scalar.activation(pr[:], pr[:], ACT.Exp).then_inc(exped, 1)

                @block.vector
                def _(dve):
                    def step(n, ins):
                        ins.then_inc(steps, 1)
                        dve.wait_ge(steps, n)

                    dve.wait_ge(logits_turned, 1)
                    dve.wait_ge(router_loaded, 32)
                    over_e = [P, NTL, E]
                    pairs = [P, NTL * E, E]
                    flat = "p t e f -> p (t e) f"
                    step(1, nc.vector.tensor_reduce(mx[:, :, 0], lg, AX.X, ALU.max))
                    step(2, nc.vector.tensor_tensor(pr[:], lg, mx[:].broadcast_to(over_e), ALU.subtract))
                    dve.wait_ge(exped, 1)
                    step(3, nc.vector.tensor_reduce(den[:, :, 0], pr[:], AX.X, ALU.add))
                    step(4, nc.vector.reciprocal(den[:], den[:]))
                    step(5, nc.vector.tensor_tensor(pr[:], pr[:], den[:].broadcast_to(over_e), ALU.mult))
                    for t in range(NTL):
                        pf = pr[:, t:t + 1, :].broadcast_to([P, E, E])
                        pe_ = pr[:, t, :].rearrange("p (e a) -> p e a", a=1).broadcast_to([P, E, E])
                        nc.vector.tensor_tensor(above[:, t, :, :], pf, pe_, ALU.is_gt)
                        last = nc.vector.tensor_tensor(equal[:, t, :, :], pf, pe_, ALU.is_equal)
                    step(6, last)
                    step(7, nc.vector.tensor_tensor(equal[:].rearrange("p t e f -> p t (e f)"), equal[:].rearrange("p t e f -> p t (e f)"),
                                                    tri[:].rearrange("p (a e) f -> p a (e f)", a=1).broadcast_to([P, NTL, E * E]), ALU.mult))
                    step(8, nc.vector.tensor_tensor(above[:], above[:], equal[:], ALU.add))
                    step(9, nc.vector.tensor_reduce(rank[:, :, :, 0], above[:], AX.X, ALU.add))
                    step(10, nc.vector.tensor_scalar(rank[:], rank[:], TOPK - 0.5, TOPK / (TOPK + 1.0), ALU.is_lt, ALU.mult))
                    step(11, nc.vector.tensor_tensor(cw[:], pr[:], rank[:, :, :, 0], ALU.mult))
                    step(12, nc.vector.tensor_reduce(den[:, :, 0], cw[:], AX.X, ALU.add))
                    step(13, nc.vector.tensor_scalar(den[:], den[:], (TOPK + 1.0) / TOPK, None, ALU.mult))
                    step(14, nc.vector.reciprocal(den[:], den[:]))
                    step(15, nc.vector.tensor_tensor(cw[:], cw[:], den[:].broadcast_to(over_e), ALU.mult))

        sg = sb("sg", [P, 2, 4 * P])
        gT = sb("gT", [P, 2, 4 * P])
        h_ready = PerSlot(sem("h_ready"), NE)
        silu = PerSlot(sem("silu"), NE)
        g_ready = PerSlot(sem("g_ready"), NE)
        y_ready = PerSlot(sem("y_ready"), NE)
        y_added = PerSlot(sem("y_added"), NE)
        Yv = Yt[:].rearrange("p c b d -> p (c b) d")
        out_banks = lambda e: (4, 5) if e < NSH or e % 2 else (6, 7)
        with nc.Block() as block:
            @block.sync
            def _(sp):
                for x in (h_ready, silu, g_ready, y_ready, y_added):
                    sp.sem_inc(x.sem, x.n)
        with nc.Block() as block:
            @block.tensor
            def _(pe):
                def up(n, e):
                    pe.wait_ge(silu.sem, silu.step(n, e - 1))
                    pe.wait_ge(g_ready.sem, g_ready.step(n, e - 1))
                    for w, bk in ((W1, bank[e % 2]), (W3, bank[2 + e % 2])):
                        for k in range(KD):
                            last = nc.tensor.matmul(bk[:], w[:, k, e, :], XT[:, k, ds(n * 4 * P, 4 * P)], start=(k == 0), stop=(k == KD - 1))
                    last.then_inc(h_ready.sem, 1)

                def down(n, e):
                    pe.wait_ge(g_ready.sem, g_ready.step(n, e + 1))
                    shared = e < NSH
                    pe.wait_ge(y_added.sem, y_added.before(n) if e <= NSH else y_added.step(n, e - 1))
                    for j in range(4):
                        bk = bank[out_banks(e)[j // 2]]
                        last = nc.tensor.matmul(bk[:, (j % 2) * D:(j % 2 + 1) * D], gT[:, e % 2, j * P:(j + 1) * P], W2[:, e, :],
                                                start=(j % 2 == 0) if not shared else (e == 0 and j % 2 == 0),
                                                stop=not shared or e == NSH - 1, skip_group_check=True)
                    last.then_inc(y_ready.sem, 1)

                pe.wait_ge(w_loaded, 16 * (2 * KD + 1))
                with pe.Fori(0, NB) as n:
                    up(n, 0)
                    for e in range(NE):
                        if e + 1 < NE:
                            up(n, e + 1)
                        down(n, e)

            @block.scalar
            def _(act):
                with act.Fori(0, NB) as n:
                    for e in range(NE):
                        act.wait_ge(h_ready.sem, h_ready.step(n, e + 1))
                        act.wait_ge(g_ready.sem, g_ready.step(n, e - 1))
                        nc.scalar.activation(sg[:, e % 2, :], bank[e % 2][:], ACT.Silu).then_inc(silu.sem, 1)

            @block.vector
            def _(dve):
                def gated(n, e):
                    dve.wait_ge(silu.sem, silu.step(n, e + 1))
                    dve.wait_ge(y_ready.sem, y_ready.step(n, e - 1))
                    nc.vector.tensor_tensor(gT[:, e % 2, :], bank[2 + e % 2][:], sg[:, e % 2, :], ALU.mult).then_inc(g_ready.sem, 1)

                def add(n, e):
                    dve.wait_ge(y_ready.sem, y_ready.step(n, e + 1))
                    if e < NSH - 1:
                        dve.sem_inc(y_added.sem, 1)
                        return
                    dve.wait_ge(y_added.sem, y_added.step(n, e))
                    for j in range(4):
                        src = bank[out_banks(e)[j // 2]][:, (j % 2) * D:(j % 2 + 1) * D]
                        y = Yv[:, ds(n * 4 + j, 1), :].rearrange("p a d -> p (a d)")
                        if e == NSH - 1:
                            last = nc.vector.tensor_scalar(y, src, 1.0 / (TOPK + 1), None, ALU.mult)
                        else:
                            last = nc.vector.scalar_tensor_tensor(y, src, cw[:, ds(n * 4 + j, 1), e - NSH], y, ALU.mult, ALU.add)
                    last.then_inc(y_added.sem, 1)

                with dve.Fori(0, NB) as n:
                    gated(n, 0)
                    for e in range(NE):
                        if e + 1 < NE:
                            gated(n, e + 1)
                        add(n, e)


def two_layers(nc, A, out):
    with ExitStack() as ctx:
        tools = Tools(nc, ctx)
        PS = ctx.enter_context(nc.psum_tensor("PS", [P, 8, 512], F32))
        bank = [PS[:, i, :] for i in range(8)]
        X = tools.sb("X", [P, NC, B, D])
        Yt = tools.sb("Yt", [P, NC, B, D])
        ident = tools.sb("ident", [P, P])
        cumsum_mask = tools.sb("cumsum_mask", [P, P])
        level0 = tools.sb("level0", [P, P])
        level0_t = tools.sb("level0_t", [P, P])
        level_masks = tools.sb("level_masks", [P, LEVELS - 1, 64])
        causal = tools.sb("causal", [P, U * P])
        causal16 = tools.sb("causal16", [P, U * P], BF16)
        diag16 = tools.sb("diag16", [P, P], BF16)
        ident16 = tools.sb("ident16", [P, P], BF16)
        ones = tools.sb("ones", [P, P])
        half = tools.sb("half", [P, 1])
        consts_loaded = tools.sem("consts_loaded")
        consts_made = tools.sem("consts_made")

        with nc.Block() as block:
            @block.sync
            def _(sp):
                at = 0
                for t, n in ((ident, P), (cumsum_mask, P), (level0, P), (level0_t, P), (level_masks, 64 * (LEVELS - 1)), (causal, U * P)):
                    dst = t[:].rearrange("p a n -> p (a n)") if t is level_masks else t[:]
                    sp.dma_start(dst, A["masks"][:, at:at + n]).then_inc(consts_loaded, 16)
                    at += n

            @block.vector
            def _(dve):
                nc.vector.memset(ones[:], 1.0)
                nc.vector.memset(half[:], -0.5)
                dve.wait_ge(consts_loaded, 16 * 6)
                nc.vector.tensor_copy(ident16[:], ident[:])
                nc.vector.tensor_copy(causal16[:], causal[:])

            @block.gpsimd
            def _(pool):
                pool.wait_ge(consts_loaded, 16 * 6)
                nc.gpsimd.memset(diag16[:], 0.0).then_inc(consts_made, 1)
                pool.wait_ge(consts_made, 1)
                nc.gpsimd.affine_select(out=diag16[:], in_=diag16[:], compare_op=ALU.is_ge, fill=NEG, base=0,
                                        pattern=[[-1, P]], channel_multiplier=1)

        with ExitStack() as c1:
            Xc = tools.sb("Xc", [P, NC + 2, KD, B, CW], F32, c1)

            def put_chunks(act, c, b, src):
                return nc.scalar.activation(Xc[:, c, :, b, HALO:CW], src, ACT.Copy)

            residual_and_norm(nc, tools, "n0", bank, ident, half, X, None, put_chunks, x_in=A["x"])
            with nc.Block() as block:
                @block.gpsimd
                def _(pool):
                    rows = Xc[:].rearrange("p c k b n -> p c (k b) n")
                    nc.gpsimd.memset(rows[:, 0, :, 0:HALO], 0.0)
                    nc.gpsimd.memset(rows[:, NC, :, 0:HALO], 0.0)
                    nc.gpsimd.tensor_copy(rows[:, 1:NC, :, 0:HALO], rows[:, 0:NC - 1, :, P:CW])
                    nc.gpsimd.tensor_copy(rows[:, NC, :, HALO:CW], rows[:, 0, :, HALO:CW])
                    nc.gpsimd.tensor_copy(rows[:, NC + 1, :, HALO:CW], rows[:, 1, :, HALO:CW])
                    nc.gpsimd.tensor_copy(rows[:, NC + 1, :, 0:HALO], rows[:, 0, :, P:CW])
            cst = (ident, half, cumsum_mask, ones, ident16, causal16, level0, level0_t, level_masks)
            delta_rule(nc, tools, bank, cst, X, Xc, Yt, A["L0_W_qkv"], A["L0_W_ab"], A["conv_w"], A["A_log"], A["dt_bias"],
                       A["o_norm_w"], A["L0_W_o"])

        with ExitStack() as c1:
            XT = tools.sb("XT", [P, KD, NC * B * P], F32, c1)

            def put_tokens(act, c, b, src):
                t = (c * B + b) * P
                return nc.scalar.activation(XT[:, :, t:t + P], src, ACT.Copy)

            plain = lambda c, b: Yt[:, c, b, :]
            rotated = lambda c, b: Yt[:, (c + 1) % NC, b, :]
            with ExitStack() as c3:
                ffn_weights = FfnWeights(tools, c3, A["gate_w"], A["gate_s"], A["up_w"], A["up_s"], A["down_w"], A["down_s"])
                residual_and_norm(nc, tools, "n1", bank, ident, half, X, rotated, put_tokens, loads_ahead=ffn_weights.load)
                int_ffn(nc, tools, bank, XT, Yt, ffn_weights)
            with ExitStack() as c3:
                attention_weights = AttentionWeights(tools, c3, A["at_wq"], A["at_bq"], A["at_cs"], A["at_wv"], A["at_bv"],
                                                     A["L1_W_dense"], A["L1_b_dense"])
                residual_and_norm(nc, tools, "n2", bank, ident, half, X, plain, put_tokens, loads_ahead=attention_weights.load)
                attention(nc, tools, PS, bank, ident16, causal16, diag16, XT, Yt, attention_weights)
            with ExitStack() as c3:
                expert_weights = ExpertWeights(tools, c3, A["w_router"], A["tri"], A["w1"], A["w3"], A["w2"])
                residual_and_norm(nc, tools, "n3", bank, ident, half, X, plain, put_tokens, loads_ahead=expert_weights.load)
                experts(nc, tools, bank, ident, XT, Yt, expert_weights)
            residual_and_norm(nc, tools, "n4", bank, ident, half, X, plain, None, store=out)


def constants():
    i = np.arange(P)
    r, c = i[:, None], i[None, :]
    parts = [r == c, r <= c]
    level0 = (r == c) | ((r // 2 == c // 2) & (r > c))
    parts += [level0, level0.T]
    for l in range(1, LEVELS):
        n = 1 << l
        first = i[(i // n) % 2 == 0]
        cc = first[None, :]
        parts.append((r == cc) | ((r // (2 * n) == cc // (2 * n)) & ((r // n) % 2 == 1)))
    masks = np.concatenate([p.astype(np.float32) for p in parts] + [np.where(r > c, np.float32(NEG), np.float32(0))] * U, axis=1)
    tri = (i[None, :E] < i[:E, None]).astype(np.float32).reshape(-1)
    rot = AD // 4
    inv = (np.float32(1) / np.float32(10000.0) ** (np.arange(0, rot, 2, dtype=np.float32) / np.float32(rot))).astype(np.float32)
    ang = np.outer(np.arange(T, dtype=np.float32), inv).astype(np.float32)
    cs = np.zeros((2, AD, T), np.float32)
    cs[0] = 1.0
    for d in range(rot):
        cs[0, d] = np.cos(ang[:, d % 2])
        cs[1, d] = np.sin(ang[:, d % 2]) * (-1.0 if d < rot // 2 else 1.0)
    return masks.astype(np.float32), tri, np.tile(cs, (1, P // AD, 1)).astype(np.float32)


def lay_out(a):
    masks, tri, cs = constants()
    rot = AD // 4
    partner = np.arange(AD)
    partner[:rot] = (partner[:rot] + rot // 2) % rot
    w = a["L1_attn_W_qkv"].reshape(D, AH, 3, AD)
    bias = a["L1_attn_b_qkv"].reshape(AH, 3, AD)
    wq = np.stack([w[:, :, 0, :], w[:, :, 0, partner], w[:, :, 1, :], w[:, :, 1, partner]]).reshape(4, D, AH * AD)
    bq = np.stack([bias[:, 0, :], bias[:, 0, partner], bias[:, 1, :], bias[:, 1, partner]]).reshape(4, KD, P).transpose(2, 0, 1)
    quarters = lambda s: s.reshape(D, NSH, EH).transpose(1, 0, 2)
    return {
        "x": a["L0_attn_hidden_states"], "L0_W_qkv": a["L0_attn_W_qkv"], "L0_W_ab": a["L0_attn_W_ab"],
        "conv_w": a["L0_attn_conv_w"], "A_log": a["L0_attn_A_log"], "dt_bias": a["L0_attn_dt_bias"],
        "o_norm_w": a["L0_attn_o_norm_w"], "L0_W_o": a["L0_attn_W_o"],
        "gate_w": a["L0_ffn_gate_w"].T, "gate_s": a["L0_ffn_gate_scale"].reshape(FI // P, P).T,
        "up_w": a["L0_ffn_up_w"].T, "up_s": a["L0_ffn_up_scale"].reshape(FI // P, P).T,
        "down_w": a["L0_ffn_down_w"].T, "down_s": a["L0_ffn_down_scale"],
        "at_wq": wq, "at_bq": bq, "at_cs": cs, "at_wv": w[:, :, 2, :].reshape(D, AH * AD), "at_bv": bias[:, 2, :].reshape(-1),
        "L1_W_dense": a["L1_attn_W_dense"], "L1_b_dense": a["L1_attn_b_dense"],
        "w_router": a["L1_ffn_w_router"],
        "w1": np.concatenate([quarters(a["L1_ffn_ws1"]), a["L1_ffn_we1"]]),
        "w3": np.concatenate([quarters(a["L1_ffn_ws3"]), a["L1_ffn_we3"]]),
        "w2": np.concatenate([a["L1_ffn_ws2"].reshape(NSH, EH, D), a["L1_ffn_we2"]]),
        "masks": masks, "tri": tri,
    }


def kernel(**inputs):
    import concourse.bacc as _bacc
    from concourse.bass_utils import run_bass_kernel_spmd as _run

    nc = _bacc.Bacc("TRN2", target_bir_lowering=False, num_devices=1)
    arrays, aps = {}, {}
    for name, a in lay_out({k: np.asarray(v) for k, v in inputs.items()}).items():
        a = np.ascontiguousarray(a)
        arrays[f"in_{name}"] = a
        aps[name] = nc.dram_tensor(f"in_{name}", a.shape, mybir.dt.from_np(a.dtype), kind="ExternalInput").ap()
    out = nc.dram_tensor("out_0", (B, T, D), F32, kind="ExternalOutput").ap()
    two_layers(nc, aps, out)
    r = _run(nc, [arrays], core_ids=[0])
    return r.results[0]["out_0"]
```
